# Optimizing a Trainium2 kernel written in Bass

```python
import numpy as np
import jax
import jax.numpy as jnp

def _softmax(x, axis=-1):
    return jax.nn.softmax(x, axis=axis)

def _gelu(x):
    return jax.nn.gelu(x, approximate=True)

def _silu(x):
    return jax.nn.silu(x)

def _sigmoid(x):
    return jax.nn.sigmoid(x)

def _layernorm(x, axis=-1, eps=1e-05):
    m = jnp.mean(x, axis=axis, keepdims=True)
    v = jnp.var(x, axis=axis, keepdims=True)
    return (x - m) / jnp.sqrt(v + eps)

def _scatter_add(tgt, idx, src, axis=0):
    return tgt.at[idx].add(src)

def _segment_sum(src, seg, n):
    return jax.ops.segment_sum(src, seg, n)
kernel_name = 'mk_vit_tower_cls_d4_tok_img1024_r4_ba8ff5'

def setup_inputs(seed: int=0):
    np.random.seed(seed)
    _w = jnp.asarray

    def _rec_inputs():
        import jax
        import jax.numpy as jnp
        _rk = jax.random.key(seed)
        x = -0.00016672 + 0.999947 * jax.random.normal(jax.random.fold_in(_rk, 1), (16, 3, 96, 96), jnp.float32)
        cls_tok = 0.02 * jax.random.normal(jax.random.fold_in(_rk, 5), (1, 1, 256), jnp.float32)
        return (x, cls_tok)
    x, cls_tok = _rec_inputs()

    def _L0_tok_setup():
        import jax, jax.numpy as jnp
        import numpy as np
        IMG = 96
        PATCH = 16
        C_IN = 3
        EMBED = 256
        NPH = IMG // PATCH
        NUM_PATCHES = NPH * NPH
        PATCH_DIM = PATCH * PATCH * C_IN
        key = jax.random.key(seed)
        k_x, k_w, k_b, k_cls, k_pos = jax.random.split(key, 5)
        x = jax.random.normal(k_x, (64, C_IN, IMG, IMG), dtype=jnp.float32)
        W = jax.random.normal(k_w, (EMBED, PATCH_DIM), dtype=jnp.float32) * (1.0 / np.sqrt(PATCH_DIM))
        b = jax.random.normal(k_b, (EMBED,), dtype=jnp.float32) * 0.01
        cls_token = jax.random.normal(k_cls, (1, 1, EMBED), dtype=jnp.float32) * 0.02
        pos_embed = jax.random.normal(k_pos, (1, NUM_PATCHES + 1, EMBED), dtype=jnp.float32) * 0.02
        return {'x': x, 'W': W, 'b': b, 'cls_token': cls_token, 'pos_embed': pos_embed}
    _L0_tok_all = _L0_tok_setup()
    _L0_tok_in = {k: v for k, v in _L0_tok_all.items() if k in ('W', 'b', 'cls_token', 'pos_embed')}
    del _L0_tok_all

    def _L0_attn_setup():
        import jax, jax.numpy as jnp
        import numpy as np
        import math
        D_MODEL = 256
        N_HEAD = 16
        D_HEAD = D_MODEL // N_HEAD
        D_KMAP = 128
        D_INNER = 1024

        def _layer_norm(x, g, b, eps=1e-05):
            mu = jnp.mean(x, axis=-1, keepdims=True)
            var = jnp.mean(jnp.square(x - mu), axis=-1, keepdims=True)
            return (x - mu) * jax.lax.rsqrt(var + eps) * g + b

        def _fourier_kernel(x, proj_mat):
            p = jnp.einsum('blhd,dm->blhm', x, proj_mat) / math.sqrt(D_HEAD)
            return jnp.concatenate([jnp.cos(p), jnp.sin(p)], axis=-1) / math.sqrt(D_KMAP)
        key = jax.random.key(seed)
        ks = jax.random.split(key, 12)
        s = 0.02
        return {'x': jax.random.normal(ks[0], (4, 1024, D_MODEL), dtype=jnp.float32), 'proj_mat': jax.random.normal(ks[1], (D_HEAD, D_KMAP), dtype=jnp.float32), 'wq': jax.random.normal(ks[2], (D_MODEL, D_MODEL), dtype=jnp.float32) * s, 'bq': jnp.zeros((D_MODEL,), jnp.float32), 'wk': jax.random.normal(ks[3], (D_MODEL, D_MODEL), dtype=jnp.float32) * s, 'bk': jnp.zeros((D_MODEL,), jnp.float32), 'wv': jax.random.normal(ks[4], (D_MODEL, D_MODEL), dtype=jnp.float32) * s, 'bv': jnp.zeros((D_MODEL,), jnp.float32), 'wo': jax.random.normal(ks[5], (D_MODEL, D_MODEL), dtype=jnp.float32) * s, 'bo': jnp.zeros((D_MODEL,), jnp.float32), 'ln1_g': jnp.ones((D_MODEL,), jnp.float32), 'ln1_b': jnp.zeros((D_MODEL,), jnp.float32), 'w1': jax.random.normal(ks[6], (D_MODEL, D_INNER), dtype=jnp.float32) * s, 'b1': jnp.zeros((D_INNER,), jnp.float32), 'w2': jax.random.normal(ks[7], (D_INNER, D_MODEL), dtype=jnp.float32) * s, 'b2': jnp.zeros((D_MODEL,), jnp.float32), 'ln2_g': jnp.ones((D_MODEL,), jnp.float32), 'ln2_b': jnp.zeros((D_MODEL,), jnp.float32)}
    _L0_attn_all = _L0_attn_setup()
    _L0_attn_in = {k: v for k, v in _L0_attn_all.items() if k in ('proj_mat', 'wq', 'bq', 'wk', 'bk', 'wv', 'bv', 'wo', 'bo', 'ln1_g', 'ln1_b', 'w1', 'b1', 'w2', 'b2', 'ln2_g', 'ln2_b')}
    del _L0_attn_all

    def _L0_ffn_setup():
        import jax, jax.numpy as jnp
        import numpy as np
        E = 8
        H = 256
        F = 896
        JITTER_EPS = 0.01

        def _route(scores):
            vals, idx = jax.lax.top_k(scores, 2)
            neg_inf = -jnp.inf
            t1 = vals[:, 0:1]
            factor1 = jnp.maximum(jnp.abs(scores), t1)
            mask1 = (t1 - scores) / factor1 > 2 * JITTER_EPS
            p1 = jax.nn.softmax(jnp.where(mask1, neg_inf, scores), axis=-1)
            mult1 = jnp.take_along_axis(p1, idx[:, 0:1], axis=-1)
            t2 = vals[:, 1:2]
            factor2 = jnp.maximum(jnp.abs(scores), t2)
            mask2 = (t2 - scores) / factor2 > 2 * JITTER_EPS
            onehot0 = jax.nn.one_hot(idx[:, 0], scores.shape[-1], dtype=bool)
            scores2 = jnp.where(onehot0, neg_inf, scores)
            p2 = jax.nn.softmax(jnp.where(mask2, neg_inf, scores2), axis=-1)
            mult2 = jnp.take_along_axis(p2, idx[:, 1:2], axis=-1)
            return (jnp.concatenate([mult1, mult2], axis=-1), idx)
        key = jax.random.key(seed)
        ks = jax.random.split(key, 5)
        hidden_states = jax.random.normal(ks[0], (2, 256, H), jnp.float32)
        gate_w = jax.random.normal(ks[1], (E, H), jnp.float32) * 0.02
        w1 = jax.random.normal(ks[2], (E, F, H), jnp.float32) * 0.02
        w2 = jax.random.normal(ks[3], (E, H, F), jnp.float32) * 0.02
        w3 = jax.random.normal(ks[4], (E, F, H), jnp.float32) * 0.02
        return {'hidden_states': hidden_states, 'gate_w': gate_w, 'w1': w1, 'w2': w2, 'w3': w3}
    _L0_ffn_all = _L0_ffn_setup()
    _L0_ffn_in = {k: v for k, v in _L0_ffn_all.items() if k in ('gate_w', 'w1', 'w2', 'w3')}
    del _L0_ffn_all

    def _L1_attn_setup():
        import jax, jax.numpy as jnp
        import numpy as np
        B, S, H = (8, 256, 256)
        HEADS = 8
        HD = H // HEADS
        LAMBDA_INIT = 0.8
        LN_EPS = 1e-05
        key = jax.random.key(seed)
        ks = jax.random.split(key, 16)
        xavier = float(np.sqrt(6.0 / (H + H)))
        inp = {'hidden_states': jax.random.normal(ks[0], (B, S, H), dtype=jnp.float32), 'Wq': jax.random.uniform(ks[1], (H, H), jnp.float32, -xavier, xavier), 'bq': jnp.zeros((H,), jnp.float32), 'Wk': jax.random.uniform(ks[2], (H, H), jnp.float32, -xavier, xavier), 'bk': jnp.zeros((H,), jnp.float32), 'Wv': jax.random.uniform(ks[3], (H, H), jnp.float32, -xavier, xavier), 'bv': jnp.zeros((H,), jnp.float32), 'Wo': jax.random.uniform(ks[4], (H, H), jnp.float32, -xavier, xavier), 'bo': jnp.zeros((H,), jnp.float32), 'lambda_q1': 0.02 * jax.random.normal(ks[5], (HD,), jnp.float32), 'lambda_k1': 0.02 * jax.random.normal(ks[6], (HD,), jnp.float32), 'lambda_q2': 0.02 * jax.random.normal(ks[7], (HD,), jnp.float32), 'lambda_k2': 0.02 * jax.random.normal(ks[8], (HD,), jnp.float32), 'ln_w': jnp.ones((H,), jnp.float32), 'ln_b': jnp.zeros((H,), jnp.float32)}
        return inp
    _L1_attn_all = _L1_attn_setup()
    _L1_attn_in = {k: v for k, v in _L1_attn_all.items() if k in ('Wq', 'bq', 'Wk', 'bk', 'Wv', 'bv', 'Wo', 'bo', 'lambda_q1', 'lambda_k1', 'lambda_q2', 'lambda_k2', 'ln_w', 'ln_b')}
    del _L1_attn_all

    def _L1_ffn_setup():
        import jax, jax.numpy as jnp
        import numpy as np
        B, S, D, E, K = (2, 512, 256, 8, 2)
        H = 4 * D
        key = jax.random.key(seed)
        ks = jax.random.split(key, 6)
        x = jax.random.normal(ks[0], (B, S, D), dtype=jnp.float32)
        lim_g = np.sqrt(6.0 / (D + E)).astype(np.float32)
        W_gate = jax.random.uniform(ks[1], (D, E), minval=-lim_g, maxval=lim_g, dtype=jnp.float32)
        lim1 = np.sqrt(1.0 / D).astype(np.float32)
        lim2 = np.sqrt(1.0 / H).astype(np.float32)
        W1 = jax.random.uniform(ks[2], (E, D, H), minval=-lim1, maxval=lim1, dtype=jnp.float32)
        b1 = jax.random.uniform(ks[3], (E, H), minval=-lim1, maxval=lim1, dtype=jnp.float32)
        W2 = jax.random.uniform(ks[4], (E, H, D), minval=-lim2, maxval=lim2, dtype=jnp.float32)
        b2 = jax.random.uniform(ks[5], (E, D), minval=-lim2, maxval=lim2, dtype=jnp.float32)
        return {'x': x, 'W_gate': W_gate, 'W1': W1, 'b1': b1, 'W2': W2, 'b2': b2}
    _L1_ffn_all = _L1_ffn_setup()
    _L1_ffn_in = {k: v for k, v in _L1_ffn_all.items() if k in ('W_gate', 'W1', 'b1', 'W2', 'b2')}
    del _L1_ffn_all

    def _L2_attn_setup():
        import jax, jax.numpy as jnp
        import numpy as np
        NUM_HEADS = 32
        EPS = 1e-15
        key = jax.random.key(seed)
        k1, k2, k3, k4 = jax.random.split(key, 4)
        B, N, C = (8, 1024, 256)
        x = jax.random.normal(k1, (B, N, C), dtype=jnp.float32)
        qkv_weight = jax.random.normal(k2, (3 * C, C), dtype=jnp.float32) * C ** (-0.5)
        proj_weight = jax.random.normal(k3, (C, C), dtype=jnp.float32) * C ** (-0.5)
        proj_bias = jax.random.normal(k4, (C,), dtype=jnp.float32) * 0.01
        return {'x': x, 'qkv_weight': qkv_weight, 'proj_weight': proj_weight, 'proj_bias': proj_bias}
    _L2_attn_all = _L2_attn_setup()
    _L2_attn_in = {k: v for k, v in _L2_attn_all.items() if k in ('qkv_weight', 'proj_weight', 'proj_bias')}
    del _L2_attn_all

    def _L2_ffn_setup():
        import jax, jax.numpy as jnp
        import numpy as np
        B, S, D, O, E, K = (2, 512, 256, 256, 8, 2)
        key = jax.random.key(seed)
        ks = jax.random.split(key, 6)

        def w(k, shape, fan_in):
            return jax.random.normal(k, shape, jnp.float32) * fan_in ** (-0.5)
        return {'x': jax.random.normal(ks[0], (B, S, D), jnp.float32), 'gate_w': w(ks[1], (E, D), D), 'gate_b': jnp.zeros((E,), jnp.float32), 'w1': w(ks[2], (E, D, O), D), 'b1': jnp.zeros((E, O), jnp.float32), 'w2': w(ks[3], (E, O, O), O), 'b2': jnp.zeros((E, O), jnp.float32), 'w3': w(ks[4], (E, O, O), O), 'b3': jnp.zeros((E, O), jnp.float32)}
    _L2_ffn_all = _L2_ffn_setup()
    _L2_ffn_in = {k: v for k, v in _L2_ffn_all.items() if k in ('gate_w', 'gate_b', 'w1', 'b1', 'w2', 'b2', 'w3', 'b3')}
    del _L2_ffn_all

    def _L3_attn_setup():
        import jax, jax.numpy as jnp
        import numpy as np
        B, S, D_IN, D_OUT, H = (2, 512, 256, 256, 16)
        HD = D_OUT // H
        key = jax.random.key(seed)
        ks = jax.random.split(key, 6)
        x = jax.random.normal(ks[0], (B, S, D_IN), jnp.float32)
        Wq = jax.random.normal(ks[1], (D_IN, D_OUT), jnp.float32) * 0.02
        Wk = jax.random.normal(ks[2], (D_IN, D_OUT), jnp.float32) * 0.02
        Wv = jax.random.normal(ks[3], (D_IN, D_OUT), jnp.float32) * 0.02
        Wo = jax.random.normal(ks[4], (D_OUT, D_OUT), jnp.float32) * 0.02
        bo = jax.random.normal(ks[5], (D_OUT,), jnp.float32) * 0.02
        return {'x': x, 'Wq': Wq, 'Wk': Wk, 'Wv': Wv, 'Wo': Wo, 'bo': bo}
    _L3_attn_all = _L3_attn_setup()
    _L3_attn_in = {k: v for k, v in _L3_attn_all.items() if k in ('Wq', 'Wk', 'Wv', 'Wo', 'bo')}
    del _L3_attn_all

    def _L3_ffn_setup():
        import jax, jax.numpy as jnp
        import numpy as np
        HIDDEN = 256
        FF = 1024
        N_EXPERTS = 8
        CAP_FACTOR = 1.0
        B, S = (4, 512)
        STD = 0.02

        def _gelu(x):
            return x * 0.5 * (1.0 + jax.lax.erf(x / 1.41421))
        key = jax.random.key(seed)
        ks = jax.random.split(key, 6)
        x = jax.random.normal(ks[0], (B, S, HIDDEN), dtype=jnp.float32)
        W_sw = jax.random.normal(ks[1], (HIDDEN, N_EXPERTS), dtype=jnp.float32) * STD
        b_sw = jnp.zeros((N_EXPERTS,), dtype=jnp.float32)
        W1 = jax.random.normal(ks[2], (N_EXPERTS, HIDDEN, FF), dtype=jnp.float32) * STD
        b1 = jnp.zeros((N_EXPERTS, FF), dtype=jnp.float32)
        W2 = jax.random.normal(ks[3], (N_EXPERTS, FF, HIDDEN), dtype=jnp.float32) * STD
        b2 = jnp.zeros((N_EXPERTS, HIDDEN), dtype=jnp.float32)
        return {'x': x, 'W_sw': W_sw, 'b_sw': b_sw, 'W1': W1, 'b1': b1, 'W2': W2, 'b2': b2}
    _L3_ffn_all = _L3_ffn_setup()
    _L3_ffn_in = {k: v for k, v in _L3_ffn_all.items() if k in ('W_sw', 'b_sw', 'W1', 'b1', 'W2', 'b2')}
    del _L3_ffn_all
    return {'x': x, 'cls_tok': cls_tok, 'L0_tok_W': _L0_tok_in['W'], 'L0_tok_b': _L0_tok_in['b'], 'L0_tok_cls_token': _L0_tok_in['cls_token'], 'L0_tok_pos_embed': _L0_tok_in['pos_embed'], 'L0_attn_proj_mat': _L0_attn_in['proj_mat'], 'L0_attn_wq': _L0_attn_in['wq'], 'L0_attn_bq': _L0_attn_in['bq'], 'L0_attn_wk': _L0_attn_in['wk'], 'L0_attn_bk': _L0_attn_in['bk'], 'L0_attn_wv': _L0_attn_in['wv'], 'L0_attn_bv': _L0_attn_in['bv'], 'L0_attn_wo': _L0_attn_in['wo'], 'L0_attn_bo': _L0_attn_in['bo'], 'L0_attn_ln1_g': _L0_attn_in['ln1_g'], 'L0_attn_ln1_b': _L0_attn_in['ln1_b'], 'L0_attn_w1': _L0_attn_in['w1'], 'L0_attn_b1': _L0_attn_in['b1'], 'L0_attn_w2': _L0_attn_in['w2'], 'L0_attn_b2': _L0_attn_in['b2'], 'L0_attn_ln2_g': _L0_attn_in['ln2_g'], 'L0_attn_ln2_b': _L0_attn_in['ln2_b'], 'L0_ffn_gate_w': _L0_ffn_in['gate_w'], 'L0_ffn_w1': _L0_ffn_in['w1'], 'L0_ffn_w2': _L0_ffn_in['w2'], 'L0_ffn_w3': _L0_ffn_in['w3'], 'L1_attn_Wq': _L1_attn_in['Wq'], 'L1_attn_bq': _L1_attn_in['bq'], 'L1_attn_Wk': _L1_attn_in['Wk'], 'L1_attn_bk': _L1_attn_in['bk'], 'L1_attn_Wv': _L1_attn_in['Wv'], 'L1_attn_bv': _L1_attn_in['bv'], 'L1_attn_Wo': _L1_attn_in['Wo'], 'L1_attn_bo': _L1_attn_in['bo'], 'L1_attn_lambda_q1': _L1_attn_in['lambda_q1'], 'L1_attn_lambda_k1': _L1_attn_in['lambda_k1'], 'L1_attn_lambda_q2': _L1_attn_in['lambda_q2'], 'L1_attn_lambda_k2': _L1_attn_in['lambda_k2'], 'L1_attn_ln_w': _L1_attn_in['ln_w'], 'L1_attn_ln_b': _L1_attn_in['ln_b'], 'L1_ffn_W_gate': _L1_ffn_in['W_gate'], 'L1_ffn_W1': _L1_ffn_in['W1'], 'L1_ffn_b1': _L1_ffn_in['b1'], 'L1_ffn_W2': _L1_ffn_in['W2'], 'L1_ffn_b2': _L1_ffn_in['b2'], 'L2_attn_qkv_weight': _L2_attn_in['qkv_weight'], 'L2_attn_proj_weight': _L2_attn_in['proj_weight'], 'L2_attn_proj_bias': _L2_attn_in['proj_bias'], 'L2_ffn_gate_w': _L2_ffn_in['gate_w'], 'L2_ffn_gate_b': _L2_ffn_in['gate_b'], 'L2_ffn_w1': _L2_ffn_in['w1'], 'L2_ffn_b1': _L2_ffn_in['b1'], 'L2_ffn_w2': _L2_ffn_in['w2'], 'L2_ffn_b2': _L2_ffn_in['b2'], 'L2_ffn_w3': _L2_ffn_in['w3'], 'L2_ffn_b3': _L2_ffn_in['b3'], 'L3_attn_Wq': _L3_attn_in['Wq'], 'L3_attn_Wk': _L3_attn_in['Wk'], 'L3_attn_Wv': _L3_attn_in['Wv'], 'L3_attn_Wo': _L3_attn_in['Wo'], 'L3_attn_bo': _L3_attn_in['bo'], 'L3_ffn_W_sw': _L3_ffn_in['W_sw'], 'L3_ffn_b_sw': _L3_ffn_in['b_sw'], 'L3_ffn_W1': _L3_ffn_in['W1'], 'L3_ffn_b1': _L3_ffn_in['b1'], 'L3_ffn_W2': _L3_ffn_in['W2'], 'L3_ffn_b2': _L3_ffn_in['b2']}

def reference(x, cls_tok, L0_tok_W, L0_tok_b, L0_tok_cls_token, L0_tok_pos_embed, L0_attn_proj_mat, L0_attn_wq, L0_attn_bq, L0_attn_wk, L0_attn_bk, L0_attn_wv, L0_attn_bv, L0_attn_wo, L0_attn_bo, L0_attn_ln1_g, L0_attn_ln1_b, L0_attn_w1, L0_attn_b1, L0_attn_w2, L0_attn_b2, L0_attn_ln2_g, L0_attn_ln2_b, L0_ffn_gate_w, L0_ffn_w1, L0_ffn_w2, L0_ffn_w3, L1_attn_Wq, L1_attn_bq, L1_attn_Wk, L1_attn_bk, L1_attn_Wv, L1_attn_bv, L1_attn_Wo, L1_attn_bo, L1_attn_lambda_q1, L1_attn_lambda_k1, L1_attn_lambda_q2, L1_attn_lambda_k2, L1_attn_ln_w, L1_attn_ln_b, L1_ffn_W_gate, L1_ffn_W1, L1_ffn_b1, L1_ffn_W2, L1_ffn_b2, L2_attn_qkv_weight, L2_attn_proj_weight, L2_attn_proj_bias, L2_ffn_gate_w, L2_ffn_gate_b, L2_ffn_w1, L2_ffn_b1, L2_ffn_w2, L2_ffn_b2, L2_ffn_w3, L2_ffn_b3, L3_attn_Wq, L3_attn_Wk, L3_attn_Wv, L3_attn_Wo, L3_attn_bo, L3_ffn_W_sw, L3_ffn_b_sw, L3_ffn_W1, L3_ffn_b1, L3_ffn_W2, L3_ffn_b2):
    import jax
    import jax.numpy as jnp

    def _L0_tok_ref(x, W, b, cls_token, pos_embed):
        import jax, jax.numpy as jnp
        import numpy as np
        IMG = 96
        PATCH = 16
        C_IN = 3
        EMBED = 256
        NPH = IMG // PATCH
        NUM_PATCHES = NPH * NPH
        PATCH_DIM = PATCH * PATCH * C_IN
        B, C, H, Wd = x.shape
        nph, npw = (H // PATCH, Wd // PATCH)
        patches = x.reshape(B, C, nph, PATCH, npw, PATCH)
        patches = patches.transpose(0, 2, 4, 1, 3, 5)
        patches = patches.reshape(B, nph * npw, C * PATCH * PATCH)
        proj = jnp.einsum('bnd,ed->bne', patches, W) + b
        cls = jnp.broadcast_to(cls_token, (B, 1, cls_token.shape[-1]))
        out = jnp.concatenate([cls, proj], axis=1) + pos_embed
        return out

    def _L0_attn_ref(x, proj_mat, wq, bq, wk, bk, wv, bv, wo, bo, ln1_g, ln1_b, w1, b1, w2, b2, ln2_g, ln2_b):
        import jax, jax.numpy as jnp
        import numpy as np
        import math
        D_MODEL = 256
        N_HEAD = 16
        D_HEAD = D_MODEL // N_HEAD
        D_KMAP = 128
        D_INNER = 1024

        def _layer_norm(x, g, b, eps=1e-05):
            mu = jnp.mean(x, axis=-1, keepdims=True)
            var = jnp.mean(jnp.square(x - mu), axis=-1, keepdims=True)
            return (x - mu) * jax.lax.rsqrt(var + eps) * g + b

        def _fourier_kernel(x, proj_mat):
            p = jnp.einsum('blhd,dm->blhm', x, proj_mat) / math.sqrt(D_HEAD)
            return jnp.concatenate([jnp.cos(p), jnp.sin(p)], axis=-1) / math.sqrt(D_KMAP)
        B, L, _ = x.shape
        x2 = _layer_norm(x, ln1_g, ln1_b)
        q = (x2 @ wq + bq).reshape(B, L, N_HEAD, D_HEAD)
        k = (x2 @ wk + bk).reshape(B, L, N_HEAD, D_HEAD)
        v = (x2 @ wv + bv).reshape(B, L, N_HEAD, D_HEAD)
        qp = _fourier_kernel(q, proj_mat)
        kp = _fourier_kernel(k, proj_mat)
        kv = jnp.einsum('blhm,blhd->bhmd', kp, v)
        attn = jnp.einsum('blhm,bhmd->blhd', qp, kv)
        attn = attn.reshape(B, L, D_MODEL) @ wo + bo
        x = x + attn
        x2 = _layer_norm(x, ln2_g, ln2_b)
        h = jax.nn.relu(x2 @ w1 + b1)
        x = x + (h @ w2 + b2)
        return x

    def _L0_ffn_ref(hidden_states, gate_w, w1, w2, w3):
        import jax, jax.numpy as jnp
        import numpy as np
        E = 8
        H = 256
        F = 896
        JITTER_EPS = 0.01

        def _route(scores):
            vals, idx = jax.lax.top_k(scores, 2)
            neg_inf = -jnp.inf
            t1 = vals[:, 0:1]
            factor1 = jnp.maximum(jnp.abs(scores), t1)
            mask1 = (t1 - scores) / factor1 > 2 * JITTER_EPS
            p1 = jax.nn.softmax(jnp.where(mask1, neg_inf, scores), axis=-1)
            mult1 = jnp.take_along_axis(p1, idx[:, 0:1], axis=-1)
            t2 = vals[:, 1:2]
            factor2 = jnp.maximum(jnp.abs(scores), t2)
            mask2 = (t2 - scores) / factor2 > 2 * JITTER_EPS
            onehot0 = jax.nn.one_hot(idx[:, 0], scores.shape[-1], dtype=bool)
            scores2 = jnp.where(onehot0, neg_inf, scores)
            p2 = jax.nn.softmax(jnp.where(mask2, neg_inf, scores2), axis=-1)
            mult2 = jnp.take_along_axis(p2, idx[:, 1:2], axis=-1)
            return (jnp.concatenate([mult1, mult2], axis=-1), idx)
        B, S, Hd = hidden_states.shape
        x = hidden_states.reshape(-1, Hd)
        scores = x @ gate_w.T
        mult, idx = _route(scores)
        g = (jax.nn.one_hot(idx, E, dtype=x.dtype) * mult[..., None]).sum(axis=1)
        h1 = jnp.einsum('th,efh->tef', x, w1)
        h3 = jnp.einsum('th,efh->tef', x, w3)
        inter = jax.nn.silu(h1) * h3 * g[:, :, None]
        y = jnp.einsum('tef,ehf->th', inter, w2)
        return y.reshape(B, S, Hd)

    def _L1_attn_ref(hidden_states, Wq, bq, Wk, bk, Wv, bv, Wo, bo, lambda_q1, lambda_k1, lambda_q2, lambda_k2, ln_w, ln_b):
        import jax, jax.numpy as jnp
        import numpy as np
        B, S, H = (8, 256, 256)
        HEADS = 8
        HD = H // HEADS
        LAMBDA_INIT = 0.8
        LN_EPS = 1e-05
        b, s, h = hidden_states.shape
        q = hidden_states @ Wq + bq
        k = hidden_states @ Wk + bk
        v = hidden_states @ Wv + bv
        q = q.reshape(b, s, HEADS, HD).transpose(0, 2, 1, 3)
        k = k.reshape(b, s, HEADS, HD).transpose(0, 2, 1, 3)
        v = v.reshape(b, s, HEADS, HD).transpose(0, 2, 1, 3)
        scores = jnp.einsum('bhqd,bhkd->bhqk', q, k) / jnp.sqrt(jnp.float32(HD))
        attn = jax.nn.softmax(scores, axis=-1)
        half = HEADS // 2
        v1 = jnp.concatenate([v[:, :half], v[:, :half]], axis=1)
        v2 = jnp.concatenate([v[:, half:], v[:, half:]], axis=1)
        out1 = jnp.einsum('bhqk,bhkd->bhqd', attn, v1)
        out2 = jnp.einsum('bhqk,bhkd->bhqd', attn, v2)
        lam1 = jnp.exp(jnp.sum(lambda_q1 * lambda_k1))
        lam2 = jnp.exp(jnp.sum(lambda_q2 * lambda_k2))
        lam = lam1 - lam2 + LAMBDA_INIT
        attn_out = out1 - lam * out2
        attn_out = attn_out.transpose(0, 2, 1, 3).reshape(b, s, h)
        mu = jnp.mean(attn_out, axis=-1, keepdims=True)
        var = jnp.var(attn_out, axis=-1, keepdims=True)
        normed = (attn_out - mu) / jnp.sqrt(var + LN_EPS) * ln_w + ln_b
        attn_out = (1.0 - LAMBDA_INIT) * normed
        return attn_out @ Wo + bo

    def _L1_ffn_ref(x, W_gate, W1, b1, W2, b2):
        import jax, jax.numpy as jnp
        import numpy as np
        B, S, D, E, K = (2, 512, 256, 8, 2)
        H = 4 * D
        gate = jnp.einsum('bsd,de->bse', x, W_gate)
        kth = jax.lax.top_k(gate, K)[0][..., -1:]
        mask = jax.nn.softmax(jnp.where(gate >= kth, gate, -jnp.inf), axis=-1)
        h = jax.nn.relu(jnp.einsum('bsd,edh->bseh', x, W1) + b1)
        y = jnp.einsum('bseh,ehd->bsed', h, W2) + b2
        return (y * mask[..., None]).mean(axis=-2)

    def _L2_attn_ref(x, qkv_weight, proj_weight, proj_bias):
        import jax, jax.numpy as jnp
        import numpy as np
        NUM_HEADS = 32
        EPS = 1e-15
        B, N, C = x.shape
        H = NUM_HEADS
        D = C // H
        qkv = jax.nn.relu(jnp.einsum('bnc,oc->bno', x, qkv_weight))
        qkv = qkv.reshape(B, N, 3, H, D)
        q, k, v = (qkv[:, :, 0], qkv[:, :, 1], qkv[:, :, 2])
        v_pad = jnp.concatenate([v, jnp.ones((B, N, H, 1), dtype=v.dtype)], axis=-1)
        vk = jnp.einsum('bnhe,bnhd->bhed', v_pad.astype(jnp.float32), k.astype(jnp.float32))
        vk_q = jnp.einsum('bhed,bnhd->bnhe', vk, q.astype(jnp.float32))
        proj_input = (vk_q[..., :D] / (vk_q[..., D:] + EPS)).astype(qkv.dtype)
        proj_input = proj_input.reshape(B, N, C)
        y = jnp.einsum('bnc,oc->bno', proj_input, proj_weight) + proj_bias
        return y

    def _L2_ffn_ref(x, gate_w, gate_b, w1, b1, w2, b2, w3, b3):
        import jax, jax.numpy as jnp
        import numpy as np
        B, S, D, O, E, K = (2, 512, 256, 256, 8, 2)
        probs = jax.nn.softmax(x @ gate_w.T + gate_b, axis=-1)
        _, topi = jax.lax.top_k(probs, K)
        onehot = jax.nn.one_hot(topi, E, dtype=probs.dtype)
        cw = jnp.einsum('bske,bsk->bse', onehot, probs[..., :K])
        out = jnp.zeros(x.shape[:2] + (O,), x.dtype)
        for e in range(E):
            h = jax.nn.relu(x @ w1[e] + b1[e])
            h = jax.nn.relu(h @ w2[e] + b2[e])
            h = h @ w3[e] + b3[e]
            out = out + cw[..., e:e + 1] * h
        return out

    def _L3_attn_ref(x, Wq, Wk, Wv, Wo, bo):
        import jax, jax.numpy as jnp
        import numpy as np
        B, S, D_IN, D_OUT, H = (2, 512, 256, 256, 16)
        HD = D_OUT // H
        b, s, _ = x.shape

        def to_heads(t):
            return t.reshape(b, s, H, HD).transpose(0, 2, 1, 3)
        Q = to_heads(x @ Wq)
        K = to_heads(x @ Wk)
        V = to_heads(x @ Wv)
        scale = 1.0 / jnp.sqrt(jnp.asarray(HD, x.dtype))
        scores = jnp.einsum('bhqd,bhkd->bhqk', Q, K) * scale
        causal_mask = jnp.triu(jnp.ones((s, s), dtype=bool), k=1)
        scores = jnp.where(causal_mask, jnp.asarray(-1000000.0, scores.dtype), scores)
        weights = jax.nn.softmax(scores, axis=-1)
        attn = jnp.einsum('bhqk,bhkd->bhqd', weights, V)
        attn = attn.reshape(b, s, D_OUT)
        return attn @ Wo + bo

    def _L3_ffn_ref(x, W_sw, b_sw, W1, b1, W2, b2):
        import jax, jax.numpy as jnp
        import numpy as np
        HIDDEN = 256
        FF = 1024
        N_EXPERTS = 8
        CAP_FACTOR = 1.0
        B, S = (4, 512)
        STD = 0.02

        def _gelu(x):
            return x * 0.5 * (1.0 + jax.lax.erf(x / 1.41421))
        Bb, Ss, D = x.shape
        T = Bb * Ss
        E = W1.shape[0]
        capacity = int(CAP_FACTOR * T / E)
        xf = x.reshape(T, D)
        logits = xf @ W_sw + b_sw
        probs = jax.nn.softmax(logits, axis=-1)
        pmax = jnp.max(probs, axis=-1)
        routes = jnp.argmax(probs, axis=-1)
        factor = pmax / jax.lax.stop_gradient(pmax)
        xs = xf * factor[:, None]
        onehot = jax.nn.one_hot(routes, E, dtype=jnp.int32)
        pos = jnp.cumsum(onehot, axis=0) - 1
        pos_tok = jnp.take_along_axis(pos, routes[:, None], axis=1)[:, 0]
        keep = pos_tok < capacity
        pos_safe = jnp.where(keep, pos_tok, capacity)
        buf = jnp.zeros((E, capacity + 1, D), dtype=xs.dtype)
        buf = buf.at[routes, pos_safe].set(xs)
        buf = buf[:, :capacity]
        h = _gelu(jnp.einsum('ecd,edf->ecf', buf, W1) + b1[:, None, :])
        expert_out = jnp.einsum('ecf,efd->ecd', h, W2) + b2[:, None, :]
        gathered = expert_out[routes, jnp.minimum(pos_tok, capacity - 1)]
        final = jnp.where(keep[:, None], gathered, xs)
        return final.reshape(Bb, Ss, D)
    h = _L0_tok_ref(x, L0_tok_W, L0_tok_b, L0_tok_cls_token, L0_tok_pos_embed)
    h = jnp.concatenate([jnp.broadcast_to(cls_tok, (h.shape[0], 1, h.shape[2])), h], axis=1)
    h = h + _L0_attn_ref(_layernorm(h, axis=-1), L0_attn_proj_mat, L0_attn_wq, L0_attn_bq, L0_attn_wk, L0_attn_bk, L0_attn_wv, L0_attn_bv, L0_attn_wo, L0_attn_bo, L0_attn_ln1_g, L0_attn_ln1_b, L0_attn_w1, L0_attn_b1, L0_attn_w2, L0_attn_b2, L0_attn_ln2_g, L0_attn_ln2_b)
    h = h + _L0_ffn_ref(_layernorm(h, axis=-1), L0_ffn_gate_w, L0_ffn_w1, L0_ffn_w2, L0_ffn_w3)
    h = h + _L1_attn_ref(_layernorm(h, axis=-1), L1_attn_Wq, L1_attn_bq, L1_attn_Wk, L1_attn_bk, L1_attn_Wv, L1_attn_bv, L1_attn_Wo, L1_attn_bo, L1_attn_lambda_q1, L1_attn_lambda_k1, L1_attn_lambda_q2, L1_attn_lambda_k2, L1_attn_ln_w, L1_attn_ln_b)
    h = h + _L1_ffn_ref(_layernorm(h, axis=-1), L1_ffn_W_gate, L1_ffn_W1, L1_ffn_b1, L1_ffn_W2, L1_ffn_b2)
    h = h + _L2_attn_ref(_layernorm(h, axis=-1), L2_attn_qkv_weight, L2_attn_proj_weight, L2_attn_proj_bias)
    h = h + _L2_ffn_ref(_layernorm(h, axis=-1), L2_ffn_gate_w, L2_ffn_gate_b, L2_ffn_w1, L2_ffn_b1, L2_ffn_w2, L2_ffn_b2, L2_ffn_w3, L2_ffn_b3)
    h = h + _L3_attn_ref(_layernorm(h, axis=-1), L3_attn_Wq, L3_attn_Wk, L3_attn_Wv, L3_attn_Wo, L3_attn_bo)
    h = h + _L3_ffn_ref(_layernorm(h, axis=-1), L3_ffn_W_sw, L3_ffn_b_sw, L3_ffn_W1, L3_ffn_b1, L3_ffn_W2, L3_ffn_b2)
    return h

_drawn_inputs = setup_inputs


def setup_inputs(seed=0):
    import zlib

    import numpy as np

    out = dict(_drawn_inputs(seed))
    spreads = {'L0_attn_bq': (0.0, 0.273),
     'L0_attn_bk': (0.0, 0.1),
     'L0_attn_bv': (0.0, 0.1),
     'L0_attn_bo': (0.0, 0.1),
     'L0_attn_ln1_g': (1.0, 0.2),
     'L0_attn_ln1_b': (0.0, 0.1),
     'L0_attn_b1': (0.0, 0.1),
     'L0_attn_b2': (0.0, 0.1),
     'L0_attn_ln2_g': (1.0, 0.2),
     'L0_attn_ln2_b': (0.0, 0.365),
     'L1_attn_bq': (0.0, 0.393),
     'L1_attn_bk': (0.0, 2.0),
     'L1_attn_bv': (0.0, 0.1),
     'L1_attn_bo': (0.0, 0.1),
     'L1_attn_ln_w': (1.0, 0.2),
     'L1_attn_ln_b': (0.0, 0.1),
     'L2_ffn_gate_b': (0.0, 0.1),
     'L2_ffn_b1': (0.0, 0.355),
     'L2_ffn_b2': (0.0, 0.272),
     'L2_ffn_b3': (0.0, 0.357),
     'L3_ffn_b_sw': (0.0, 0.1),
     'L3_ffn_b1': (0.0, 0.8),
     'L3_ffn_b2': (0.0, 0.307)}
    factors = {'L0_attn_proj_mat': 2.731,
     'L1_attn_lambda_q1': 8.0,
     'L1_attn_lambda_k1': 133.761,
     'L1_attn_lambda_q2': 132.493,
     'L1_attn_lambda_k2': 200.0,
     'L1_ffn_W1': 2.838,
     'L1_ffn_b1': 13.981,
     'L1_ffn_b2': 21.713,
     'L3_attn_Wq': 8.0,
     'L3_attn_Wk': 8.0,
     'L2_attn_proj_bias': 4.692}
    for name, (base, spread) in spreads.items():
        noise = np.random.default_rng([zlib.crc32(name.encode()), seed]).standard_normal(out[name].shape)
        drawn = base * np.exp(spread * noise) if base else spread * noise
        out[name] = jnp.asarray(drawn.astype(out[name].dtype))
    for name, factor in factors.items():
        out[name] = (out[name] * factor).astype(out[name].dtype)
    return out
```

```python
from contextlib import ExitStack

import concourse.bass as bass
from concourse import mybir

F32 = mybir.dt.float32
ALU = mybir.AluOpType
ACT = mybir.ActivationFunctionType
AX = mybir.AxisListType.X

P = 128
IMAGES, PATCHES, D = 16, 36, 256
SEQ = PATCHES + 2
TOK = IMAGES * SEQ
PER = 3
GT = PER * SEQ
G = -(-IMAGES // PER)
SLOTS = G * GT
C = D // P
HT = TOK // 2
HS = SLOTS // 2
PD = 768
PC = PD // P
E = 8
CAP = TOK // E
EPS = 1e-5
NEG = -1e30
MAGIC = 12582912.0
TWO_PI = 6.2831850
F0, F1 = 7, 8
ROW = ["L0_bv", "L0_bo", "L0_b2", "L1_bv", "L1_bo", "L2_bo", "L3_bo", "gate_b"]
COL = ["L0_bq", "L0_bk", "L0_g1", "L0_n1", "L0_g2", "L0_n2", "L1_bq", "L1_bk", "L1_g", "L1_n"]
ATTN = ["L0", "L1", "L2", "L3"]


def build(nc, t):
    ctx = ExitStack()
    with ctx:
        def sb(name, shape, dt=F32):
            return ctx.enter_context(nc.sbuf_tensor(name, shape, dt))

        sems = {}

        def sem(name):
            if name not in sems:
                sems[name] = ctx.enter_context(nc.semaphore(name))
            return sems[name]

        bank = [ctx.enter_context(nc.psum_tensor(f"bank{i}", [P, 512], F32)) for i in range(8)]

        H = sb("H", [P, G, D])
        R0 = sb("R0", [P, G, D])
        X = sb("X", [P, G, D])
        O = sb("O", [P, G, D])
        XT = sb("XT", [P, C, SLOTS])
        QT = sb("QT", [P, C, SLOTS])
        KT = sb("KT", [P, C, SLOTS])
        V = sb("V", [P, G, 16 * 17])
        stats = sb("stats", [P, G, 6])
        mv = sb("mv", [P, G, 2])
        sd = sb("sd", [P, G])
        rs = sb("rs", [P, G])
        wA = [sb(f"wA{i}", [P, 4 * C * D]) for i in range(2)]
        EXP0 = C * F0 * P * 2 + F0 * D
        EXP1 = C * F1 * P + F1 * D + F1
        EXP2 = 3 * C * D + 4
        wE = [sb(f"wE{i}", [P, max(EXP0, EXP1)]) for i in range(2)]
        arena = sb("arena", [P, 2 * 8 * SLOTS])
        arena2 = sb("arena2", [P, 3 * 16 * GT])
        hT = sb("hT", [P, 8, TOK])
        act1 = hT[:, 6, :].rearrange("p (h n) -> p h n", h=2)
        ident = sb("ident", [P, P])
        ones = sb("ones", [P, P])
        tri = sb("tri", [P, P])
        same = sb("same", [P, GT])
        far = sb("far", [P, GT])
        causal = sb("causal", [P, GT])
        head16 = sb("head16", [P, 8])
        head32 = sb("head32", [P, 4])
        block8 = sb("block8", [P, P])
        iotaE = sb("iotaE", [P, E])
        revE = sb("revE", [P, E])
        slot_id = sb("slot_id", [P, TOK])
        slot_own = sb("slot_own", [P, E])
        i32 = hT[:, 7, :].bitcast(mybir.dt.int32)
        rows = sb("rows", [1, len(ROW) * D])
        cols = sb("cols", [P, len(COL) * C])
        gates = sb("gates", [P, 4, C, E])
        tab = sb("tab", [E, 2, D])
        lam_in = sb("lam_in", [P, 4, 32])
        lam = sb("lam", [P, 8])
        proj8 = hT[:, 2:4, 0:4 * P].rearrange("p a (h n) -> p a h n", h=4)
        posA = arena[:, PC * (SLOTS + D):PC * (SLOTS + D) + 2 * D].rearrange("p (a n) -> p a n", a=2)
        score = sb("score", [P, G, E])
        rt = sb("rt", [P, 12, G, E])
        r1 = sb("r1", [P, 8, G])
        gate = sb("gate", [P, G, E])
        gateT = QT[0:E, 0, :].rearrange("p (g n) -> p g n", g=G)
        gcur = sb("gcur", [P, 2, G])
        b1s = sb("b1s", [P, 2, F1])
        b2all = wA[0][:, :].rearrange("p (e n) -> p e n", e=E)
        r_mx = sb("r_mx", [P, 3, 16])
        eps = sb("eps", [P, 2])
        aff = sb("aff", [P, 4])
        ksum = arena2[:, 2 * C * D:2 * C * D + 4 * SEQ].rearrange("p (a n) -> p a n", a=2)

        def row(name):
            i = ROW.index(name)
            return rows[0:1, i * D:(i + 1) * D]

        def col(name, c):
            i = COL.index(name)
            return cols[:, i * C + c:i * C + c + 1]

        def a_w(layer, which):
            v = wA[layer % 2][:, which * C * D:(which + 1) * C * D]
            return v.rearrange("p (c n) -> p c n", c=C)

        def tok(g):
            return slice(g * GT, (g + 1) * GT)

        class Chain:

            def __init__(self, name):
                self.s, self.n = sem(name), 0

            def link(self, eng, ins):
                self.n += 1
                ins.then_inc(self.s, 1)
                eng.wait_ge(self.s, self.n)

        vchain = Chain("vector_order")
        pchain = Chain("pool_order")
        heads_dram = nc.dram_tensor("heads_by_image", (IMAGES * 16 * SEQ * 16,), F32, kind="Internal").ap()
        by_head = heads_dram.rearrange("(i h q d) -> i h q d", i=IMAGES, h=16, q=SEQ)
        by_token = heads_dram.rearrange("(n d) -> n d", d=D)
        in_small, in_patch, in_proj = sem("in_small"), sem("in_patch"), sem("in_proj")
        in_attn = [sem("in_attn0"), sem("in_attn1")]
        in_exp = [sem("in_exp0"), sem("in_exp1")]
        consts = sem("consts")
        stored = sem("stored")

        NORMS = ["L0i_", "L0_", "L0m_", "L0f_", "L1_", "L1o_", "L1f_", "L2_", "L2f_", "L3_", "L3f_"]
        TURNS = ["L0_", "L0o_", "L0m_", "L0f_", "L1_", "L1o_", "L1f_", "L2_", "L2f_", "L3_", "L3o_", "L3f_"]
        stats_done, var_done, sd_done = sem("stats_done"), sem("var_done"), sem("sd_done")
        turned, xt_done = sem("turned"), sem("xt_done")
        norm_nth = NORMS.index

        normed = sem("normed")

        def normed_of(s):
            return lambda g: (normed, norm_nth(s) * G + g + 1)

        def xt_count(s, n):
            return TURNS.index(s) * G + n

        def norm_vector(v, s, src, dst):
            for g in range(G):
                v.bn_stats(stats[0:GT, g, :], src[0:GT, g, :]).then_inc(stats_done, 1)
            v.wait_ge(stats_done, (norm_nth(s) + 1) * G)
            for g in range(G):
                last = v.bn_aggr(mv[0:GT, g, :], stats[0:GT, g, :])
            last.then_inc(var_done, 1)
            v.wait_ge(sd_done, norm_nth(s) + 1)
            vchain.link(v, v.reciprocal(rs[0:GT, :], sd[0:GT, :]))
            for g in range(G):
                v.tensor_scalar(dst[0:GT, g, :], src[0:GT, g, :], mv[0:GT, g, 0:1], rs[0:GT, g:g + 1],
                                ALU.subtract, ALU.mult).then_inc(normed, 1)

        def norm_scalar(a, s):
            a.wait_ge(var_done, norm_nth(s) + 1)
            a.activation(sd[0:GT, :], mv[0:GT, :, 1], ACT.Sqrt, bias=eps[0:GT, 0:1]).then_inc(sd_done, 1)

        def turn_tensor(pe, s, src, ready):
            for g in range(G):
                pe.wait_ge(*ready(g))
                if g >= 2:
                    pe.wait_ge(xt_done, xt_count(s, g - 1))
                for c in range(C):
                    last = pe.transpose(bank[g % 2][:, c * GT:(c + 1) * GT],
                                        src[0:GT, g, c * P:(c + 1) * P], ident[0:GT, 0:GT])
                last.then_inc(turned, 1)

        def turn_scalar(a, s, scale=None, shift=None):
            for g in range(G):
                a.wait_ge(turned, xt_count(s, g + 1))
                if scale is None:
                    last = a.activation(XT[:, :, tok(g)], bank[g % 2][:, 0:C * GT].rearrange("p (c n) -> p c n", c=C),
                                        ACT.Copy)
                else:
                    for c in range(C):
                        last = a.activation(XT[:, c, tok(g)], bank[g % 2][:, c * GT:(c + 1) * GT],
                                            ACT.Identity, bias=shift(c), scale=scale(c))
                last.then_inc(xt_done, 1)

        def qk_tensor(pe, s, layer, which):
            pe.wait_ge(in_attn[layer % 2], 16 * (layer // 2 + 1))
            pe.wait_ge(xt_done, xt_count(s, G))
            u = 0
            for w in which:
                for c in range(C):
                    for half in range(2):
                        if u >= 4:
                            pe.wait_ge(sem(s + "qk_out"), u - 3)
                        for k in range(C):
                            last = pe.matmul(bank[2 + u % 4][:, 0:HS], a_w(layer, w)[:, k, c * P:(c + 1) * P],
                                             XT[:, k, half * HS:(half + 1) * HS], start=(k == 0), stop=(k == C - 1))
                        last.then_inc(sem(s + "qk"), 1)
                        u += 1

        def qk_scalar(a, s, which, func, bias):
            u = 0
            for w in which:
                for c in range(C):
                    for half in range(2):
                        a.wait_ge(sem(s + "qk"), u + 1)
                        dst = (QT, KT)[w][:, c, half * HS:(half + 1) * HS]
                        b = bias(w, c)
                        if b is None:
                            a.activation(dst, bank[2 + u % 4][:, 0:HS], func).then_inc(sem(s + "qk_out"), 1)
                        else:
                            a.activation(dst, bank[2 + u % 4][:, 0:HS], func, bias=b).then_inc(sem(s + "qk_out"), 1)
                        u += 1

        def v_tensor(pe, s, layer, bias):
            for g in range(G):
                if g >= 2:
                    pe.wait_ge(sem(s + "v_out"), g - 1)
                for k in range(C):
                    last = pe.matmul(bank[6 + g % 2][0:GT, 0:D], XT[:, k, tok(g)], a_w(layer, 2)[:, k, :],
                                     start=(k == 0), stop=(bias is None and k == C - 1))
                if bias is not None:
                    last = pe.matmul(bank[6 + g % 2][0:GT, 0:D], ones[0:1, 0:GT], bias, start=False, stop=True)
                last.then_inc(sem(s + "v"), 1)

        def v_vector(v, s, heads, hd):
            for g in range(G):
                v.wait_ge(sem(s + "v"), g + 1)
                v.tensor_copy(V[0:GT, g, 0:heads * (hd + 1)].rearrange("p (h d) -> p h d", h=heads)[:, :, 0:hd],
                              bank[6 + g % 2][0:GT, 0:D].rearrange("p (h d) -> p h d", h=heads))\
                    .then_inc(sem(s + "v_out"), 1)

        def v_ones(v, s, heads, hd):
            v.memset(V[0:GT, :, 0:heads * (hd + 1)].rearrange("p g (h d) -> p g h d", d=hd + 1)[:, :, :, hd],
                     1.0).then_inc(sem(s + "v_ones"), 1)

        def proj_tensor(pe, s, layer, ready, bias):
            for g in range(G):
                pe.wait_ge(*ready(g))
                if g >= 2:
                    pe.wait_ge(sem(s + "added"), g - 1)
                for k in range(C):
                    pe.matmul(bank[2 + g % 2][0:GT, 0:D], XT[:, k, tok(g)], a_w(layer, 3)[:, k, :],
                              start=(k == 0), stop=False)
                pe.matmul(bank[2 + g % 2][0:GT, 0:D], ones[0:1, 0:GT], bias, start=False, stop=True)\
                    .then_inc(sem(s + "proj"), 1)

        def proj_vector(v, s, dst, src):
            for g in range(G):
                v.wait_ge(sem(s + "proj"), g + 1)
                v.tensor_tensor(dst[0:GT, g, :], bank[2 + g % 2][0:GT, 0:D], src[0:GT, g, :], ALU.add)\
                    .then_inc(sem(s + "added"), 1)
            v.wait_ge(sem(s + "added"), G)

        def keys_vector(v, s, heads):
            per = heads // C
            KM = arena[:, 0:heads * SLOTS].rearrange("p (h n) -> p h n", h=heads)
            mask = head16 if per == 8 else head32
            v.wait_ge(sem(s + "qk_out"), 8)
            for h in range(heads):
                last = v.tensor_scalar(KM[:, h, :], KT[:, h // per, :], mask[:, h % per:h % per + 1], None, ALU.mult)
            last.then_inc(sem(s + "keys"), 1)

        def score_tensor(pe, s, g, heads):
            KM = arena[:, 0:heads * SLOTS].rearrange("p (h n) -> p h n", h=heads)
            if g == 0:
                pe.wait_ge(sem(s + "keys"), 1)
            else:
                pe.wait_ge(sem(s + "masked"), g)
            for j in range(heads // 4):
                c = j // (heads // 8)
                last = pe.matmul(bank[j][0:GT, 0:4 * GT], QT[:, c, tok(g)], KM[:, 4 * j:4 * j + 4, tok(g)],
                                 start=True, stop=True)
            last.then_inc(sem(s + "score"), 1)

        def score_vector(v, s, g, heads, mask):
            S = arena2[0:GT, (g % 2) * 16 * GT:((g % 2) * 16 + heads) * GT].rearrange("p (h n) -> p h n", h=heads)
            mx = arena2_mx(g, heads)
            v.wait_ge(sem(s + "score"), g + 1)
            if g >= 2:
                v.wait_ge(sem(s + "pT"), (g - 1) * (heads // 4))
            for j in range(heads // 4):
                last = v.tensor_tensor(S[:, 4 * j:4 * j + 4, :],
                                       bank[j][0:GT, 0:4 * GT].rearrange("p (h n) -> p h n", h=4),
                                       mask[0:GT, :].unsqueeze(1).to_broadcast([GT, 4, GT]), ALU.add)
            last.then_inc(sem(s + "masked"), 1)
            v.wait_ge(sem(s + "masked"), g + 1)
            vchain.link(v, v.tensor_reduce(mx, S, AX, ALU.max))
            v.tensor_tensor(S, S, mx.unsqueeze(2).to_broadcast([GT, heads, GT]), ALU.subtract)\
                .then_inc(sem(s + "shifted"), 1)

        def arena2_mx(g, heads):
            return r_mx[0:GT, g % 2, 0:heads]

        def soft_scalar(a, s, g, heads, scale):
            S = arena2[0:GT, (g % 2) * 16 * GT:((g % 2) * 16 + heads) * GT].rearrange("p (h n) -> p h n", h=heads)
            PT = arena2[0:GT, 32 * GT:(32 + heads) * GT].rearrange("p (h n) -> p h n", h=heads)
            a.wait_ge(sem(s + "shifted"), g + 1)
            a.activation(S, S, ACT.Exp, scale=scale).then_inc(sem(s + "exp"), 1)
            if g >= 1:
                a.wait_ge(sem(s + "pv"), g)
            for j in range(heads // 4):
                a.wait_ge(sem(s + "pT"), g * (heads // 4) + j + 1)
                a.activation(PT[:, 4 * j:4 * j + 4, :],
                             bank[4 + j % 2][0:GT, 0:4 * GT].rearrange("p (h n) -> p h n", h=4), ACT.Copy)\
                    .then_inc(sem(s + "pT_out"), 1)

        def pv_tensor(pe, s, g, heads, hd, shared):
            S = arena2[0:GT, (g % 2) * 16 * GT:((g % 2) * 16 + heads) * GT].rearrange("p (h n) -> p h n", h=heads)
            PT = arena2[0:GT, 32 * GT:(32 + heads) * GT].rearrange("p (h n) -> p h n", h=heads)
            pe.wait_ge(sem(s + "exp"), g + 1)
            for j in range(heads // 4):
                n = g * (heads // 4) + j
                if n >= 2:
                    pe.wait_ge(sem(s + "pT_out"), n - 1)
                for h in range(4):
                    last = pe.transpose(bank[4 + j % 2][0:GT, h * GT:(h + 1) * GT], S[:, 4 * j + h, :],
                                        ident[0:GT, 0:GT])
                last.then_inc(sem(s + "pT"), 1)
            pe.wait_ge(sem(s + "pT_out"), (g + 1) * (heads // 4))
            if g == 0:
                pe.wait_ge(sem(s + "v_out"), G)
                pe.wait_ge(sem(s + "v_ones"), 1)
            else:
                pe.wait_ge(sem(s + "o"), g)
            n = hd + 1
            for h in range(heads):
                hv = h % shared
                last = pe.matmul(bank[6][0:GT, h * n:(h + 1) * n], PT[:, h, :], V[0:GT, g, hv * n:(hv + 1) * n],
                                 start=True, stop=True)
            last.then_inc(sem(s + "pv"), 1)

        def out_vector(v, s, g, heads, hd):
            o = bank[6][0:GT, 0:heads * (hd + 1)].rearrange("p (h d) -> p h d", h=heads)
            den = r_mx[0:GT, 2, 0:heads]
            v.wait_ge(sem(s + "pv"), g + 1)
            if g:
                v.wait_ge(sem(s + "o"), g)
            vchain.link(v, v.reciprocal(den, o[:, :, hd]))
            v.tensor_tensor(O[0:GT, g, :].rearrange("p (h d) -> p h d", h=heads), o[:, :, 0:hd],
                            den.unsqueeze(2).to_broadcast([GT, heads, hd]), ALU.mult).then_inc(sem(s + "o"), 1)


        FE = arena[:, 0:32 * GT].rearrange("p (w h n) -> p w h n", w=2, h=16)
        FS = arena[:, 32 * GT:64 * GT].rearrange("p (w h n) -> p w h n", w=2, h=16)
        FC = arena2[:, 0:32 * GT].rearrange("p (w h n) -> p w h n", w=2, h=16)
        FPT = arena2[0:GT, 32 * GT:48 * GT].rearrange("p (h n) -> p h n", h=16)
        FR = hT[:, 0:2, 0:4 * GT]

        def fourier_tensor(pe, g):
            s = "L0_"
            if g == 0:
                pe.wait_ge(sem("proj_scaled"), 1)
                pe.wait_ge(sem(s + "qk_out"), 8)
            for w in range(2):
                for j in range(4):
                    u = g * 8 + w * 4 + j
                    if u >= 4:
                        pe.wait_ge(sem(s + "phase_out"), u - 3)
                    for h in range(4):
                        last = pe.matmul(bank[j][:, h * GT:(h + 1) * GT], proj8[:, j % 2, h, :],
                                         (QT, KT)[w][:, j // 2, tok(g)], start=True, stop=True)
                    last.then_inc(sem(s + "phase"), 1)

        def similar_tensor(pe, g):
            s = "L0_"
            pe.wait_ge(sem(s + "cos"), g + 1)
            for j in range(4):
                n = g * 4 + j
                if n >= 2:
                    pe.wait_ge(sem(s + "sim_out"), n - 1)
                for h in range(4):
                    for k, f in enumerate((FS, FC)):
                        last = pe.matmul(bank[4 + j % 2][0:GT, h * GT:(h + 1) * GT], f[:, 1, 4 * j + h, :],
                                         f[:, 0, 4 * j + h, :], start=(k == 0), stop=(k == 1))
                last.then_inc(sem(s + "sim"), 1)
            pe.wait_ge(sem(s + "sim_out"), 4 * g + 4)
            if g == 0:
                pe.wait_ge(sem(s + "v_out"), G)
            else:
                pe.wait_ge(sem(s + "o"), g)
            for h in range(16):
                last = pe.matmul(bank[6][0:GT, h * 16:(h + 1) * 16], FPT[:, h, :], V[0:GT, g, h * 17:h * 17 + 16],
                                 start=True, stop=True)
            last.then_inc(sem(s + "pv"), 1)

        def phase_vector(v, g):
            s = "L0_"
            for w in range(2):
                for j in range(4):
                    u = g * 8 + w * 4 + j
                    v.wait_ge(sem(s + "phase"), u + 1)
                    if u >= 2:
                        v.wait_ge(sem(s + "phase_out"), u - 1)
                    if g and u % 8 == 0:
                        v.wait_ge(sem(s + "sin"), g)
                    vchain.link(v, v.tensor_scalar(FR[:, u % 2, :], bank[j][:, 0:4 * GT], MAGIC, -MAGIC,
                                                   ALU.add, ALU.add))
                    v.tensor_tensor(FE[:, w, 4 * j:4 * j + 4, :],
                                    bank[j][:, 0:4 * GT].rearrange("p (h n) -> p h n", h=4),
                                    FR[:, u % 2, :].rearrange("p (h n) -> p h n", h=4), ALU.subtract)\
                        .then_inc(sem(s + "phase_out"), 1)

        def similar_vector(v, g):
            s = "L0_"
            for j in range(4):
                v.wait_ge(sem(s + "sim"), 4 * g + j + 1)
                if j == 0 and g:
                    v.wait_ge(sem(s + "pv"), g)
                v.scalar_tensor_tensor(FPT[:, 4 * j:4 * j + 4, :],
                                       bank[4 + j % 2][0:GT, 0:4 * GT].rearrange("p (h n) -> p h n", h=4),
                                       1.0 / 128, same[0:GT, :].unsqueeze(1).to_broadcast([GT, 4, GT]),
                                       ALU.mult, ALU.mult).then_inc(sem(s + "sim_out"), 1)
            v.wait_ge(sem(s + "pv"), g + 1)
            v.tensor_copy(O[0:GT, g, :], bank[6][0:GT, 0:D]).then_inc(sem(s + "o"), 1)

        def fourier_scalar(a, g):
            s = "L0_"
            a.wait_ge(sem(s + "phase_out"), 8 * g + 8)
            if g:
                a.wait_ge(sem(s + "sim"), 4 * g)
            for w in range(2):
                last = a.activation(FC[:, w], FE[:, w], ACT.Abs)
            last.then_inc(sem(s + "abs"), 1)
            for w in range(2):
                last = a.activation(FS[:, w], FE[:, w], ACT.Sin, scale=TWO_PI)
            last.then_inc(sem(s + "sin"), 1)
            a.wait_ge(sem(s + "abs"), g + 1)
            for w in range(2):
                last = a.activation(FC[:, w], FC[:, w], ACT.Sin, scale=-TWO_PI, bias=eps[:, 1:2])
            last.then_inc(sem(s + "cos"), 1)

        KV = arena[0:SEQ, 0:IMAGES * 2 * D].rearrange("p (i n) -> p i n", i=IMAGES)
        KVM = arena2[:, 0:2 * C * D].rearrange("p (b c n) -> p b c n", b=2, c=C)

        def linear_tensor(pe):
            s = "L2_"
            pe.wait_ge(sem(s + "qk_out"), 4)
            for i in range(IMAGES):
                if i >= 2:
                    pe.wait_ge(sem(s + "kv_out"), i - 1)
                for k in range(C):
                    last = pe.matmul(bank[6 + i % 2][0:SEQ, :], XT[:, k, i * SEQ:(i + 1) * SEQ],
                                     wA[0][:, D * C:3 * D * C].rearrange("p (c n) -> p c n", c=C)[:, k, :],
                                     start=(k == 0), stop=(k == C - 1))
                last.then_inc(sem(s + "kv"), 1)
            pe.wait_ge(sem(s + "kv_out"), IMAGES)
            for i in range(IMAGES):
                if i >= 2:
                    pe.wait_ge(sem(s + "outer_out"), i - 1)
                for c in range(C):
                    k = KV[:, i, c * P:(c + 1) * P]
                    pe.matmul(bank[i % 2][:, c * 129:c * 129 + P], k, KV[:, i, D + c * P:D + (c + 1) * P],
                              start=True, stop=True)
                    last = pe.matmul(bank[i % 2][:, c * 129 + P:c * 129 + 129], k, ones[0:SEQ, 0:1],
                                     start=True, stop=True)
                last.then_inc(sem(s + "outer"), 1)
                if i:
                    linear_apply(pe, i - 1)
            linear_apply(pe, IMAGES - 1)

        def linear_apply(pe, i):
            s = "L2_"
            pe.wait_ge(sem(s + "outer_out"), i + 1)
            if i >= 2:
                pe.wait_ge(sem(s + "image"), i - 1)
            for half in range(2):
                for c in range(C):
                    o = (half * C + c) * SEQ
                    last = pe.matmul(bank[4 + i % 2][:, o:o + SEQ], KVM[:, i % 2, c, half * P:(half + 1) * P],
                                     QT[:, c, i * SEQ:(i + 1) * SEQ], start=True, stop=True)
            last.then_inc(sem(s + "applied"), 1)

        def linear_vector(v):
            s = "L2_"
            for i in range(IMAGES):
                v.wait_ge(sem(s + "outer"), i + 1)
                if i >= 2:
                    v.wait_ge(sem(s + "applied"), i - 1)
                for c in range(C):
                    b = bank[i % 2]
                    v.tensor_tensor(KVM[:, i % 2, c, 0:P], b[:, c * 129:c * 129 + P], block8[:, :], ALU.mult)
                    last = v.tensor_scalar(KVM[:, i % 2, c, P:2 * P], block8[:, :],
                                           b[:, c * 129 + P:c * 129 + 129], None, ALU.mult)
                last.then_inc(sem(s + "outer_out"), 1)
                if i:
                    linear_divide(v, i - 1)
            linear_divide(v, IMAGES - 1)

        def linear_divide(v, i):
            s = "L2_"
            v.wait_ge(sem(s + "applied"), i + 1)
            b = bank[4 + i % 2]
            vchain.link(v, v.tensor_scalar(ksum[:, 0, :], b[:, 2 * SEQ:4 * SEQ], 1e-15, None, ALU.add))
            vchain.link(v, v.reciprocal(ksum[:, 1, :], ksum[:, 0, :]))
            v.tensor_tensor(XT[:, :, i * SEQ:(i + 1) * SEQ], b[:, 0:2 * SEQ].rearrange("p (c n) -> p c n", c=C),
                            ksum[:, 1, :].rearrange("p (c n) -> p c n", c=C), ALU.mult).then_inc(sem(s + "image"), 1)

        def linear_scalar(a):
            s = "L2_"
            for i in range(IMAGES):
                a.wait_ge(sem(s + "kv"), i + 1)
                a.activation(KV[:, i, :], bank[6 + i % 2][0:SEQ, :], ACT.Relu).then_inc(sem(s + "kv_out"), 1)

        def relu_w(b, nf, last=False):
            w = wE[b]
            w1 = w[:, 0:C * nf * P].rearrange("p (c n) -> p c n", c=C)
            w2 = w[:, C * nf * P:C * nf * P + nf * D].rearrange("p (f n) -> p f n", f=nf)
            b1 = w[:, C * nf * P + nf * D:C * nf * P + nf * D + nf]
            return w1, w2, b1

        def silu_w(b):
            w = wE[b]
            n = C * F0 * P
            return (w[:, 0:n].rearrange("p (c n) -> p c n", c=C), w[:, n:2 * n].rearrange("p (c n) -> p c n", c=C),
                    w[:, 2 * n:2 * n + F0 * D].rearrange("p (f n) -> p f n", f=F0))

        def half_of(h):
            return slice(h * HT, (h + 1) * HT)

        def y_bank(g):
            return bank[4 + g // 2][0:GT, (g % 2) * D:(g % 2) * D + D]

        def y_rows(g):
            return min(GT, TOK - g * GT)

        def y_tensor(pe, s, i, b, f, nf, slot, w2, hready):
            for half in range(2):
                pe.wait_ge(sem(s + f"h_ready{half}"), hready)
            if f == 0:
                pe.wait_ge(sem(s + "y_added"), 6 * (2 * i + b) + 6)
            for g in range(G):
                n = y_rows(g)
                last = pe.matmul(y_bank(g)[0:n, :], hT[:, slot, g * GT:g * GT + n], w2, start=(f == 0 and g % 2 == 0),
                                 stop=(f == nf - 1), skip_group_check=True)
            last.then_inc(sem(s + "y"), 1)

        def ffn_tensor(pe, s, kind, nf, wave, bufs, rounds):
            units = len(bufs) * nf

            def body(i):
                for k in range(units):
                    b, f = bufs[k // nf], k % nf
                    if f == 0:
                        pe.wait_ge(in_exp[b], 16 * (i + wave + 2 - b))
                    for half in range(2):
                        pe.wait_ge(sem(s + f"h_ready{half}"), i * units + k + 1)
                        if kind == "silu":
                            w1, w3, _ = silu_w(b)
                            pairs = ((bank[2 * half], w1), (bank[2 * half + 1], w3))
                        else:
                            pairs = ((bank[2 * (k % 2) + half], relu_w(b, nf)[0]),)
                        for dst, w in pairs:
                            for c in range(C):
                                last = pe.matmul(dst[:, 0:HT], w[:, c, f * P:(f + 1) * P], XT[:, c, half_of(half)],
                                                 start=(c == 0), stop=(c == C - 1))
                        last.then_inc(sem(s + f"h{half}"), 1)
                    if k:
                        y(i, k - 1)
                y(i, units - 1)

            def y(i, k):
                b, f = bufs[k // nf], k % nf
                w2 = silu_w(b)[2] if kind == "silu" else relu_w(b, nf)[1]
                y_tensor(pe, s, i, k // nf, f, nf, k % 2, w2[:, f, :],
                         i * units + k + 1 + (1 if kind == "silu" else 2))

            if rounds == 1:
                body(0)
            else:
                with pe.Fori(0, rounds) as i:
                    body(i)

        def free_banks(eng, s, half, n):
            eng.sem_inc(sem(s + f"h_ready{half}"), n)

        def y_vector(v, s, i, b, units_done, nf, gcol):
            v.wait_ge(sem(s + "y"), units_done)
            for g in range(G):
                n = y_rows(g)
                v.wait_ge(sem(s + "y_added"), 6 * (2 * i + b) + g + 1)
                if gcol is None:
                    v.tensor_tensor(dst_of(s)[0:n, g, :], y_bank(g)[0:n, :], dst_of(s)[0:n, g, :], ALU.add)\
                        .then_inc(sem(s + "y_added"), 1)
                else:
                    v.scalar_tensor_tensor(H[0:n, g, :], y_bank(g)[0:n, :], gcol(g)[0:n, :], H[0:n, g, :],
                                           ALU.mult, ALU.add).then_inc(sem(s + "y_added"), 1)

        def dst_of(s):
            return R0 if s == "L0m_" else H

        def ffn_vector(v, s, kind, nf, bufs, rounds):
            units = len(bufs) * nf

            def body(i):
                for k in range(units + 1):
                    if k < units:
                        b, f = bufs[k // nf], k % nf
                        if f == 0 and gated:
                            e = 2 * i + b
                            v.tensor_copy(gcur[0:GT, b, :], gate[0:GT, :, bass.ds(e, 1)].rearrange("p g e -> p (g e)"))\
                                .then_inc(sem(s + "gcur"), 1)
                        halves = (0, 1) if kind == "silu" else (1,)
                        for half in halves:
                            if kind == "silu":
                                v.wait_ge(sem(s + f"silu{half}"), i * units + k + 1)
                                v.tensor_tensor(hT[:, k % 2, half_of(half)], bank[2 * half + 1][:, 0:HT],
                                                act1[:, half, :], ALU.mult).then_inc(sem(s + f"h_ready{half}"), 1)
                            else:
                                v.wait_ge(sem(s + f"h{half}"), i * units + k + 1)
                                v.tensor_scalar(hT[:, k % 2, half_of(half)], bank[2 * (k % 2) + half][:, 0:HT],
                                                relu_w(b, nf)[2][:, f:f + 1], 0.0, ALU.add, ALU.max)\
                                    .then_inc(sem(s + f"h_ready{half}"), 1)
                    if k and k % nf == 0:
                        b = k // nf - 1
                        if gated:
                            v.wait_ge(sem(s + "gcur"), 2 * i + b + 1)
                        y_vector(v, s, i, b, i * units + k, nf, (lambda g, b=b: gcur[:, b, g:g + 1]) if gated else None)

            gated = s != "L0m_"
            if rounds == 1:
                body(0)
            else:
                with v.Fori(0, rounds) as i:
                    body(i)

        def ffn_scalar(a, s, kind, nf, bufs, rounds):
            units = len(bufs) * nf

            def body(i):
                for k in range(units):
                    b, f = bufs[k // nf], k % nf
                    for half in ((0, 1) if kind == "silu" else (0,)):
                        a.wait_ge(sem(s + f"h{half}"), i * units + k + 1)
                        if kind == "silu":
                            a.activation(act1[:, half, :], bank[2 * half][:, 0:HT], ACT.Silu)\
                                .then_inc(sem(s + f"silu{half}"), 1)
                        else:
                            a.activation(hT[:, k % 2, half_of(half)], bank[2 * (k % 2) + half][:, 0:HT], ACT.Relu,
                                         bias=relu_w(b, nf)[2][:, f:f + 1]).then_inc(sem(s + f"h_ready{half}"), 1)

            if rounds == 1:
                body(0)
            else:
                with a.Fori(0, rounds) as i:
                    body(i)

        def deep_w(b):
            w = wE[b]
            m = C * D
            return ([w[:, j * m:(j + 1) * m].rearrange("p (c n) -> p c n", c=C) for j in range(3)],
                    [w[:, 3 * m + 2 * j:3 * m + 2 * j + 2] for j in range(2)])

        def deep_tensor(pe, s, wave):
            with pe.Fori(0, E // 2) as i:
                for k in range(8):
                    layer, b, f = k // 4, k // 2 % 2, k % 2
                    if k % 2 == 0 and layer == 0:
                        pe.wait_ge(in_exp[b], 16 * (i + wave + 2 - b))
                    for half in range(2):
                        if layer == 1:
                            pe.wait_ge(sem(s + f"h_ready{half}"), i * 8 + 2 * b + 4)
                        pe.wait_ge(sem(s + f"h_ready{half}"), i * 8 + k + 1)
                        for c in range(C):
                            src = XT[:, c, half_of(half)] if layer == 0 else hT[:, 2 * b + c, half_of(half)]
                            last = pe.matmul(bank[2 * (k % 2) + half][:, 0:HT], deep_w(b)[0][layer][:, c, f * P:(f + 1) * P],
                                             src, start=(c == 0), stop=(c == C - 1))
                        last.then_inc(sem(s + f"h{half}"), 1)
                for b in range(2):
                    for f in range(2):
                        y_tensor(pe, s, i, b, f, 2, 4 + 2 * b + f, deep_w(b)[0][2][:, f, :], i * 8 + 8 + 2 * b)

        def deep_vector(v, s):
            with v.Fori(0, E // 2) as i:
                for k in range(8):
                    b = k // 2 % 2
                    if k < 4 and k % 2 == 0:
                        v.wait_ge(sem(s + "y_added"), 2 * G * i + G)
                        v.tensor_copy(gcur[0:GT, b, :], gate[0:GT, :, bass.ds(2 * i + b, 1)].rearrange("p g e -> p (g e)"))\
                            .then_inc(sem(s + "gcur"), 1)
                    v.wait_ge(sem(s + "h1"), i * 8 + k + 1)
                    v.tensor_scalar(hT[:, k, half_of(1)], bank[2 * (k % 2) + 1][:, 0:HT],
                                    deep_w(b)[1][k // 4][:, k % 2:k % 2 + 1], 0.0, ALU.add, ALU.max)\
                        .then_inc(sem(s + "h_ready1"), 1)
                v.wait_ge(sem(s + "gcur"), 2 * i + 2)
                for b in range(2):
                    y_vector(v, s, i, b, i * 4 + 2 * b + 2, 2, lambda g, b=b: gcur[:, b, g:g + 1])

        def deep_scalar(a, s):
            with a.Fori(0, E // 2) as i:
                for k in range(8):
                    b = k // 2 % 2
                    a.wait_ge(sem(s + "h0"), i * 8 + k + 1)
                    a.activation(hT[:, k, half_of(0)], bank[2 * (k % 2)][:, 0:HT], ACT.Relu,
                                 bias=deep_w(b)[1][k // 4][:, k % 2:k % 2 + 1]).then_inc(sem(s + "h_ready0"), 1)

        def gate_tensor(pe, s, which, bias):
            pe.wait_ge(xt_done, xt_count(s, G))
            for g in range(G):
                for k in range(C):
                    last = pe.matmul(bank[7][0:GT, g * E:(g + 1) * E], XT[:, k, tok(g)], gates[:, which, k, :],
                                     start=(k == 0), stop=(bias is None and k == C - 1))
                if bias is not None:
                    last = pe.matmul(bank[7][0:GT, g * E:(g + 1) * E], ones[0:1, 0:GT], bias, start=False, stop=True)
            last.then_inc(sem(s + "gate_mm"), 1)

        def wide(x):
            return x.unsqueeze(2).to_broadcast([GT, G, E])

        def over_groups(x):
            return x[0:GT, :].unsqueeze(1).to_broadcast([GT, G, E])

        def first_of(v, values, best, hot, tmp, one):
            vchain.link(v, v.tensor_tensor(tmp, values, wide(best), ALU.is_equal))
            vchain.link(v, v.tensor_tensor(tmp, tmp, over_groups(revE), ALU.mult))
            vchain.link(v, v.tensor_reduce(one, tmp, AX, ALU.max))
            vchain.link(v, v.tensor_tensor(hot, tmp, wide(one), ALU.is_equal))

        def R(i):
            return rt[0:GT, i]

        def r(i):
            return r1[0:GT, i]

        def get_scores(v, s):
            v.wait_ge(sem(s + "gate_mm"), 1)
            vchain.link(v, v.tensor_copy(score[0:GT], bank[7][0:GT, 0:G * E].rearrange("p (g e) -> p g e", g=G)))

        def exp_on_scalar(a, s, n, src, dst):
            a.wait_ge(sem(s + "to_exp"), n)
            a.activation(dst, src, ACT.Exp).then_inc(sem(s + "exped"), 1)

        def route0_vector(v):
            s = "L0f_"
            get_scores(v, s)
            S = score[0:GT]
            L = lambda ins: vchain.link(v, ins)
            L(v.tensor_reduce(r(0), S, AX, ALU.max))
            first_of(v, S, r(0), R(0), R(1), r(1))
            L(v.scalar_tensor_tensor(R(2), R(0), NEG, S, ALU.mult, ALU.add))
            L(v.tensor_reduce(r(2), R(2), AX, ALU.max))
            first_of(v, R(2), r(2), R(3), R(1), r(1))
            L(v.scalar_tensor_tensor(R(4), S, -1.0, S, ALU.mult, ALU.max))
            for n, (top, src, d, keep) in enumerate(((r(0), S, R(5), R(6)), (r(2), R(2), R(7), R(8)))):
                L(v.tensor_tensor(R(9), R(4), wide(top), ALU.max))
                L(v.tensor_tensor(R(10), S, wide(top), ALU.subtract))
                L(v.scalar_tensor_tensor(R(11), R(9), 0.02, R(10), ALU.mult, ALU.add))
                L(v.tensor_scalar(keep, R(11), 0.0, None, ALU.is_ge))
                v.tensor_tensor(d, src, wide(top), ALU.subtract).then_inc(sem(s + "to_exp"), 1)
            for n, (d, keep, hot) in enumerate(((R(5), R(6), R(0)), (R(7), R(8), R(3)))):
                v.wait_ge(sem(s + "exped"), n + 1)
                L(v.tensor_tensor(keep, keep, d, ALU.mult))
                L(v.tensor_reduce(r(3), keep, AX, ALU.add))
                L(v.reciprocal(r(4), r(3)))
                L(v.tensor_tensor(hot, hot, wide(r(4)), ALU.mult))
            v.tensor_tensor(gate[0:GT], R(0), R(3), ALU.add).then_inc(sem(s + "gate"), 1)
            v.wait_ge(sem(s + "gate"), 1)

        def route0_scalar(a):
            exp_on_scalar(a, "L0f_", 1, R(5), R(5))
            exp_on_scalar(a, "L0f_", 2, R(7), R(7))

        def route1_vector(v):
            s = "L1f_"
            get_scores(v, s)
            S = score[0:GT]
            L = lambda ins: vchain.link(v, ins)
            for g in range(G):
                last = v.max(R(0)[:, g, :], S[:, g, :])
            L(last)
            L(v.tensor_tensor(R(1), S, wide(R(0)[:, :, 1]), ALU.is_ge))
            v.tensor_tensor(R(2), S, wide(R(0)[:, :, 0]), ALU.subtract).then_inc(sem(s + "to_exp"), 1)
            v.wait_ge(sem(s + "exped"), 1)
            L(v.tensor_tensor(R(3), R(1), R(2), ALU.mult))
            L(v.tensor_reduce(r(0), R(3), AX, ALU.add))
            L(v.reciprocal(r(1), r(0)))
            v.scalar_tensor_tensor(gate[0:GT], R(3), 1.0 / E, wide(r(1)), ALU.mult, ALU.mult)\
                .then_inc(sem(s + "gate"), 1)
            v.wait_ge(sem(s + "gate"), 1)

        def probs_vector(v, s):
            get_scores(v, s)
            S = score[0:GT]
            L = lambda ins: vchain.link(v, ins)
            L(v.tensor_reduce(r(0), S, AX, ALU.max))
            v.tensor_tensor(R(2), S, wide(r(0)), ALU.subtract).then_inc(sem(s + "to_exp"), 1)
            v.wait_ge(sem(s + "exped"), 1)
            L(v.tensor_reduce(r(1), R(2), AX, ALU.add))
            L(v.reciprocal(r(2), r(1)))
            L(v.tensor_tensor(R(3), R(2), wide(r(2)), ALU.mult))
            L(v.tensor_reduce(r(3), R(3), AX, ALU.max))
            first_of(v, R(3), r(3), R(4), R(5), r(4))

        def route2_vector(v):
            s = "L2f_"
            probs_vector(v, s)
            L = lambda ins: vchain.link(v, ins)
            L(v.scalar_tensor_tensor(R(6), R(4), -2.0, R(3), ALU.mult, ALU.add))
            L(v.tensor_reduce(r(5), R(6), AX, ALU.max))
            first_of(v, R(6), r(5), R(7), R(5), r(4))
            L(v.tensor_tensor(R(8), R(4), wide(R(3)[:, :, 0]), ALU.mult))
            L(v.tensor_tensor(R(9), R(7), wide(R(3)[:, :, 1]), ALU.mult))
            v.tensor_tensor(gate[0:GT], R(8), R(9), ALU.add).then_inc(sem(s + "gate"), 1)
            v.wait_ge(sem(s + "gate"), 1)

        def bias_tensor(pe, s, which):
            pe.wait_ge(sem(s + "gate"), 1)
            for g in range(G):
                pe.transpose(bank[2 + g // 4][0:E, g % 4 * GT:(g % 4 + 1) * GT], gate[0:GT, g, :], ident[0:GT, 0:GT])\
                    .then_inc(sem(s + "gateT"), 1)
            pe.wait_ge(sem(s + "gateT_out"), 2)
            for g in range(G):
                pe.matmul(y_bank(g), gateT[:, g, :], tab[:, which, :], start=True, stop=True)\
                    .then_inc(sem(s + "bias"), 1)

        def bias_scalar(a, s):
            for j, n in enumerate((4, 2)):
                a.wait_ge(sem(s + "gateT"), 4 * j + n)
                a.activation(gateT[:, 4 * j:4 * j + n, :],
                             bank[2 + j][0:E, 0:n * GT].rearrange("p (g n) -> p g n", g=n), ACT.Copy)\
                    .then_inc(sem(s + "gateT_out"), 1)

        def bias_vector(v, s, dst):
            v.wait_ge(sem(s + "bias"), G)
            for g in range(G):
                v.tensor_tensor(dst[0:GT, g, :], y_bank(g), dst[0:GT, g, :], ALU.add).then_inc(sem(s + "y_added"), 1)

        DSP = arena[0:GT, 0:G * TOK].rearrange("p (g n) -> p g n", g=G)
        DST = arena[0:CAP, G * TOK:G * TOK + E * SLOTS].rearrange("p (e n) -> p e n", e=E)
        SL = arena2[:, 0:C * TOK].rearrange("p (c n) -> p c n", c=C)
        YS = arena2[0:CAP, C * TOK:C * TOK + E * D].rearrange("p (e n) -> p e n", e=E)
        diag = arena2[0:GT, C * TOK + E * D:C * TOK + E * D + 2 * GT].rearrange("p (b n) -> p b n", b=2)
        destB = KT[0:CAP, 0, :]
        GELU_IN = 2.0 ** 0.5 / 1.41421

        def switch_vector(v):
            s = "L3f_"
            probs_vector(v, s)
            L = lambda ins: vchain.link(v, ins)
            L(v.reciprocal(r(5), r(3)))
            L(v.tensor_tensor(r(6), r(3), r(5), ALU.mult))
            for g in range(G):
                v.tensor_scalar(X[0:GT, g, :], X[0:GT, g, :], r(6)[:, g:g + 1], None, ALU.mult)\
                    .then_inc(sem(s + "xs"), 1)
            L(v.tensor_tensor(R(5), R(4), over_groups(iotaE), ALU.mult))
            L(v.tensor_reduce(r(0), R(5), AX, ALU.add))
            L(v.tensor_scalar(R(4)[:, G - 1, :], R(4)[:, G - 1, :], same[0:GT, 0:1], None, ALU.mult))
            v.tensor_copy(R(6), R(4)).then_inc(sem(s + "hot"), 1)
            v.wait_ge(sem(s + "cum"), 1)
            L(v.tensor_tensor(R(7), R(4), bank[7][0:GT, 64:64 + G * E].rearrange("p (g e) -> p g e", g=G), ALU.mult))
            L(v.tensor_reduce(r(1), R(7), AX, ALU.add))
            L(v.tensor_scalar(r(2), r(1), float(CAP), None, ALU.is_le))
            L(v.tensor_reduce(r(7), R(4), AX, ALU.add))
            L(v.tensor_tensor(r(0), r(0), r(7), ALU.mult))
            L(v.scalar_tensor_tensor(r(3), r(0), float(CAP), r(1), ALU.mult, ALU.add))
            L(v.tensor_tensor(r(4), r(3), r(2), ALU.mult))
            L(v.tensor_scalar(r(4), r(4), -1.0, None, ALU.add))
            L(v.tensor_scalar(r(5), r(2), -1.0, 1.0, ALU.mult, ALU.add))
            for g in range(G):
                v.tensor_scalar(DSP[:, g, :], slot_id[0:GT, :], r(4)[:, g:g + 1], None, ALU.is_equal)\
                    .then_inc(sem(s + "dispatch"), 1)
            for g in range(G):
                if g >= 2:
                    v.wait_ge(sem(s + "dest"), g - 1)
                v.tensor_scalar(diag[:, g % 2, :], ident[0:GT, 0:GT], r(4)[:, g:g + 1], None, ALU.mult)\
                    .then_inc(sem(s + "diag"), 1)
            for j, n in enumerate((4, 2)):
                v.wait_ge(sem(s + "dest"), 4 * j + n)
                last = v.tensor_copy(destB[:, 4 * j * GT:(4 * j + n) * GT], bank[4 + j][0:CAP, 0:n * GT])
            L(last)
            for e in range(E):
                last = v.tensor_scalar(DST[:, e, :], destB, slot_own[0:CAP, e:e + 1], None, ALU.is_equal)
            last.then_inc(sem(s + "combine"), 1)

        def switch_tensor(pe, wave):
            s = "L3f_"
            pe.wait_ge(sem(s + "hot"), 1)
            for g in range(G):
                for k in range(g + 1):
                    last = pe.matmul(bank[7][0:GT, 64 + g * E:64 + (g + 1) * E], (tri if k == g else ones)[0:GT, 0:GT],
                                     R(6)[:, k, :], start=(k == 0), stop=(k == g))
            last.then_inc(sem(s + "cum"), 1)
            pe.wait_ge(sem(s + "dispatch"), G)
            pe.wait_ge(sem(s + "xs"), G)
            for c in range(C):
                for half in range(2):
                    for g in range(G):
                        last = pe.matmul(bank[2 * c + half][:, 0:HT], X[0:GT, g, c * P:(c + 1) * P],
                                         DSP[:, g, half_of(half)], start=(g == 0), stop=(g == G - 1))
                    last.then_inc(sem(s + "slots"), 1)
            for g in range(G):
                pe.wait_ge(sem(s + "diag"), g + 1)
                pe.matmul(bank[4 + g // 4][0:CAP, g % 4 * GT:(g % 4 + 1) * GT], ones[0:GT, 0:CAP], diag[:, g % 2, :],
                          start=True, stop=True).then_inc(sem(s + "dest"), 1)
            pe.wait_ge(sem(s + "slots_out"), 4)
            with pe.Fori(0, E // 2) as i:
                for b in range(2):
                    w1, w2, _ = relu_w(b, F1)
                    pe.wait_ge(in_exp[b], 16 * (i + wave + 2 - b))
                    pe.wait_ge(sem(s + "gelu"), 2 * i + b + 1)
                    for f in range(F1):
                        for c in range(C):
                            last = pe.matmul(bank[2 * b + f // 4][:, f % 4 * CAP:(f % 4 + 1) * CAP],
                                             w1[:, c, f * P:(f + 1) * P], SL[:, c, bass.ds((2 * i + b) * CAP, CAP)],
                                             start=(c == 0), stop=(c == C - 1))
                        if f % 4 == 3:
                            last.then_inc(sem(s + "hid"), 1)
                for b in range(2):
                    w1, w2, _ = relu_w(b, F1)
                    pe.wait_ge(sem(s + "gelu"), 2 * i + b + 3)
                    pe.wait_ge(sem(s + "ys_free"), 2 * i + b + 1)
                    for f in range(F1):
                        last = pe.matmul(bank[6 + b][0:CAP, 0:D], hT[:, b, f * CAP:(f + 1) * CAP], w2[:, f, :],
                                         start=(f == 0), stop=(f == F1 - 1))
                    last.then_inc(sem(s + "ys"), 1)
            pe.wait_ge(sem(s + "ys_free"), E + 2)
            pe.wait_ge(sem(s + "combine"), 1)
            for g in range(G):
                if g >= 2:
                    pe.wait_ge(sem(s + "final"), g - 1)
                for e in range(E):
                    last = pe.matmul(bank[4 + g % 2][0:GT, 0:D], DST[:, e, tok(g)], YS[:, e, :], start=(e == 0),
                                     stop=(e == E - 1))
                last.then_inc(sem(s + "gathered"), 1)

        def switch_scalar(a):
            s = "L3f_"
            exp_on_scalar(a, s, 1, R(2), R(2))
            for c in range(C):
                for half in range(2):
                    a.wait_ge(sem(s + "slots"), 2 * c + half + 1)
                    a.activation(SL[:, c, half_of(half)], bank[2 * c + half][:, 0:HT], ACT.Copy)\
                        .then_inc(sem(s + "slots_out"), 1)
            with a.Fori(0, E // 2) as i:
                for b in range(2):
                    a.wait_ge(sem(s + "b1s"), 2 * i + b + 1)
                    for f in range(F1):
                        if f % 4 == 0:
                            a.wait_ge(sem(s + "hid"), 4 * i + 2 * b + f // 4 + 1)
                        last = a.activation(hT[:, b, f * CAP:(f + 1) * CAP],
                                            bank[2 * b + f // 4][:, f % 4 * CAP:(f % 4 + 1) * CAP], ACT.Gelu,
                                            bias=b1s[:, b, f:f + 1], scale=GELU_IN)
                    last.then_inc(sem(s + "gelu"), 1)

        def switch_loop_vector(v, wave):
            s = "L3f_"
            v.wait_ge(in_attn[0], 16 * 3)
            with v.Fori(0, E // 2) as i:
                for b in range(2):
                    v.wait_ge(in_exp[b], 16 * (i + wave + 2 - b))
                    v.tensor_scalar(b1s[:, b, :], relu_w(b, F1)[2], GELU_IN, None, ALU.mult)\
                        .then_inc(sem(s + "b1s"), 1)
                for b in range(2):
                    v.wait_ge(sem(s + "ys"), 2 * i + b + 1)
                    v.scalar_tensor_tensor(YS[:, bass.ds(2 * i + b, 1), :].rearrange("p e n -> p (e n)"),
                                           bank[6 + b][0:CAP, 0:D], 1.0 / GELU_IN,
                                           b2all[0:CAP, bass.ds(2 * i + b, 1), :].rearrange("p e n -> p (e n)"),
                                           ALU.mult, ALU.add).then_inc(sem(s + "ys_free"), 1)
            for g in range(G):
                v.scalar_tensor_tensor(H[0:GT, g, :], X[0:GT, g, :], r(5)[:, g:g + 1], H[0:GT, g, :],
                                       ALU.mult, ALU.add).then_inc(sem(s + "kept"), 1)
            v.wait_ge(sem(s + "kept"), G)
            for g in range(G):
                v.wait_ge(sem(s + "gathered"), g + 1)
                v.tensor_tensor(H[0:GT, g, :], bank[4 + g % 2][0:GT, 0:D], H[0:GT, g, :], ALU.add)\
                    .then_inc(sem(s + "final"), 1)

        patches = arena[:, 0:PC * SLOTS].rearrange("p (c n) -> p c n", c=PC)
        w_patch = arena[:, PC * SLOTS:PC * SLOTS + PC * D].rearrange("p (c n) -> p c n", c=PC)

        def embed_tensor(pe):
            pe.wait_ge(in_patch, 32)
            for g in range(G):
                if g >= 2:
                    pe.wait_ge(sem("embedded"), g - 1)
                for k in range(PC):
                    last = pe.matmul(bank[g % 2][0:GT, 0:D], patches[:, k, tok(g)], w_patch[:, k, :],
                                     start=(k == 0), stop=(k == PC - 1))
                last.then_inc(sem("embed"), 1)

        def embed_vector(v):
            v.wait_ge(in_small, 16 * n_small)
            vchain.link(v, v.tensor_tensor(posA[0:GT, 0, :], posA[0:GT, 0, :], posA[0:GT, 1, :], ALU.add))
            for g in range(G):
                v.wait_ge(sem("embed"), g + 1)
                v.tensor_tensor(H[0:GT, g, :], bank[g % 2][0:GT, 0:D], posA[0:GT, 0, :], ALU.add)\
                    .then_inc(sem("embedded"), 1)
            v.wait_ge(sem("embedded"), G)

        n_small = 6
        block = ctx.enter_context(nc.Block())

        @block.sync
        def _(sp):
            sp.dma_start(patches, t["patches"]).then_inc(in_patch, 16)
            sp.dma_start(w_patch, t["w_patch"]).then_inc(in_patch, 16)
            sp.dma_start(rows[:, :], t["rows"]).then_inc(in_small, 16)
            sp.dma_start(cols[:, :], t["cols"]).then_inc(in_small, 16)
            sp.dma_start(gates[:, :, :, :], t["gates"]).then_inc(in_small, 16)
            sp.dma_start(tab[:, :, :], t["tab"]).then_inc(in_small, 16)
            sp.dma_start(lam_in[0:GT], t["lam"]).then_inc(in_small, 16)
            sp.dma_start(posA[0:GT], t["pos"]).then_inc(in_small, 16)
            sp.wait_ge(sem("proj_clear"), 1)
            for h in range(8):
                sp.dma_start(proj8[16 * h:16 * h + 16, h // 4, h % 4, :], t["proj"]).then_inc(in_proj, 16)
            sp.dma_start(wA[0][:, :], t["attn0"]).then_inc(in_attn[0], 16)
            sp.dma_start(wA[1][:, :], t["attn1"]).then_inc(in_attn[1], 16)
            sp.dma_start(wE[0][:, 0:EXP1], t["mlp0"]).then_inc(in_exp[0], 16)
            sp.dma_start(wE[1][:, 0:EXP0], t["ffn0"][1]).then_inc(in_exp[1], 16)

            def stream(dram, size, used, per_expert, rounds=E // 2):
                with sp.Fori(1, rounds) as i:
                    for b in range(2):
                        sp.wait_ge(sem(used), (2 * i + b - 1) * per_expert)
                        sp.dma_start(wE[b][:, 0:size], dram[bass.ds(2 * i + b, 1)].rearrange("e p n -> (e p) n"))\
                            .then_inc(in_exp[b], 16)

            sp.wait_ge(sem("L0m_y"), F1)
            sp.dma_start(wE[0][:, 0:EXP0], t["ffn0"][0]).then_inc(in_exp[0], 16)
            sp.dma_start(wA[0][:, :], t["attn2"]).then_inc(in_attn[0], 16)
            stream(t["ffn0"], EXP0, "L0f_y", F0)
            for b in range(2):
                sp.wait_ge(sem("L0f_y"), (E - 1 + b) * F0)
                sp.dma_start(wE[b][:, 0:EXP1], t["ffn1"][b]).then_inc(in_exp[b], 16)
            sp.wait_ge(sem("L1_added"), G)
            sp.dma_start(wA[1][:, :], t["attn3"]).then_inc(in_attn[1], 16)
            stream(t["ffn1"], EXP1, "L1f_y", F1)
            for b in range(2):
                sp.wait_ge(sem("L1f_y"), (E - 1 + b) * F1)
                sp.dma_start(wE[b][:, 0:EXP2], t["ffn2"][b]).then_inc(in_exp[b], 16)
            stream(t["ffn2"], EXP2, "L2f_y", 2)
            sp.dma_start(b2all[0:CAP], t["b2"]).then_inc(in_attn[0], 16)
            for b in range(2):
                sp.wait_ge(sem("L2f_y"), (E - 1 + b) * 2)
                sp.dma_start(wE[b][:, 0:EXP1], t["ffn3"][b]).then_inc(in_exp[b], 16)
            written = 0
            for g in range(G):
                sp.wait_ge(sem("L3_o"), g + 1)
                for i in range(g * PER, min((g + 1) * PER, IMAGES)):
                    q = (i - g * PER) * SEQ
                    sp.dma_start(by_head[i].rearrange("h q d -> q h d"),
                                 O[q:q + SEQ, g, :].rearrange("p (h d) -> p h d", h=16))\
                        .then_inc(sem("L3_heads_out"), 16)
                    written += 16
                sp.wait_ge(sem("L3_heads_out"), written)
                if g:
                    sp.wait_ge(sem("L3_regrouped"), 16 * g)
                n = y_rows(g)
                sp.dma_start(X[0:n, g, :], by_token[g * GT:g * GT + n, :]).then_inc(sem("L3_regrouped"), 16)
            stream(t["ffn3"], EXP1, "L3f_ys", 1)
            sp.wait_ge(sem("finished"), 1)
            full = TOK // GT
            sp.dma_start(t["out"][0:full * GT, :].rearrange("(g p) d -> p g d", p=GT), H[0:GT, 0:full, :])\
                .then_inc(stored, 16)
            sp.dma_start(t["out"][full * GT:TOK, :], H[0:TOK - full * GT, full, :]).then_inc(stored, 16)
            sp.wait_ge(stored, 32)

        @block.gpsimd
        def _(p):
            def L(ins):
                pchain.link(p, ins)

            def keep(x, pattern, base, mult, fill, op=ALU.is_ge):
                L(p.affine_select(out=x, in_=x, pattern=pattern, compare_op=op, fill=fill, base=base,
                                  channel_multiplier=mult))

            def same_block(x, n, size, value_in, fill):
                inner = x.shape[1] // n
                xv = x if inner == 1 else x.rearrange("p (b n) -> p b n", b=n)
                pat = [[-size, n]] if inner == 1 else [[-size, n], [0, inner]]
                keep(xv, pat, 0, 1, fill)
                pat = [[size, n]] if inner == 1 else [[size, n], [0, inner]]
                keep(xv, pat, size - 1, -1, fill)

            p.memset(hT[:, 2:4, 0:4 * P], 0.0).then_inc(sem("proj_clear"), 1)
            L(p.memset(ident[:, :], 0.0))
            keep(ident[:, :], [[-1, P]], 0, 1, 1.0, ALU.not_equal)
            L(p.memset(ones[:, :], 1.0))
            L(p.memset(tri[:, :], 1.0))
            keep(tri[:, :], [[1, P]], 0, -1, 0.0)
            L(p.memset(same[:, :], 1.0))
            same_block(same[:, :], PER, SEQ, 1.0, 0.0)
            L(p.memset(far[:, :], 0.0))
            same_block(far[:, :], PER, SEQ, 0.0, NEG)
            L(p.memset(causal[:, :], 0.0))
            same_block(causal[:, :], PER, SEQ, 0.0, NEG)
            keep(causal[:, :], [[-1, GT]], 0, 1, NEG)
            L(p.memset(head16[:, :], 1.0))
            same_block(head16[:, :], 8, 16, 1.0, 0.0)
            L(p.memset(head32[:, :], 1.0))
            same_block(head32[:, :], 4, 32, 1.0, 0.0)
            L(p.memset(block8[:, :], 1.0))
            same_block(block8[:, :], 16, 8, 1.0, 0.0)
            L(p.iota(i32[:, 0:E], [[1, E]], base=0, channel_multiplier=0))
            L(p.tensor_copy(iotaE[:, :], i32[:, 0:E]))
            L(p.iota(i32[:, 0:E], [[-1, E]], base=E, channel_multiplier=0))
            L(p.tensor_copy(revE[:, :], i32[:, 0:E]))
            L(p.iota(i32[:, 0:E], [[CAP, E]], base=0, channel_multiplier=1))
            L(p.tensor_copy(slot_own[:, :], i32[:, 0:E]))
            L(p.iota(i32[:, :], [[1, TOK]], base=0, channel_multiplier=0))
            L(p.tensor_copy(slot_id[:, :], i32[:, :]))
            L(p.memset(eps[:, 0:1], EPS))
            L(p.memset(eps[:, 1:2], 1.5707963))
            p.memset(XT[:, :, TOK:SLOTS], 0.0).then_inc(consts, 1)
        @block.tensor
        def _(pe):
            pe.wait_ge(consts, 1)
            embed_tensor(pe)
            s = "L0_"
            turn_tensor(pe, s, X, normed_of(s))
            qk_tensor(pe, s, 0, (0, 1))
            v_tensor(pe, s, 0, row("L0_bv"))
            fourier_tensor(pe, 0)
            for g in range(G):
                if g + 1 < G:
                    fourier_tensor(pe, g + 1)
                similar_tensor(pe, g)
            turn_tensor(pe, "L0o_", O, lambda g: (sem("L0_o"), g + 1))
            proj_tensor(pe, "L0a_", 0, lambda g: (xt_done, xt_count("L0o_", g + 1)), row("L0_bo"))
            s = "L0m_"
            turn_tensor(pe, s, X, normed_of(s))
            pe.wait_ge(xt_done, xt_count(s, G))
            for g in range(G):
                pe.matmul(y_bank(g), ones[0:1, 0:GT], row("L0_b2"), start=True, stop=True)\
                    .then_inc(sem(s + "bias"), 1)
            ffn_tensor(pe, s, "relu", F1, -1, [0], 1)
            s = "L0f_"
            turn_tensor(pe, s, X, normed_of(s))
            gate_tensor(pe, s, 0, None)
            ffn_tensor(pe, s, "silu", F0, 0, [0, 1], E // 2)
            s = "L1_"
            turn_tensor(pe, s, X, normed_of(s))
            qk_tensor(pe, s, 1, (0, 1))
            v_tensor(pe, s, 1, row("L1_bv"))
            score_tensor(pe, s, 0, 8)
            for g in range(G):
                if g + 1 < G:
                    score_tensor(pe, s, g + 1, 8)
                pv_tensor(pe, s, g, 8, 32, 4)
            turn_tensor(pe, "L1o_", X, normed_of("L1o_"))
            proj_tensor(pe, s, 1, lambda g: (xt_done, xt_count("L1o_", g + 1)), row("L1_bo"))
            s = "L1f_"
            turn_tensor(pe, s, X, normed_of(s))
            gate_tensor(pe, s, 1, None)
            bias_tensor(pe, s, 0)
            ffn_tensor(pe, s, "relu", F1, 4, [0, 1], E // 2)
            s = "L2_"
            turn_tensor(pe, s, X, normed_of(s))
            qk_tensor(pe, s, 2, (0,))
            linear_tensor(pe)
            proj_tensor(pe, s, 2, lambda g: (sem("L2_image"), IMAGES), row("L2_bo"))
            s = "L2f_"
            turn_tensor(pe, s, X, normed_of(s))
            gate_tensor(pe, s, 2, rows[0:1, 7 * D:7 * D + E])
            bias_tensor(pe, s, 1)
            deep_tensor(pe, s, 8)
            s = "L3_"
            turn_tensor(pe, s, X, normed_of(s))
            qk_tensor(pe, s, 3, (0, 1))
            v_tensor(pe, s, 3, None)
            score_tensor(pe, s, 0, 16)
            for g in range(G):
                if g + 1 < G:
                    score_tensor(pe, s, g + 1, 16)
                pv_tensor(pe, s, g, 16, 16, 16)
            turn_tensor(pe, "L3o_", X, lambda g: (sem("L3_regrouped"), 16 * (g + 1)))
            proj_tensor(pe, s, 3, lambda g: (xt_done, xt_count("L3o_", g + 1)), row("L3_bo"))
            s = "L3f_"
            turn_tensor(pe, s, X, normed_of(s))
            gate_tensor(pe, s, 3, rows[0:1, 7 * D + E:7 * D + 2 * E])
            switch_tensor(pe, 12)

        @block.vector
        def _(v):
            v.wait_ge(consts, 1)
            embed_vector(v)
            v.wait_ge(in_proj, 16 * 8)
            v.tensor_scalar(hT[:, 2:4, 0:4 * P], hT[:, 2:4, 0:4 * P], 0.25 / (2 * 3.141592653589793), None, ALU.mult)\
                .then_inc(sem("proj_scaled"), 1)
            norm_vector(v, "L0i_", H, R0)
            v.wait_ge(normed, G)
            s = "L0_"
            norm_vector(v, s, R0, X)
            v_vector(v, s, 16, 16)
            phase_vector(v, 0)
            for g in range(G):
                if g + 1 < G:
                    phase_vector(v, g + 1)
                similar_vector(v, g)
            proj_vector(v, "L0a_", R0, R0)
            s = "L0m_"
            norm_vector(v, s, R0, X)
            bias_vector(v, s, R0)
            free_banks(v, s, 0, 2)
            free_banks(v, s, 1, 2)
            ffn_vector(v, s, "relu", F1, [0], 1)
            v.wait_ge(sem(s + "y_added"), 2 * G)
            for g in range(G):
                last = v.tensor_tensor(H[0:GT, g, :], H[0:GT, g, :], R0[0:GT, g, :], ALU.add)
            vchain.link(v, last)
            s = "L0f_"
            norm_vector(v, s, H, X)
            free_banks(v, s, 0, 1)
            free_banks(v, s, 1, 1)
            v.sem_inc(sem(s + "y_added"), G)
            route0_vector(v)
            ffn_vector(v, s, "silu", F0, [0, 1], E // 2)
            v.wait_ge(sem(s + "y_added"), (E + 1) * G)
            s = "L1_"
            for j in range(2):
                last = v.tensor_tensor_reduce(lam_in[0:GT, 2 * j, :], lam_in[0:GT, 2 * j, :],
                                              lam_in[0:GT, 2 * j + 1, :], 1.0, 0.0, ALU.mult, ALU.add,
                                              lam[0:GT, j:j + 1])
            last.then_inc(sem(s + "lam"), 1)
            v.wait_ge(sem(s + "lam_exp"), 1)
            vchain.link(v, v.tensor_tensor(lam[0:GT, 4:5], lam[0:GT, 3:4], lam[0:GT, 2:3], ALU.subtract))
            vchain.link(v, v.tensor_scalar(lam[0:GT, 5:6], lam[0:GT, 4:5], -0.8, None, ALU.add))
            norm_vector(v, s, H, X)
            v_ones(v, s, 4, 32)
            for g in range(G):
                v.wait_ge(sem(s + "v"), g + 1)
                b = bank[6 + g % 2]
                vchain.link(v, v.tensor_scalar(O[0:GT, g, 0:P], b[0:GT, P:D], lam[0:GT, 5:6], None, ALU.mult))
                v.tensor_tensor(V[0:GT, g, 0:4 * 33].rearrange("p (h d) -> p h d", h=4)[:, :, 0:32],
                                b[0:GT, 0:P].rearrange("p (h d) -> p h d", h=4),
                                O[0:GT, g, 0:P].rearrange("p (h d) -> p h d", h=4), ALU.add)\
                    .then_inc(sem(s + "v_out"), 1)
            keys_vector(v, s, 8)
            score_vector(v, s, 0, 8, far)
            for g in range(G):
                if g + 1 < G:
                    score_vector(v, s, g + 1, 8, far)
                out_vector(v, s, g, 8, 32)
            v.wait_ge(sem(s + "o"), G)
            norm_vector(v, "L1o_", O, X)
            proj_vector(v, s, H, H)
            s = "L1f_"
            norm_vector(v, s, H, X)
            free_banks(v, s, 0, 2)
            free_banks(v, s, 1, 2)
            route1_vector(v)
            bias_vector(v, s, H)
            ffn_vector(v, s, "relu", F1, [0, 1], E // 2)
            v.wait_ge(sem(s + "y_added"), (E + 1) * G)
            s = "L2_"
            norm_vector(v, s, H, X)
            linear_vector(v)
            proj_vector(v, s, H, H)
            s = "L2f_"
            norm_vector(v, s, H, X)
            free_banks(v, s, 0, 2)
            free_banks(v, s, 1, 2)
            route2_vector(v)
            bias_vector(v, s, H)
            deep_vector(v, s)
            v.wait_ge(sem(s + "y_added"), (E + 1) * G)
            s = "L3_"
            norm_vector(v, s, H, X)
            v_ones(v, s, 16, 16)
            v_vector(v, s, 16, 16)
            keys_vector(v, s, 16)
            score_vector(v, s, 0, 16, causal)
            for g in range(G):
                if g + 1 < G:
                    score_vector(v, s, g + 1, 16, causal)
                out_vector(v, s, g, 16, 16)
            proj_vector(v, s, H, H)
            s = "L3f_"
            norm_vector(v, s, H, X)
            v.sem_inc(sem(s + "gelu"), 2)
            v.sem_inc(sem(s + "ys_free"), 2)
            switch_vector(v)
            switch_loop_vector(v, 12)
            v.wait_ge(sem(s + "final"), G)
            v.memset(r_mx[0:1, 0, 0:1], 0.0).then_inc(sem("finished"), 1)

        @block.scalar
        def _(a):
            a.wait_ge(consts, 1)
            a.wait_ge(in_small, 16 * n_small)
            norm_scalar(a, "L0i_")
            s = "L0_"
            norm_scalar(a, s)
            turn_scalar(a, s, lambda c: col("L0_g1", c), lambda c: col("L0_n1", c))
            qk_scalar(a, s, (0, 1), ACT.Identity, lambda w, c: col(("L0_bq", "L0_bk")[w], c))
            for g in range(G):
                fourier_scalar(a, g)
            turn_scalar(a, "L0o_")
            s = "L0m_"
            norm_scalar(a, s)
            turn_scalar(a, s, lambda c: col("L0_g2", c), lambda c: col("L0_n2", c))
            ffn_scalar(a, s, "relu", F1, [0], 1)
            s = "L0f_"
            norm_scalar(a, s)
            turn_scalar(a, s)
            route0_scalar(a)
            ffn_scalar(a, s, "silu", F0, [0, 1], E // 2)
            s = "L1_"
            a.wait_ge(sem(s + "lam"), 1)
            a.activation(lam[0:GT, 2:4], lam[0:GT, 0:2], ACT.Exp).then_inc(sem(s + "lam_exp"), 1)
            norm_scalar(a, s)
            turn_scalar(a, s)
            qk_scalar(a, s, (0, 1), ACT.Identity, lambda w, c: col(("L1_bq", "L1_bk")[w], c))
            for g in range(G):
                soft_scalar(a, s, g, 8, 1.0 / 32 ** 0.5)
            norm_scalar(a, "L1o_")
            last = a.activation(aff[:, :], cols[:, 2 * COL.index("L1_g"):2 * COL.index("L1_g") + 4], ACT.Copy,
                                scale=0.2)
            last.then_inc(sem("aff"), 1)
            a.wait_ge(sem("aff"), 1)
            turn_scalar(a, "L1o_", lambda c: aff[:, c:c + 1], lambda c: aff[:, 2 + c:3 + c])
            s = "L1f_"
            norm_scalar(a, s)
            turn_scalar(a, s)
            exp_on_scalar(a, s, 1, R(2), R(2))
            bias_scalar(a, s)
            ffn_scalar(a, s, "relu", F1, [0, 1], E // 2)
            s = "L2_"
            norm_scalar(a, s)
            turn_scalar(a, s)
            qk_scalar(a, s, (0,), ACT.Relu, lambda w, c: None)
            linear_scalar(a)
            s = "L2f_"
            norm_scalar(a, s)
            turn_scalar(a, s)
            exp_on_scalar(a, s, 1, R(2), R(2))
            bias_scalar(a, s)
            deep_scalar(a, s)
            s = "L3_"
            norm_scalar(a, s)
            turn_scalar(a, s)
            qk_scalar(a, s, (0, 1), ACT.Identity, lambda w, c: None)
            for g in range(G):
                soft_scalar(a, s, g, 16, 0.25)
            turn_scalar(a, "L3o_")
            s = "L3f_"
            norm_scalar(a, s)
            turn_scalar(a, s)
            switch_scalar(a)


def _layout(x):
    import numpy as np

    def chunked(w):
        k, n = w.shape
        return w.reshape(k // P, P, n).transpose(1, 0, 2).reshape(P, -1)

    def slots(a):
        out = np.zeros(a.shape[:-1] + (SLOTS,), a.dtype)
        out[..., :TOK] = a
        return out

    side = 6
    pt = x["x"].reshape(IMAGES, 3, side, 16, side, 16).transpose(1, 3, 5, 0, 2, 4).reshape(PD, IMAGES, PATCHES)
    full = np.zeros((PD, IMAGES, SEQ), pt.dtype)
    full[:, :, 2:] = pt
    t = {"patches": slots(full.reshape(PC, P, TOK)).transpose(1, 0, 2),
         "w_patch": x["L0_tok_W"].T.reshape(PC, P, D).transpose(1, 0, 2)}
    z = np.zeros(D, pt.dtype)
    pos = np.zeros((2, SEQ, D), pt.dtype)
    pos[0, 0] = x["cls_tok"][0, 0]
    pos[0, 1:] = x["L0_tok_pos_embed"][0]
    pos[1, 1] = x["L0_tok_cls_token"][0, 0]
    pos[1, 2:] = x["L0_tok_b"]
    t["pos"] = np.tile(pos.transpose(1, 0, 2), (PER, 1, 1))
    gb = np.zeros(D, pt.dtype)
    gb[:E], gb[E:2 * E] = x["L2_ffn_gate_b"], x["L3_ffn_b_sw"]
    t["rows"] = np.concatenate([x["L0_attn_bv"], x["L0_attn_bo"], x["L0_attn_b2"], x["L1_attn_bv"], x["L1_attn_bo"],
                                x["L2_attn_proj_bias"], x["L3_attn_bo"], gb])[None]
    names = ["L0_attn_bq", "L0_attn_bk", "L0_attn_ln1_g", "L0_attn_ln1_b", "L0_attn_ln2_g", "L0_attn_ln2_b",
             "L1_attn_bq", "L1_attn_bk", "L1_attn_ln_w", "L1_attn_ln_b"]
    t["cols"] = np.concatenate([x[n].reshape(C, P).T for n in names], 1)
    t["gates"] = np.stack([w.reshape(C, P, E).transpose(1, 0, 2) for w in (
        x["L0_ffn_gate_w"].T, x["L1_ffn_W_gate"], x["L2_ffn_gate_w"].T, x["L3_ffn_W_sw"])], 1)
    t["tab"] = np.stack([x["L1_ffn_b2"], x["L2_ffn_b3"]], 1)
    t["lam"] = np.tile(np.stack([x["L1_attn_lambda_" + n] for n in ("q1", "k1", "q2", "k2")])[None], (GT, 1, 1))
    t["b2"] = np.tile(x["L3_ffn_b2"][None], (CAP, 1, 1))
    t["proj"] = x["L0_attn_proj_mat"]
    t["attn0"] = np.concatenate([chunked(x["L0_attn_w" + n]) for n in "qkvo"], 1)
    t["attn1"] = np.concatenate([chunked(x["L1_attn_W" + n]) for n in "qkvo"], 1)
    qkv = x["L2_attn_qkv_weight"].T
    t["attn2"] = np.concatenate([chunked(qkv[:, :D]), chunked(qkv[:, D:]), chunked(x["L2_attn_proj_weight"].T)], 1)
    t["attn3"] = np.concatenate([chunked(x["L3_attn_W" + n]) for n in "qkvo"], 1)

    def expert(*parts):
        return np.concatenate(parts, 1)

    def bias(b):
        return b.reshape(-1, P).T

    t["mlp0"] = expert(chunked(x["L0_attn_w1"]), chunked(x["L0_attn_w2"]), bias(x["L0_attn_b1"]))
    t["ffn0"] = np.stack([expert(chunked(x["L0_ffn_w1"][e].T), chunked(x["L0_ffn_w3"][e].T),
                                 chunked(x["L0_ffn_w2"][e].T)) for e in range(E)])
    for layer in (1, 3):
        n = f"L{layer}_ffn_"
        t[f"ffn{layer}"] = np.stack([expert(chunked(x[n + "W1"][e]), chunked(x[n + "W2"][e]), bias(x[n + "b1"][e]))
                                     for e in range(E)])
    n = "L2_ffn_"
    t["ffn2"] = np.stack([expert(chunked(x[n + "w1"][e]), chunked(x[n + "w2"][e]), chunked(x[n + "w3"][e]),
                                 bias(x[n + "b1"][e]), bias(x[n + "b2"][e])) for e in range(E)])
    return {k: np.ascontiguousarray(v) for k, v in t.items()}


def kernel(**inputs):
    import numpy as np
    import concourse.bacc as bacc
    from concourse.bass_utils import run_bass_kernel_spmd

    nc = bacc.Bacc("TRN2", target_bir_lowering=False, num_devices=1)
    arrays = _layout({k: np.asarray(v) for k, v in inputs.items()})
    t = {k: nc.dram_tensor(k + "_dram", v.shape, mybir.dt.from_np(v.dtype), kind="ExternalInput").ap()
         for k, v in arrays.items()}
    t["out"] = nc.dram_tensor("out_dram", (TOK, D), F32, kind="ExternalOutput").ap()
    build(nc, t)
    r = run_bass_kernel_spmd(nc, [{k + "_dram": v for k, v in arrays.items()}], core_ids=[0])
    return r.results[0]["out_dram"].reshape(IMAGES, SEQ, D)
```

```python
from contextlib import ExitStack

import concourse.bass as bass
from concourse import mybir

F32 = mybir.dt.float32
F32R = mybir.dt.float32r
ALU = mybir.AluOpType
ACT = mybir.ActivationFunctionType
AX = mybir.AxisListType.X

P = 128
IMAGES, PATCHES, D = 16, 36, 256
SEQ = PATCHES + 2
TOK = IMAGES * SEQ
PER = 3
GT = PER * SEQ
G = -(-IMAGES // PER)
NT = -(-TOK // P)
SLOTS = G * GT
C = D // P
HT = TOK // 2
HS = SLOTS // 2
PD = 768
PC = PD // P
E = 8
CAP = TOK // E
EPS = 1e-5
NEG = -1e30
MAGIC = 12582912.0
TWO_PI = 6.2831850
F0, F1 = 7, 8
ROW = ["L0_bv", "L0_bo", "L0_b2", "L1_bv", "L1_bo", "L2_bo", "L3_bo", "gate_b"]
COL = ["L0_bq", "L0_bk", "L0_g1", "L0_n1", "L0_g2", "L0_n2", "L1_bq", "L1_bk", "L1_g", "L1_n"]
ATTN = ["L0", "L1", "L2", "L3"]


def build(nc, t):
    ctx = ExitStack()
    with ctx:
        def sb(name, shape, dt=F32):
            return ctx.enter_context(nc.sbuf_tensor(name, shape, dt))

        sems = {}

        def sem(name):
            if name not in sems:
                sems[name] = ctx.enter_context(nc.semaphore(name))
            return sems[name]

        bank = [ctx.enter_context(nc.psum_tensor(f"bank{i}", [P, 512], F32)) for i in range(8)]

        H = sb("H", [P, NT, D])
        RO = sb("RO", [P, 2, G, D])
        R0 = RO[:, 0]
        X = sb("X", [P, G, D])
        O = RO[:, 1]
        feat = sb("feat", [P, 3, C, SLOTS])
        XT = feat[:, 0]
        QT = feat[:, 1]
        KT = feat[:, 2]
        parts = sb("parts", [P, 8 * TOK + 6 * 4 * P], F32R)

        def part(at, n, form, **sizes):
            return parts[:, at:at + n].rearrange(form, **sizes)

        XH, XL = [part(i * 2 * TOK, 2 * TOK, "p (c n) -> p c n", c=C) for i in (0, 1)]
        HH, HL = [part(i * 2 * TOK, 2 * TOK, "p (k n) -> p k n", k=2) for i in (2, 3)]
        UH, UL = [part(8 * TOK + i * 8 * P, 8 * P, "p (k c n) -> p k c n", k=2, c=4) for i in (0, 1)]
        DH, DL = [part(8 * TOK + (4 + i) * 4 * P, 4 * P, "p (k n) -> p k n", k=2) for i in (0, 1)]
        YL = sb("YL", [P, E, D], F32R)
        V = sb("V", [P, G, 16 * 17])
        stats = sb("stats", [P, G, 6])
        mv = sb("mv", [P, G, 2])
        sd = sb("sd", [P, G])
        warm = sb("warm", [P, 11])
        rs = sb("rs", [P, G])
        wA = [sb(f"wA{i}", [P, 4 * C * D]) for i in range(2)]
        EXP0 = C * F0 * P * 2 + F0 * D
        EXP1 = C * F1 * P + F1 * D + F1
        EXP2 = 3 * C * D + 4
        arena = sb("arena", [P, 2 * 8 * SLOTS])
        wE = [arena[:, i * EXP0:(i + 1) * EXP0] for i in range(2)]
        arena2 = sb("arena2", [P, 3 * 16 * GT])
        hT = sb("hT", [P, 4, TOK])
        ident = sb("ident", [P, P])
        ones = sb("ones", [P, P])
        valid = sb("valid", [P, 1])
        tri = sb("tri", [P, P])
        same = sb("same", [P, GT])
        far = sb("far", [P, GT])
        causal = sb("causal", [P, GT])
        parity = sb("parity", [P, 2])
        head16 = sb("head16", [P, 8])
        block8 = sb("block8", [P, P])
        iotaE = sb("iotaE", [P, E])
        revE = sb("revE", [P, E])
        slot_id = sb("slot_id", [P, TOK])
        slot_own = sb("slot_own", [P, E])
        i32 = hT[:, 0, :].bitcast(mybir.dt.int32)
        rows = sb("rows", [1, len(ROW) * D])
        cols = sb("cols", [P, len(COL) * C])
        gates = sb("gates", [P, 4, C, E])
        tab = sb("tab", [E, 2, D])
        lam_in = sb("lam_in", [P, 4, 32])
        lam = sb("lam", [P, 8])
        proj8 = hT[:, 2:4, 0:4 * P].rearrange("p a (h n) -> p a h n", h=4)
        posA = arena[0:2 * SEQ, PC * (TOK + D):PC * (TOK + D) + D]
        place = arena[0:2 * SEQ, PC * (TOK + D) + D:PC * (TOK + D) + D + TOK]
        score = sb("score", [P, NT, E])
        rt = sb("rt", [P, 12, NT, E])
        r1 = sb("r1", [P, 8, NT])
        gate = sb("gate", [P, NT, E])
        gateT = QT[0:E, 0, 0:NT * P].rearrange("p (g n) -> p g n", g=NT)
        gcur = sb("gcur", [P, 2, NT])
        b1s = sb("b1s", [P, 2, F1])
        b2all = wA[0][:, :].rearrange("p (e n) -> p e n", e=E)
        r_mx = sb("r_mx", [P, 4, 16])
        eps = sb("eps", [P, 2])
        aff = sb("aff", [P, 4])
        ksum = arena2[:, 2 * C * D:2 * C * D + 4 * SEQ].rearrange("p (a n) -> p a n", a=2)

        def row(name):
            i = ROW.index(name)
            return rows[0:1, i * D:(i + 1) * D]

        def col(name, c):
            i = COL.index(name)
            return cols[:, i * C + c:i * C + c + 1]

        def a_w(layer, which):
            v = wA[layer % 2][:, which * C * D:(which + 1) * C * D]
            return v.rearrange("p (c n) -> p c n", c=C)

        def tok(g):
            return slice(g * GT, (g + 1) * GT)

        def rows_of(g):
            return min(P, TOK - g * P)

        def tile(g):
            return slice(g * P, g * P + rows_of(g))

        def groups_for(g):
            return -(-(g * P + rows_of(g)) // GT)

        GROUPED = ["L1o_", "L0o_"]

        class Chain:

            def __init__(self, name):
                self.s, self.n = sem(name), 0

            def link(self, eng, ins):
                self.n += 1
                ins.then_inc(self.s, 1)
                eng.wait_ge(self.s, self.n)

        vchain = Chain("vector_order")
        pchain = Chain("pool_order")
        heads_dram = nc.dram_tensor("heads_by_image", (IMAGES * 16 * SEQ * 16,), F32, kind="Internal").ap()
        by_head = heads_dram.rearrange("(i h q d) -> i h q d", i=IMAGES, h=16, q=SEQ)
        by_token = heads_dram.rearrange("(n d) -> n d", d=D)
        in_small, in_patch, in_proj = sem("in_small"), sem("in_patch"), sem("in_proj")
        in_attn = [sem("in_attn0"), sem("in_attn1")]
        in_exp = [sem("in_exp0"), sem("in_exp1")]
        in_out = [sem("in_out0"), sem("in_out1")]
        consts = sem("consts")
        stored = sem("stored")

        NORMS = ["L0i_", "L0_", "L0m_", "L0f_", "L1_", "L1o_", "L1f_", "L2_", "L2f_", "L3_", "L3f_"]
        TURNS = ["L0_", "L0o_", "L0m_", "L0f_", "L1_", "L1o_", "L1f_", "L2_", "L2f_", "L3_", "L3o_", "L3f_"]
        stats_done, var_done, sd_done = sem("stats_done"), sem("var_done"), sem("sd_done")
        turned, xt_done = sem("turned"), sem("xt_done")
        norm_nth = NORMS.index

        def cuts(s):
            return [(GT, g * GT) for g in range(G)] if s in GROUPED else [(rows_of(g), g * P) for g in range(NT)]

        def norm_count(s, n):
            return sum(len(cuts(x)) for x in NORMS[:norm_nth(s)]) + n

        normed = sem("normed")
        SPLITS = ["L0m_", "L0f_", "L1f_"]
        xl_done = sem("xl_done")

        def normed_of(s):
            return lambda g: (normed, norm_count(s, g + 1))

        def xt_count(s, n):
            return sum(len(cuts(x)) for x in TURNS[:TURNS.index(s)]) + n

        def xt_all(s):
            return xt_count(s, len(cuts(s)))

        def norm_vector(v, s, src, dst):
            m = len(cuts(s))
            for g, (n, _) in enumerate(cuts(s)):
                v.bn_stats(stats[0:n, g, :], src[0:n, g, :]).then_inc(stats_done, 1)
            for g, (n, _) in enumerate(cuts(s)):
                v.wait_ge(stats_done, norm_count(s, g + 1))
                last = v.bn_aggr(mv[0:n, g, :], stats[0:n, g, :])
            last.then_inc(var_done, 1)
            v.wait_ge(sd_done, norm_nth(s) + 1)
            vchain.link(v, v.reciprocal(rs[:, 0:m], sd[:, 0:m]))
            for g, (n, _) in enumerate(cuts(s)):
                v.tensor_scalar(dst[0:n, g, :], src[0:n, g, :], mv[0:n, g, 0:1], rs[0:n, g:g + 1],
                                ALU.subtract, ALU.mult).then_inc(normed, 1)

        def norm_scalar(a, s):
            m = len(cuts(s))
            a.activation(warm[:, norm_nth(s):norm_nth(s) + 1], eps[:, 0:1], ACT.Sqrt)
            a.wait_ge(var_done, norm_nth(s) + 1)
            a.activation(sd[:, 0:m], mv[:, 0:m, 1], ACT.Sqrt, bias=eps[:, 0:1]).then_inc(sd_done, 1)

        def turn_tensor(pe, s, src, ready):
            for g, (n, _) in enumerate(cuts(s)):
                pe.wait_ge(*ready(g))
                if g >= 2:
                    pe.wait_ge(xt_done, xt_count(s, g - 1))
                for c in range(C):
                    last = pe.transpose(bank[g % 2][:, c * P:c * P + n],
                                        src[0:n, g, c * P:(c + 1) * P], ident[0:n, 0:n])
                last.then_inc(turned, 1)

        def turn_scalar(a, s, scale=None, shift=None, split=False):
            for g, (n, at) in enumerate(cuts(s)):
                a.wait_ge(turned, xt_count(s, g + 1))
                src = bank[g % 2][:, 0:C * P].rearrange("p (c n) -> p c n", c=C)[:, :, 0:n]
                for dst in (XT, XH) if split else (XT,):
                    if scale is None:
                        last = a.activation(dst[:, :, at:at + n], src, ACT.Copy)
                    else:
                        for c in range(C):
                            last = a.activation(dst[:, c, at:at + n], src[:, c, :], ACT.Identity, bias=shift(c),
                                                scale=scale(c))
                last.then_inc(xt_done, 1)

        def split_vector(v, s):
            for g in range(NT):
                x = tile(g)
                v.wait_ge(xt_done, xt_count(s, g + 1))
                v.tensor_tensor(XL[:, :, x], XT[:, :, x], XH[:, :, x].bitcast(F32), ALU.subtract)\
                    .then_inc(xl_done, 1)

        def qk_tensor(pe, s, layer, which):
            pe.wait_ge(in_attn[layer % 2], 16 * (layer // 2 + 1))
            pe.wait_ge(xt_done, xt_all(s))
            u = 0
            for w in which:
                for c in range(C):
                    for half in range(2):
                        if u >= 4:
                            pe.wait_ge(sem(s + "qk_out"), u - 3)
                        for k in range(C):
                            last = pe.matmul(bank[2 + u % 4][:, 0:HS], a_w(layer, w)[:, k, c * P:(c + 1) * P],
                                             XT[:, k, half * HS:(half + 1) * HS], start=(k == 0), stop=(k == C - 1))
                        last.then_inc(sem(s + "qk"), 1)
                        u += 1

        def qk_scalar(a, s, which, func, bias):
            u = 0
            for w in which:
                for c in range(C):
                    for half in range(2):
                        a.wait_ge(sem(s + "qk"), u + 1)
                        dst = (QT, KT)[w][:, c, half * HS:(half + 1) * HS]
                        b = bias(w, c)
                        if s == "L3_" and w == 1:
                            for n in range(2):
                                last = a.activation(KM[:, c, n, half * HS:(half + 1) * HS], bank[2 + u % 4][:, 0:HS],
                                                    func, scale=parity[:, n:n + 1])
                            last.then_inc(sem(s + "qk_out"), 1)
                        elif b is None:
                            a.activation(dst, bank[2 + u % 4][:, 0:HS], func).then_inc(sem(s + "qk_out"), 1)
                        else:
                            a.activation(dst, bank[2 + u % 4][:, 0:HS], func, bias=b).then_inc(sem(s + "qk_out"), 1)
                        u += 1

        def v_tensor(pe, s, layer, bias):
            for g in range(G):
                if g >= 2:
                    pe.wait_ge(sem(s + "v_out"), g - 1)
                for k in range(C):
                    last = pe.matmul(bank[6 + g % 2][0:GT, 0:D], XT[:, k, tok(g)], a_w(layer, 2)[:, k, :],
                                     start=(k == 0), stop=(bias is None and k == C - 1))
                if bias is not None:
                    last = pe.matmul(bank[6 + g % 2][0:GT, 0:D], ones[0:1, 0:GT], bias, start=False, stop=True)
                last.then_inc(sem(s + "v"), 1)

        def v_vector(v, s, heads, hd):
            for g in range(G):
                v.wait_ge(sem(s + "v"), g + 1)
                v.tensor_copy(V[0:GT, g, 0:heads * (hd + 1)].rearrange("p (h d) -> p h d", h=heads)[:, :, 0:hd],
                              bank[6 + g % 2][0:GT, 0:D].rearrange("p (h d) -> p h d", h=heads))\
                    .then_inc(sem(s + "v_out"), 1)

        def v_ones(v, s, heads, hd):
            v.memset(V[0:GT, :, 0:heads * (hd + 1)].rearrange("p g (h d) -> p g h d", d=hd + 1)[:, :, :, hd],
                     1.0).then_inc(sem(s + "v_ones"), 1)

        def proj_tensor(pe, s, layer, ready, bias):
            for g in range(NT):
                pe.wait_ge(*ready(g))
                if g >= 2:
                    pe.wait_ge(sem(s + "added"), g - 1)
                for k in range(C):
                    pe.matmul(bank[2 + g % 2][0:rows_of(g), 0:D], XT[:, k, tile(g)], a_w(layer, 3)[:, k, :],
                              start=(k == 0), stop=False)
                pe.matmul(bank[2 + g % 2][0:rows_of(g), 0:D], ones[0:1, 0:rows_of(g)], bias, start=False, stop=True)\
                    .then_inc(sem(s + "proj"), 1)

        def proj_vector(v, s, dst, src):
            for g in range(NT):
                v.wait_ge(sem(s + "proj"), g + 1)
                v.tensor_tensor(dst[0:rows_of(g), g, :], bank[2 + g % 2][0:rows_of(g), 0:D], src[0:rows_of(g), g, :], ALU.add)\
                    .then_inc(sem(s + "added"), 1)
            v.wait_ge(sem(s + "added"), NT)

        KM = arena[:, 0:2 * C * SLOTS].rearrange("p (c a n) -> p c a n", c=C, a=2)

        def score_tensor(pe, s, g, heads):
            if g == 0:
                pe.wait_ge(sem(s + "qk_out"), 8)
            else:
                pe.wait_ge(sem(s + "masked"), g)
            for j in (0, 4, 1, 5, 2, 6, 3, 7):
                c, at = j // 4, slice(j % 4 * 32, j % 4 * 32 + 32)
                n = heads // 8
                keys = KM[at, c, :, tok(g)] if n == 2 else KT[at, c, tok(g)]
                last = pe.matmul(bank[j % 4][0:GT, c * n * GT:(c + 1) * n * GT], QT[at, c, tok(g)], keys,
                                 start=True, stop=True)
            last.then_inc(sem(s + "score"), 1)

        def score_vector(v, s, g, heads, mask):
            S = arena2[0:GT, (g % 3) * 16 * GT:((g % 3) * 16 + heads) * GT].rearrange("p (h n) -> p h n", h=heads)
            mx = arena2_mx(g, heads)
            v.wait_ge(sem(s + "score"), g + 1)
            if g >= 3:
                v.wait_ge(sem(s + "pT"), (g - 2) * (heads // 4))
            n = heads // 8
            by_bank = S.rearrange("p (c r a) n -> p c r a n", c=C, r=4)
            for r in range(4):
                scores = bank[r][0:GT, 0:C * n * GT]
                if n == 1:
                    last = v.tensor_tensor(by_bank[:, :, r, 0, :], scores.rearrange("p (c n) -> p c n", c=C),
                                           mask[0:GT, :].unsqueeze(1).to_broadcast([GT, C, GT]), ALU.add)
                else:
                    last = v.tensor_tensor(by_bank[:, :, r], scores.rearrange("p (c a n) -> p c a n", c=C, a=n),
                                           mask[0:GT, :].unsqueeze(1).unsqueeze(1).to_broadcast([GT, C, n, GT]),
                                           ALU.add)
            last.then_inc(sem(s + "masked"), 1)
            v.wait_ge(sem(s + "masked"), g + 1)
            vchain.link(v, v.tensor_reduce(mx, S, AX, ALU.max))
            v.tensor_tensor(S, S, mx.unsqueeze(2).to_broadcast([GT, heads, GT]), ALU.subtract)\
                .then_inc(sem(s + "shifted"), 1)

        def arena2_mx(g, heads):
            return r_mx[0:GT, g % 3, 0:heads]

        def soft_scalar(a, s, g, heads, scale):
            S = arena2[0:GT, (g % 3) * 16 * GT:((g % 3) * 16 + heads) * GT].rearrange("p (h n) -> p h n", h=heads)
            PT = hT[0:GT].rearrange("p k n -> p (k n)")[:, 0:heads * GT].rearrange("p (h n) -> p h n", h=heads)
            a.wait_ge(sem(s + "shifted"), g + 1)
            a.activation(S, S, ACT.Exp, scale=scale).then_inc(sem(s + "exp"), 1)
            if g >= 1:
                a.wait_ge(sem(s + "pv"), g)
            for j in range(heads // 4):
                a.wait_ge(sem(s + "pT"), g * (heads // 4) + j + 1)
                a.activation(PT[:, 4 * j:4 * j + 4, :],
                             bank[4 + j % 2][0:GT, 0:4 * GT].rearrange("p (h n) -> p h n", h=4), ACT.Copy)\
                    .then_inc(sem(s + "pT_out"), 1)

        def pv_tensor(pe, s, g, heads, hd, shared):
            S = arena2[0:GT, (g % 3) * 16 * GT:((g % 3) * 16 + heads) * GT].rearrange("p (h n) -> p h n", h=heads)
            PT = hT[0:GT].rearrange("p k n -> p (k n)")[:, 0:heads * GT].rearrange("p (h n) -> p h n", h=heads)
            pe.wait_ge(sem(s + "exp"), g + 1)
            for j in range(heads // 4):
                n = g * (heads // 4) + j
                if n >= 2:
                    pe.wait_ge(sem(s + "pT_out"), n - 1)
                for h in range(4):
                    last = pe.transpose(bank[4 + j % 2][0:GT, h * GT:(h + 1) * GT], S[:, 4 * j + h, :],
                                        ident[0:GT, 0:GT])
                last.then_inc(sem(s + "pT"), 1)
            pe.wait_ge(sem(s + "pT_out"), (g + 1) * (heads // 4))
            if g == 0:
                pe.wait_ge(sem(s + "v_out"), G)
                pe.wait_ge(sem(s + "v_ones"), 1)
            else:
                pe.wait_ge(sem(s + "o"), g)
            n = hd + 1
            for h in range(heads):
                hv = h % shared
                last = pe.matmul(bank[6][0:GT, h * n:(h + 1) * n], PT[:, h, :], V[0:GT, g, hv * n:(hv + 1) * n],
                                 start=True, stop=True)
            last.then_inc(sem(s + "pv"), 1)

        def out_vector(v, s, g, heads, hd):
            o = bank[6][0:GT, 0:heads * (hd + 1)].rearrange("p (h d) -> p h d", h=heads)
            den = r_mx[0:GT, 3, 0:heads]
            v.wait_ge(sem(s + "pv"), g + 1)
            if g:
                v.wait_ge(sem(s + "o"), g)
            vchain.link(v, v.reciprocal(den, o[:, :, hd]))
            v.tensor_tensor(O[0:GT, g, :].rearrange("p (h d) -> p h d", h=heads), o[:, :, 0:hd],
                            den.unsqueeze(2).to_broadcast([GT, heads, hd]), ALU.mult).then_inc(sem(s + "o"), 1)


        FE = arena[:, 0:32 * GT].rearrange("p (w h n) -> p w h n", w=2, h=16)
        FS = arena[:, 32 * GT:64 * GT].rearrange("p (w h n) -> p w h n", w=2, h=16)
        FC = arena2[:, 0:32 * GT].rearrange("p (w h n) -> p w h n", w=2, h=16)
        FPT = arena2[0:GT, 32 * GT:48 * GT].rearrange("p (h n) -> p h n", h=16)
        FR = hT[:, 0:2, 0:4 * GT]

        LEAD = 3
        def heads_of(x, w, j):
            return x[:, w, 4 * j:4 * j + 4, :]

        def phase_tensor(pe, g, j):
            s = "L0_"
            for w in range(2):
                u = 8 * g + 2 * j + w
                if u >= 4:
                    pe.wait_ge(sem(s + "phase_out"), u - 3)
                for h in range(4):
                    last = pe.matmul(bank[u % 4][:, h * GT:(h + 1) * GT], proj8[:, j % 2, h, :],
                                     (QT, KT)[w][:, j // 2, tok(g)], start=True, stop=True)
                last.then_inc(sem(s + "phase"), 1)

        def similar_tensor(pe, g, j):
            s = "L0_"
            n = g * 4 + j
            pe.wait_ge(sem(s + "cos"), n + 1)
            if n >= 2:
                pe.wait_ge(sem(s + "sim_out"), n - 1)
            for h in range(4):
                for k, f in enumerate((FS, FC)):
                    last = pe.matmul(bank[4 + j % 2][0:GT, h * GT:(h + 1) * GT], f[:, 1, 4 * j + h, :],
                                     f[:, 0, 4 * j + h, :], start=(k == 0), stop=(k == 1))
            last.then_inc(sem(s + "sim"), 1)

        def values_tensor(pe, g, j):
            s = "L0_"
            pe.wait_ge(sem(s + "sim_out"), 4 * g + j + 1)
            if g == 0 and j == 0:
                pe.wait_ge(sem(s + "v_out"), G)
            if g and j == 0:
                pe.wait_ge(sem(s + "o"), g)
            for h in range(4 * j, 4 * j + 4):
                last = pe.matmul(bank[6][0:GT, h * 16:(h + 1) * 16], FPT[:, h, :], V[0:GT, g, h * 17:h * 17 + 16],
                                 start=True, stop=True)
            last.then_inc(sem(s + "pv"), 1)

        def phase_vector(v, g, j):
            s = "L0_"
            for w in range(2):
                u = 8 * g + 2 * j + w
                v.wait_ge(sem(s + "phase"), u + 1)
                if u >= 2:
                    v.wait_ge(sem(s + "phase_out"), u - 1)
                if g and w == 0:
                    v.wait_ge(sem(s + "sin"), 4 * (g - 1) + j + 1)
                vchain.link(v, v.tensor_scalar(FR[:, u % 2, :], bank[u % 4][:, 0:4 * GT], MAGIC, -MAGIC,
                                               ALU.add, ALU.add))
                v.tensor_tensor(heads_of(FE, w, j), bank[u % 4][:, 0:4 * GT].rearrange("p (h n) -> p h n", h=4),
                                FR[:, u % 2, :].rearrange("p (h n) -> p h n", h=4), ALU.subtract)\
                    .then_inc(sem(s + "phase_out"), 1)

        def similar_vector(v, g, j):
            s = "L0_"
            v.wait_ge(sem(s + "sim"), 4 * g + j + 1)
            if g:
                v.wait_ge(sem(s + "pv"), 4 * (g - 1) + j + 1)
            v.scalar_tensor_tensor(FPT[:, 4 * j:4 * j + 4, :],
                                   bank[4 + j % 2][0:GT, 0:4 * GT].rearrange("p (h n) -> p h n", h=4),
                                   1.0 / 128, same[0:GT, :].unsqueeze(1).to_broadcast([GT, 4, GT]),
                                   ALU.mult, ALU.mult).then_inc(sem(s + "sim_out"), 1)

        def values_out_vector(v, g):
            v.wait_ge(sem("L0_pv"), 4 * g + 4)
            v.tensor_copy(O[0:GT, g, :], bank[6][0:GT, 0:D]).then_inc(sem("L0_o"), 1)

        def fourier_scalar(a, g, j):
            s = "L0_"
            n = 4 * g + j
            a.wait_ge(sem(s + "phase_out"), 2 * n + 2)
            if g:
                a.wait_ge(sem(s + "sim"), n - 3)
            a.activation(FC[:, :, 4 * j:4 * j + 4, :], FE[:, :, 4 * j:4 * j + 4, :], ACT.Abs)\
                .then_inc(sem(s + "abs"), 1)
            a.activation(FS[:, :, 4 * j:4 * j + 4, :], FE[:, :, 4 * j:4 * j + 4, :], ACT.Sin, scale=TWO_PI)\
                .then_inc(sem(s + "sin"), 1)
            a.wait_ge(sem(s + "abs"), n + 1)
            a.activation(FC[:, :, 4 * j:4 * j + 4, :], FC[:, :, 4 * j:4 * j + 4, :], ACT.Sin, scale=-TWO_PI,
                         bias=eps[:, 1:2]).then_inc(sem(s + "cos"), 1)

        KI = arena[0:GT, 0:IMAGES * D].rearrange("p (i n) -> p i n", i=IMAGES)
        VC = arena[0:GT, IMAGES * D:IMAGES * D + G * C * (P + 1)].rearrange("p (g c n) -> p g c n", g=G, c=C)
        KVM = arena2[:, 0:2 * C * 2 * P].rearrange("p (b c n) -> p b c n", b=2, c=C)

        def linear_tensor(pe):
            s = "L2_"
            pe.wait_ge(sem(s + "qk_out"), 4)
            pe.wait_ge(sem(s + "v_ones"), 1)
            linear_kv(pe, 0)
            for g in range(G):
                if g + 1 < G:
                    linear_kv(pe, g + 1)
                pe.wait_ge(sem(s + "kv_out"), g + 1)
                for i in range(g * PER, min((g + 1) * PER, IMAGES)):
                    if i >= 2:
                        pe.wait_ge(sem(s + "outer_out"), i - 1)
                    for c in range(C):
                        last = pe.matmul(bank[i % 2][:, c * (P + 1):(c + 1) * (P + 1)], KI[:, i, c * P:(c + 1) * P],
                                         VC[:, g, c, :], start=True, stop=True)
                    last.then_inc(sem(s + "outer"), 1)
                    if i:
                        linear_apply(pe, i - 1)
            linear_apply(pe, IMAGES - 1)

        def linear_kv(pe, g):
            s = "L2_"
            if g >= 2:
                pe.wait_ge(sem(s + "kv_out"), g - 1)
            for k in range(C):
                last = pe.matmul(bank[6 + g % 2][0:GT, :], XT[:, k, tok(g)],
                                 wA[0][:, D * C:3 * D * C].rearrange("p (c n) -> p c n", c=C)[:, k, :],
                                 start=(k == 0), stop=(k == C - 1))
            last.then_inc(sem(s + "kv"), 1)

        def linear_apply(pe, i):
            s = "L2_"
            pe.wait_ge(sem(s + "outer_out"), i + 1)
            if i >= 2:
                pe.wait_ge(sem(s + "image"), i - 1)
            for half in range(2):
                for c in range(C):
                    o = (half * C + c) * SEQ
                    last = pe.matmul(bank[4 + i % 2][:, o:o + SEQ], KVM[:, i % 2, c, half * P:(half + 1) * P],
                                     QT[:, c, i * SEQ:(i + 1) * SEQ], start=True, stop=True)
            last.then_inc(sem(s + "applied"), 1)

        def linear_vector(v):
            s = "L2_"
            v.memset(VC[:, :, :, P], 1.0).then_inc(sem(s + "v_ones"), 1)
            block = block8[:, :].unsqueeze(1).to_broadcast([P, C, P])
            for i in range(IMAGES):
                v.wait_ge(sem(s + "outer"), i + 1)
                if i >= 2:
                    v.wait_ge(sem(s + "applied"), i - 1)
                b = bank[i % 2][:, 0:C * (P + 1)].rearrange("p (c n) -> p c n", c=C)
                v.tensor_tensor(KVM[:, i % 2, :, 0:P], b[:, :, 0:P], block, ALU.mult)
                v.tensor_tensor(KVM[:, i % 2, :, P:2 * P], block, b[:, :, P:P + 1].to_broadcast([P, C, P]), ALU.mult)\
                    .then_inc(sem(s + "outer_out"), 1)
                if i:
                    linear_divide(v, i - 1)
            linear_divide(v, IMAGES - 1)

        def linear_divide(v, i):
            s = "L2_"
            v.wait_ge(sem(s + "applied"), i + 1)
            b = bank[4 + i % 2]
            vchain.link(v, v.tensor_scalar(ksum[:, 0, :], b[:, 2 * SEQ:4 * SEQ], 1e-15, None, ALU.add))
            vchain.link(v, v.reciprocal(ksum[:, 1, :], ksum[:, 0, :]))
            v.tensor_tensor(XT[:, :, i * SEQ:(i + 1) * SEQ], b[:, 0:2 * SEQ].rearrange("p (c n) -> p c n", c=C),
                            ksum[:, 1, :].rearrange("p (c n) -> p c n", c=C), ALU.mult).then_inc(sem(s + "image"), 1)

        def linear_scalar(a):
            s = "L2_"
            for g in range(G):
                a.wait_ge(sem(s + "kv"), g + 1)
                kv = bank[6 + g % 2][0:GT, :]
                for i in range(g * PER, min((g + 1) * PER, IMAGES)):
                    j = (i - g * PER) * SEQ
                    a.activation(KI[:, i, :], kv[:, 0:D], ACT.Relu, scale=same[0:GT, j:j + 1])
                a.activation(VC[:, g, :, 0:P], kv[:, D:2 * D].rearrange("p (c n) -> p c n", c=C), ACT.Relu)\
                    .then_inc(sem(s + "kv_out"), 1)

        def half_of(h):
            return slice(h * HT, (h + 1) * HT)

        def y_bank(g):
            return bank[4 + g // 2][0:rows_of(g), (g % 2) * D:(g % 2) * D + D]

        UNITS_BEFORE = {"L0m_": 0, "L0f_": F1, "L1f_": F1 + E * F0}
        EXPERTS_BEFORE = {"L0m_": 0, "L0f_": 1, "L1f_": 1 + E}
        names = ["ffn_h0", "ffn_h1", "ffn_silu0", "ffn_silu1", "ffn_t0", "ffn_t1", "ffn_hh0", "ffn_hh1", "ffn_hl0",
                 "ffn_hl1", "ffn_uh", "ffn_ul", "ffn_dh", "ffn_dl", "ffn_y", "ffn_y_added", "ffn_gcur"]
        f_h, f_silu, f_t, f_hh, f_hl = ([sem(n) for n in names[2 * i:2 * i + 2]] for i in range(5))
        f_uh, f_ul, f_dh, f_dl, f_y, f_y_added, f_gcur = [sem(n) for n in names[10:]]
        act1 = QT[:, 0, 0:TOK]

        def unit(bufs, nf, k):
            k %= len(bufs) * nf
            return bufs[k // nf], k % nf

        def up_w(kind, nf, b, f):
            n = 2 * C if kind == "silu" else C
            return wE[b][:, 0:n * nf * P].rearrange("p (c n) -> p c n", c=n)[:, :, f * P:(f + 1) * P]

        def down_w(kind, nf, b, f):
            o = (2 * C if kind == "silu" else C) * nf * P
            return wE[b][:, o + f * D:o + (f + 1) * D]

        def three(high_a, low_a, high_b, low_b):
            return (high_a, high_b), (high_a, low_b), (low_a, high_b)

        def rounds_of(eng, rounds, body):
            if rounds > 1:
                with eng.Fori(0, rounds - 1) as i:
                    body(i, True)
            body(rounds - 1, False)

        def ffn_tensor(pe, s, kind, nf, bufs, rounds, hook=None):
            units, base = len(bufs) * nf, UNITS_BEFORE[s]
            blocks = 2 * C if kind == "silu" else C

            def h(u, k):
                pe.wait_ge(f_ul, u + 1)
                for half in range(2):
                    if kind == "silu":
                        if k:
                            pe.wait_ge(f_t[half], u - base)
                        dst = (bank[2 * half], bank[2 * half + 1])
                    else:
                        if k >= 2:
                            pe.wait_ge(f_hh[half], u - 1)
                        dst = (bank[2 * (k % 2) + half],)
                    x = half_of(half)
                    for j in range(blocks // C):
                        for c in range(C):
                            for n, (w, xx) in enumerate(three(UH, UL, XH, XL)):
                                last = pe.matmul(dst[j][:, 0:HT], w[:, k % 2, j * C + c, :], xx[:, c, x],
                                                 start=(c == 0 and n == 0), stop=(c == C - 1 and n == 2))
                    last.then_inc(f_h[half], 1)

            def y(u, e, k):
                f = k % nf
                for half in range(2):
                    pe.wait_ge(f_hl[half], u + 1)
                pe.wait_ge(f_dl, u + 1)
                if f == 0:
                    pe.wait_ge(f_y_added, (EXPERTS_BEFORE[s] + e + 1) * NT)
                for g in range(NT):
                    for p, (hid, w) in enumerate(three(HH, HL, DH, DL)):
                        last = pe.matmul(y_bank(g), hid[:, k % 2, tile(g)], w[:, k % 2, :],
                                         start=(f == 0 and g % 2 == 0 and p == 0), stop=(f == nf - 1 and p == 2),
                                         skip_group_check=True)
                last.then_inc(f_y, 1)

            def body(i, more):
                for k in range(units):
                    if k + 1 < units or more:
                        h(base + i * units + k + 1, k + 1)
                    if hook and not more:
                        hook(k)
                    y(base + i * units + k, len(bufs) * i + k // nf, k)

            pe.wait_ge(xl_done, (SPLITS.index(s) + 1) * NT)
            h(base, 0)
            rounds_of(pe, rounds, body)

        def ffn_scalar(a, s, kind, nf, wave, bufs, rounds, hook=None):
            units, base = len(bufs) * nf, UNITS_BEFORE[s]

            def up_high(i, k):
                b, f = unit(bufs, nf, k)
                if f == 0:
                    a.wait_ge(in_exp[b], 16 * (i + k // units + wave + 2 - b))
                w = up_w(kind, nf, b, f)
                a.activation(UH[:, k % 2, 0:w.shape[1], :], w, ACT.Copy).then_inc(f_uh, 1)

            def down_high(i, k, first=False):
                b, f = unit(bufs, nf, k)
                if not first:
                    a.wait_ge(f_y, base + i * units + k - 1)
                a.activation(DH[:, k % 2, :], down_w(kind, nf, b, f), ACT.Copy).then_inc(f_dh, 1)

            def body(i, more):
                for k in range(units):
                    b, f = unit(bufs, nf, k)
                    u = base + i * units + k
                    if kind == "silu":
                        for half in range(2):
                            a.wait_ge(f_h[half], u + 1)
                            a.activation(act1[:, half_of(half)], bank[2 * half][:, 0:HT], ACT.Silu)\
                                .then_inc(f_silu[half], 1)
                        if k + 2 < units or more:
                            up_high(i, k + 2)
                        for half in range(2):
                            a.wait_ge(f_t[half], u - base + 1)
                            a.activation(HH[:, k % 2, half_of(half)], KT[:, k % 2, half_of(half)], ACT.Copy)\
                                .then_inc(f_hh[half], 1)
                    else:
                        b1 = wE[b][:, nf * (C * P + D) + f:nf * (C * P + D) + f + 1]
                        for half in range(2):
                            a.wait_ge(f_h[half], u + 1)
                            if k >= 2 or base:
                                a.wait_ge(f_hl[half], u - 1)
                            src = bank[2 * (k % 2) + half][:, 0:HT]
                            a.activation(KT[:, k % 2, half_of(half)], src, ACT.Relu, bias=b1)
                            a.activation(HH[:, k % 2, half_of(half)], src, ACT.Relu, bias=b1)\
                                .then_inc(f_hh[half], 1)
                        if k + 2 < units or more:
                            up_high(i, k + 2)
                    if k + 1 < units or more:
                        down_high(i, k + 1, base == 0 and k == 0)
                    if hook and not more:
                        hook(k)

            up_high(0, 0)
            up_high(0, 1)
            down_high(0, 0, True)
            rounds_of(a, rounds, body)

        def ffn_vector(v, s, kind, nf, bufs, rounds, hook=None):
            units, base = len(bufs) * nf, UNITS_BEFORE[s]
            gated = s != "L0m_"

            def up_low(i, k):
                b, f = unit(bufs, nf, k)
                w = up_w(kind, nf, b, f)
                n = w.shape[1]
                v.wait_ge(f_uh, base + i * units + k + 1)
                v.tensor_tensor(UL[:, k % 2, 0:n, :], w, UH[:, k % 2, 0:n, :].bitcast(F32), ALU.subtract)\
                    .then_inc(f_ul, 1)

            def down_low(i, k):
                b, f = unit(bufs, nf, k)
                v.wait_ge(f_dh, base + i * units + k + 1)
                v.tensor_tensor(DL[:, k % 2, :], down_w(kind, nf, b, f), DH[:, k % 2, :].bitcast(F32), ALU.subtract)\
                    .then_inc(f_dl, 1)

            def hidden(i, k):
                u = base + i * units + k
                if kind == "silu":
                    for half in range(2):
                        v.wait_ge(f_silu[half], u - base + 1)
                        v.wait_ge(f_hl[half], u - 1)
                        v.tensor_tensor(KT[:, k % 2, half_of(half)], bank[2 * half + 1][:, 0:HT],
                                        act1[:, half_of(half)], ALU.mult).then_inc(f_t[half], 1)
                for half in range(2):
                    v.wait_ge(f_hh[half], u + 1)
                    x = half_of(half)
                    v.tensor_tensor(HL[:, k % 2, x], KT[:, k % 2, x], HH[:, k % 2, x].bitcast(F32), ALU.subtract)\
                        .then_inc(f_hl[half], 1)

            def add(i, k):
                e, b = len(bufs) * i + k // nf, k // nf
                before = (EXPERTS_BEFORE[s] + e) * NT
                if gated:
                    v.wait_ge(f_y_added, before + NT)
                    v.tensor_copy(gcur[0:P, b, :], gate[0:P, :, bass.ds(e, 1)].rearrange("p g e -> p (g e)"))\
                        .then_inc(f_gcur, 1)
                v.wait_ge(f_y, base + i * units + k + 1)
                if gated:
                    v.wait_ge(f_gcur, EXPERTS_BEFORE[s] + e)
                for g in range(NT):
                    v.wait_ge(f_y_added, before + g + 1)
                    if gated:
                        v.scalar_tensor_tensor(H[0:rows_of(g), g, :], y_bank(g), gcur[0:rows_of(g), b, g:g + 1], H[0:rows_of(g), g, :],
                                               ALU.mult, ALU.add).then_inc(f_y_added, 1)
                    else:
                        v.tensor_tensor(R0[0:rows_of(g), g, :], y_bank(g), R0[0:rows_of(g), g, :], ALU.add)\
                            .then_inc(f_y_added, 1)

            def body(i, more):
                for k in range(units):
                    if k + 1 < units or more:
                        hidden(i, k + 1)
                    if hook and not more:
                        hook(k)
                    if k % nf == nf - 1:
                        add(i, k)
                    if k + 3 < units or more:
                        up_low(i, k + 3)
                    if k + 2 < units or more:
                        down_low(i, k + 2)

            up_low(0, 0)
            up_low(0, 1)
            down_low(0, 0)
            hidden(0, 0)
            up_low(0, 2)
            down_low(0, 1)
            rounds_of(v, rounds, body)

        deep_h = arena2[:, 0:8 * TOK].rearrange("p (k n) -> p k n", k=8)

        def y_tensor(pe, s, i, b, f, nf, slot, w2, hready):
            for half in range(2):
                pe.wait_ge(sem(s + f"h_ready{half}"), hready)
            if f == 0:
                pe.wait_ge(sem(s + "y_added"), NT * (2 * i + b + 1))
            for g in range(NT):
                last = pe.matmul(y_bank(g), deep_h[:, slot, tile(g)], w2,
                                 start=(f == 0 and g % 2 == 0), stop=(f == nf - 1), skip_group_check=True)
            last.then_inc(sem(s + "y"), 1)

        def free_banks(eng, s, half, n):
            eng.sem_inc(sem(s + f"h_ready{half}"), n)

        def y_vector(v, s, i, b, units_done, nf, gcol):
            v.wait_ge(sem(s + "y"), units_done)
            for g in range(NT):
                v.wait_ge(sem(s + "y_added"), NT * (2 * i + b) + g + 1)
                v.scalar_tensor_tensor(H[0:rows_of(g), g, :], y_bank(g), gcol(g)[0:rows_of(g), :], H[0:rows_of(g), g, :],
                                       ALU.mult, ALU.add).then_inc(sem(s + "y_added"), 1)

        def deep_w(b):
            w = wE[b]
            m = C * D
            return ([w[:, j * m:(j + 1) * m].rearrange("p (c n) -> p c n", c=C) for j in range(3)],
                    [w[:, 3 * m + 2 * j:3 * m + 2 * j + 2] for j in range(2)])

        def deep_tensor(pe, s, wave):
            with pe.Fori(0, E // 2) as i:
                for k in range(8):
                    layer, b, f = k // 4, k // 2 % 2, k % 2
                    if k % 2 == 0 and layer == 0:
                        pe.wait_ge(in_exp[b], 16 * (i + wave + 2 - b))
                    for half in range(2):
                        if layer == 1:
                            pe.wait_ge(sem(s + f"h_ready{half}"), i * 8 + 2 * b + 4)
                        pe.wait_ge(sem(s + f"h_ready{half}"), i * 8 + k + 1)
                        for c in range(C):
                            src = XT[:, c, half_of(half)] if layer == 0 else deep_h[:, 2 * b + c, half_of(half)]
                            last = pe.matmul(bank[2 * (k % 2) + half][:, 0:HT], deep_w(b)[0][layer][:, c, f * P:(f + 1) * P],
                                             src, start=(c == 0), stop=(c == C - 1))
                        last.then_inc(sem(s + f"h{half}"), 1)
                for b in range(2):
                    for f in range(2):
                        y_tensor(pe, s, i, b, f, 2, 4 + 2 * b + f, deep_w(b)[0][2][:, f, :], i * 8 + 8 + 2 * b)

        def deep_vector(v, s):
            with v.Fori(0, E // 2) as i:
                for k in range(8):
                    b = k // 2 % 2
                    if k < 4 and k % 2 == 0:
                        v.wait_ge(sem(s + "y_added"), 2 * NT * i + NT)
                        v.tensor_copy(gcur[0:P, b, :], gate[0:P, :, bass.ds(2 * i + b, 1)].rearrange("p g e -> p (g e)"))\
                            .then_inc(sem(s + "gcur"), 1)
                    v.wait_ge(sem(s + "h1"), i * 8 + k + 1)
                    v.tensor_scalar(deep_h[:, k, half_of(1)], bank[2 * (k % 2) + 1][:, 0:HT],
                                    deep_w(b)[1][k // 4][:, k % 2:k % 2 + 1], 0.0, ALU.add, ALU.max)\
                        .then_inc(sem(s + "h_ready1"), 1)
                v.wait_ge(sem(s + "gcur"), 2 * i + 2)
                for b in range(2):
                    y_vector(v, s, i, b, i * 4 + 2 * b + 2, 2, lambda g, b=b: gcur[:, b, g:g + 1])

        def deep_scalar(a, s):
            with a.Fori(0, E // 2) as i:
                for k in range(8):
                    b = k // 2 % 2
                    a.wait_ge(sem(s + "h0"), i * 8 + k + 1)
                    a.activation(deep_h[:, k, half_of(0)], bank[2 * (k % 2)][:, 0:HT], ACT.Relu,
                                 bias=deep_w(b)[1][k // 4][:, k % 2:k % 2 + 1]).then_inc(sem(s + "h_ready0"), 1)

        def gate_tensor(pe, s, which, bias):
            pe.wait_ge(xt_done, xt_all(s))
            for g in range(NT):
                for k in range(C):
                    last = pe.matmul(bank[7][0:P, g * E:(g + 1) * E], XT[:, k, g * P:(g + 1) * P], gates[:, which, k, :],
                                     start=(k == 0), stop=(bias is None and k == C - 1))
                if bias is not None:
                    last = pe.matmul(bank[7][0:P, g * E:(g + 1) * E], ones[0:1, 0:P], bias, start=False, stop=True)
            last.then_inc(sem(s + "gate_mm"), 1)

        def wide(x):
            return x.unsqueeze(2).to_broadcast([P, NT, E])

        def over_groups(x):
            return x[0:P, :].unsqueeze(1).to_broadcast([P, NT, E])

        def first_of(v, values, best, hot, tmp, one):
            vchain.link(v, v.tensor_tensor(tmp, values, wide(best), ALU.is_equal))
            vchain.link(v, v.tensor_tensor(tmp, tmp, over_groups(revE), ALU.mult))
            vchain.link(v, v.tensor_reduce(one, tmp, AX, ALU.max))
            vchain.link(v, v.tensor_tensor(hot, tmp, wide(one), ALU.is_equal))

        def R(i):
            return rt[0:P, i]

        def r(i):
            return r1[0:P, i]

        def get_scores(v, s):
            v.wait_ge(sem(s + "gate_mm"), 1)
            vchain.link(v, v.tensor_copy(score[0:P], bank[7][0:P, 0:NT * E].rearrange("p (g e) -> p g e", g=NT)))

        def exp_on_scalar(a, s, n, src, dst):
            a.wait_ge(sem(s + "to_exp"), n)
            a.activation(dst, src, ACT.Exp).then_inc(sem(s + "exped"), 1)

        def route0_vector(v):
            s = "L0f_"
            get_scores(v, s)
            S = score[0:P]
            L = lambda ins: vchain.link(v, ins)
            L(v.tensor_reduce(r(0), S, AX, ALU.max))
            first_of(v, S, r(0), R(0), R(1), r(1))
            L(v.scalar_tensor_tensor(R(2), R(0), NEG, S, ALU.mult, ALU.add))
            L(v.tensor_reduce(r(2), R(2), AX, ALU.max))
            first_of(v, R(2), r(2), R(3), R(1), r(1))
            L(v.scalar_tensor_tensor(R(4), S, -1.0, S, ALU.mult, ALU.max))
            for n, (top, src, d, keep) in enumerate(((r(0), S, R(5), R(6)), (r(2), R(2), R(7), R(8)))):
                L(v.tensor_tensor(R(9), R(4), wide(top), ALU.max))
                L(v.tensor_tensor(R(10), S, wide(top), ALU.subtract))
                L(v.scalar_tensor_tensor(R(11), R(9), 0.02, R(10), ALU.mult, ALU.add))
                L(v.tensor_scalar(keep, R(11), 0.0, None, ALU.is_ge))
                v.tensor_tensor(d, src, wide(top), ALU.subtract).then_inc(sem(s + "to_exp"), 1)
            for n, (d, keep, hot) in enumerate(((R(5), R(6), R(0)), (R(7), R(8), R(3)))):
                v.wait_ge(sem(s + "exped"), n + 1)
                L(v.tensor_tensor(keep, keep, d, ALU.mult))
                L(v.tensor_reduce(r(3), keep, AX, ALU.add))
                L(v.reciprocal(r(4), r(3)))
                L(v.tensor_tensor(hot, hot, wide(r(4)), ALU.mult))
            v.tensor_tensor(gate[0:P], R(0), R(3), ALU.add).then_inc(sem(s + "gate"), 1)
            v.wait_ge(sem(s + "gate"), 1)

        def route0_scalar(a):
            exp_on_scalar(a, "L0f_", 1, R(5), R(5))
            exp_on_scalar(a, "L0f_", 2, R(7), R(7))

        def route1_vector(v):
            s = "L1f_"
            get_scores(v, s)
            S = score[0:P]
            L = lambda ins: vchain.link(v, ins)
            for g in range(NT):
                last = v.max(R(0)[:, g, :], S[:, g, :])
            L(last)
            L(v.tensor_tensor(R(1), S, wide(R(0)[:, :, 1]), ALU.is_ge))
            v.tensor_tensor(R(2), S, wide(R(0)[:, :, 0]), ALU.subtract).then_inc(sem(s + "to_exp"), 1)
            v.wait_ge(sem(s + "exped"), 1)
            L(v.tensor_tensor(R(3), R(1), R(2), ALU.mult))
            L(v.tensor_reduce(r(0), R(3), AX, ALU.add))
            L(v.reciprocal(r(1), r(0)))
            v.scalar_tensor_tensor(gate[0:P], R(3), 1.0 / E, wide(r(1)), ALU.mult, ALU.mult)\
                .then_inc(sem(s + "gate"), 1)
            v.wait_ge(sem(s + "gate"), 1)

        def probs_vector(v, s):
            get_scores(v, s)
            S = score[0:P]
            L = lambda ins: vchain.link(v, ins)
            L(v.tensor_reduce(r(0), S, AX, ALU.max))
            v.tensor_tensor(R(2), S, wide(r(0)), ALU.subtract).then_inc(sem(s + "to_exp"), 1)
            v.wait_ge(sem(s + "exped"), 1)
            L(v.tensor_reduce(r(1), R(2), AX, ALU.add))
            L(v.reciprocal(r(2), r(1)))
            L(v.tensor_tensor(R(3), R(2), wide(r(2)), ALU.mult))
            L(v.tensor_reduce(r(3), R(3), AX, ALU.max))
            first_of(v, R(3), r(3), R(4), R(5), r(4))

        def route2_vector(v):
            s = "L2f_"
            probs_vector(v, s)
            L = lambda ins: vchain.link(v, ins)
            L(v.scalar_tensor_tensor(R(6), R(4), -2.0, R(3), ALU.mult, ALU.add))
            L(v.tensor_reduce(r(5), R(6), AX, ALU.max))
            first_of(v, R(6), r(5), R(7), R(5), r(4))
            L(v.tensor_tensor(R(8), R(4), wide(R(3)[:, :, 0]), ALU.mult))
            L(v.tensor_tensor(R(9), R(7), wide(R(3)[:, :, 1]), ALU.mult))
            v.tensor_tensor(gate[0:P], R(8), R(9), ALU.add).then_inc(sem(s + "gate"), 1)
            v.wait_ge(sem(s + "gate"), 1)

        def bias_tensor(pe, s, which):
            pe.wait_ge(sem(s + "gate"), 1)
            for g in range(NT):
                pe.transpose(bank[2 + g // 4][0:E, g % 4 * P:(g % 4 + 1) * P], gate[0:P, g, :], ident[0:P, 0:P])\
                    .then_inc(sem(s + "gateT"), 1)
            pe.wait_ge(sem(s + "gateT_out"), 2)
            for g in range(NT):
                pe.matmul(y_bank(g), gateT[:, g, 0:rows_of(g)], tab[:, which, :], start=True, stop=True)\
                    .then_inc(sem(s + "bias"), 1)

        def bias_scalar(a, s):
            for j, n in enumerate((4, 1)):
                a.wait_ge(sem(s + "gateT"), 4 * j + n)
                a.activation(gateT[:, 4 * j:4 * j + n, :],
                             bank[2 + j][0:E, 0:n * P].rearrange("p (g n) -> p g n", g=n), ACT.Copy)\
                    .then_inc(sem(s + "gateT_out"), 1)

        def bias_vector(v, s, dst, added):
            v.wait_ge(sem(s + "bias"), NT)
            for g in range(NT):
                v.tensor_tensor(dst[0:rows_of(g), g, :], y_bank(g), dst[0:rows_of(g), g, :], ALU.add).then_inc(added, 1)

        DSP = part(0, NT * TOK, "p (g n) -> p g n", g=NT)
        XP = [part(8 * TOK + i * NT * D, NT * D, "p (g n) -> p g n", g=NT) for i in range(2)]
        DST = [part(g * E * P, E * P, "p (e n) -> p e n", e=E)[0:CAP] for g in range(NT)]
        YH = part(8 * TOK + 8 * P, E * D, "p (e n) -> p e n", e=E)[0:CAP]
        SL = arena2[:, 0:C * TOK].rearrange("p (c n) -> p c n", c=C)
        YS = arena2[0:CAP, C * TOK:C * TOK + E * D].rearrange("p (e n) -> p e n", e=E)
        diag = arena2[0:P, C * TOK + E * D:C * TOK + E * D + 2 * P].rearrange("p (b n) -> p b n", b=2)
        destB = V[0:CAP].rearrange("p g n -> p (g n)")[:, 0:NT * P]
        GELU_IN = 2.0 ** 0.5 / 1.41421

        def switch_w(b):
            w, n = wE[b], C * F1 * P
            return (w[:, 0:n].rearrange("p (c n) -> p c n", c=C), w[:, n:n + F1],
                    w[:, n + F1:n + F1 + F1 * D].rearrange("p (f n) -> p f n", f=F1))

        def switch_vector(v):
            s = "L3f_"
            probs_vector(v, s)
            L = lambda ins: vchain.link(v, ins)
            L(v.reciprocal(r(5), r(3)))
            L(v.tensor_tensor(r(6), r(3), r(5), ALU.mult))
            for g in range(NT):
                v.tensor_scalar(X[0:rows_of(g), g, :], X[0:rows_of(g), g, :], r(6)[0:rows_of(g), g:g + 1], None, ALU.mult)\
                    .then_inc(sem(s + "xs"), 1)
            for g in range(NT):
                n = rows_of(g)
                v.wait_ge(sem(s + "xs_high"), g + 1)
                v.tensor_tensor(XP[1][0:n, g, :], X[0:n, g, :], XP[0][0:n, g, :].bitcast(F32), ALU.subtract)\
                    .then_inc(sem(s + "xs_low"), 1)
            L(v.tensor_tensor(R(5), R(4), over_groups(iotaE), ALU.mult))
            L(v.tensor_reduce(r(0), R(5), AX, ALU.add))
            L(v.tensor_scalar(R(4)[:, NT - 1, :], R(4)[:, NT - 1, :], valid[:, 0:1], None, ALU.mult))
            v.tensor_copy(R(6), R(4)).then_inc(sem(s + "hot"), 1)
            v.wait_ge(sem(s + "cum"), 1)
            L(v.tensor_tensor(R(7), R(4), bank[7][0:P, 64:64 + NT * E].rearrange("p (g e) -> p g e", g=NT), ALU.mult))
            L(v.tensor_reduce(r(1), R(7), AX, ALU.add))
            L(v.tensor_scalar(r(2), r(1), float(CAP), None, ALU.is_le))
            L(v.tensor_reduce(r(7), R(4), AX, ALU.add))
            L(v.tensor_tensor(r(0), r(0), r(7), ALU.mult))
            L(v.scalar_tensor_tensor(r(3), r(0), float(CAP), r(1), ALU.mult, ALU.add))
            L(v.tensor_tensor(r(4), r(3), r(2), ALU.mult))
            L(v.tensor_scalar(r(4), r(4), -1.0, None, ALU.add))
            L(v.tensor_scalar(r(5), r(2), -1.0, 1.0, ALU.mult, ALU.add))
            for g in range(NT):
                v.tensor_scalar(DSP[:, g, :], slot_id[0:P, :], r(4)[:, g:g + 1], None, ALU.is_equal)\
                    .then_inc(sem(s + "dispatch"), 1)
            for g in range(NT):
                if g >= 2:
                    v.wait_ge(sem(s + "dest"), g - 1)
                v.tensor_scalar(diag[:, g % 2, :], ident[0:P, 0:P], r(4)[:, g:g + 1], None, ALU.mult)\
                    .then_inc(sem(s + "diag"), 1)
            for j, n in enumerate((4, 1)):
                v.wait_ge(sem(s + "dest"), 4 * j + n)
                last = v.tensor_copy(destB[:, 4 * j * P:(4 * j + n) * P], bank[4 + j][0:CAP, 0:n * P])
            L(last)
            v.wait_ge(sem(s + "slots"), 4)
            for g in range(NT):
                for e in range(E):
                    last = v.tensor_scalar(DST[g][:, e, :], destB[:, g * P:(g + 1) * P], slot_own[0:CAP, e:e + 1], None,
                                           ALU.is_equal)
            last.then_inc(sem(s + "combine"), 1)

        def switch_tensor(pe, wave):
            s = "L3f_"
            pe.wait_ge(sem(s + "hot"), 1)
            for g in range(NT):
                for k in range(g + 1):
                    last = pe.matmul(bank[7][0:P, 64 + g * E:64 + (g + 1) * E], (tri if k == g else ones)[0:P, 0:P],
                                     R(6)[:, k, :], start=(k == 0), stop=(k == g))
            last.then_inc(sem(s + "cum"), 1)
            pe.wait_ge(sem(s + "dispatch"), NT)
            pe.wait_ge(sem(s + "xs_low"), NT)
            for c in range(C):
                for half in range(2):
                    for g in range(NT):
                        n = rows_of(g)
                        for j in range(2):
                            last = pe.matmul(bank[2 * c + half][:, 0:HT], XP[j][0:n, g, c * P:(c + 1) * P],
                                             DSP[0:n, g, half_of(half)], start=(g == 0 and j == 0),
                                             stop=(g == NT - 1 and j == 1))
                    last.then_inc(sem(s + "slots"), 1)
            for g in range(NT):
                pe.wait_ge(sem(s + "diag"), g + 1)
                pe.matmul(bank[4 + g // 4][0:CAP, g % 4 * P:(g % 4 + 1) * P], ones[0:P, 0:CAP], diag[:, g % 2, :],
                          start=True, stop=True).then_inc(sem(s + "dest"), 1)
            pe.wait_ge(sem(s + "slots_out"), 4)

            def hidden(i, b):
                pe.wait_ge(in_exp[b], 16 * (i + wave + 2 - b))
                pe.wait_ge(sem(s + "gelu"), 2 * i + b + 1)
                for f in range(F1):
                    for c in range(C):
                        last = pe.matmul(bank[2 * b + f // 4][:, f % 4 * CAP:(f % 4 + 1) * CAP],
                                         switch_w(b)[0][:, c, f * P:(f + 1) * P],
                                         SL[:, c, bass.ds((2 * i + b) * CAP, CAP)], start=(c == 0), stop=(c == C - 1))
                    if f % 4 == 3:
                        last.then_inc(sem(s + "hid"), 1)

            def body(i, more):
                for b in range(2):
                    if b == 0 or more:
                        hidden(i + b, 1 - b)
                    pe.wait_ge(in_out[b], 16 * (i + 1))
                    pe.wait_ge(sem(s + "gelu"), 2 * i + b + 3)
                    pe.wait_ge(sem(s + "ys_free"), 2 * i + b + 1)
                    for f in range(F1):
                        last = pe.matmul(bank[6 + b][0:CAP, 0:D], hT[:, b, f * CAP:(f + 1) * CAP],
                                         switch_w(b)[2][:, f, :], start=(f == 0), stop=(f == F1 - 1))
                    last.then_inc(sem(s + "ys"), 1)

            hidden(0, 0)
            rounds_of(pe, E // 2, body)
            pe.wait_ge(sem(s + "yl"), E)
            pe.wait_ge(sem(s + "combine"), 1)
            for g in range(NT):
                n = rows_of(g)
                if g >= 2:
                    pe.wait_ge(sem(s + "final"), g - 1)
                for e in range(E):
                    for j, y in enumerate((YH, YL[0:CAP])):
                        last = pe.matmul(bank[4 + g % 2][0:n, 0:D], DST[g][:, e, 0:n], y[:, e, :],
                                         start=(e == 0 and j == 0), stop=(e == E - 1 and j == 1))
                last.then_inc(sem(s + "gathered"), 1)

        def switch_scalar(a):
            s = "L3f_"
            exp_on_scalar(a, s, 1, R(2), R(2))
            for g in range(NT):
                n = rows_of(g)
                a.wait_ge(sem(s + "xs"), g + 1)
                a.activation(XP[0][0:n, g, :], X[0:n, g, :], ACT.Copy).then_inc(sem(s + "xs_high"), 1)
            for c in range(C):
                for half in range(2):
                    a.wait_ge(sem(s + "slots"), 2 * c + half + 1)
                    a.activation(SL[:, c, half_of(half)], bank[2 * c + half][:, 0:HT], ACT.Copy)\
                        .then_inc(sem(s + "slots_out"), 1)
            with a.Fori(0, E // 2) as i:
                for b in range(2):
                    a.wait_ge(sem(s + "b1s"), 2 * i + b + 1)
                    for f in range(F1):
                        if f % 4 == 0:
                            a.wait_ge(sem(s + "hid"), 4 * i + 2 * b + f // 4 + 1)
                        last = a.activation(hT[:, b, f * CAP:(f + 1) * CAP],
                                            bank[2 * b + f // 4][:, f % 4 * CAP:(f % 4 + 1) * CAP], ACT.Gelu,
                                            bias=b1s[:, b, f:f + 1], scale=GELU_IN)
                    last.then_inc(sem(s + "gelu"), 1)

        def switch_loop_vector(v, wave):
            s = "L3f_"
            v.wait_ge(in_attn[0], 16 * 3)

            def bias_in(i, b):
                v.wait_ge(in_exp[b], 16 * (i + wave + 2 - b))
                v.tensor_scalar(b1s[:, b, :], switch_w(b)[1], GELU_IN, None, ALU.mult).then_inc(sem(s + "b1s"), 1)

            def body(i, more):
                for b in range(2):
                    at = bass.ds(2 * i + b, 1)
                    y = YS[:, at, :].rearrange("p e n -> p (e n)")
                    yh = YH[:, at, :].rearrange("p e n -> p (e n)")
                    v.wait_ge(sem(s + "ys"), 2 * i + b + 1)
                    v.scalar_tensor_tensor(y, bank[6 + b][0:CAP, 0:D], 1.0 / GELU_IN,
                                           b2all[0:CAP, at, :].rearrange("p e n -> p (e n)"),
                                           ALU.mult, ALU.add).then_inc(sem(s + "ys_free"), 1)
                    v.wait_ge(sem(s + "ys_free"), 2 * i + b + 3)
                    v.tensor_copy(yh, y).then_inc(sem(s + "yh"), 1)
                    v.wait_ge(sem(s + "yh"), 2 * i + b + 1)
                    v.tensor_tensor(YL[0:CAP, at, :].rearrange("p e n -> p (e n)"), y, yh.bitcast(F32), ALU.subtract)\
                        .then_inc(sem(s + "yl"), 1)
                    if more:
                        bias_in(i + 1, b)

            for b in range(2):
                bias_in(0, b)
            rounds_of(v, E // 2, body)
            for g in range(NT):
                v.scalar_tensor_tensor(H[0:rows_of(g), g, :], X[0:rows_of(g), g, :], r(5)[0:rows_of(g), g:g + 1], H[0:rows_of(g), g, :],
                                       ALU.mult, ALU.add).then_inc(sem(s + "kept"), 1)
            v.wait_ge(sem(s + "kept"), NT)
            for g in range(NT):
                v.wait_ge(sem(s + "gathered"), g + 1)
                v.tensor_tensor(H[0:rows_of(g), g, :], bank[4 + g % 2][0:rows_of(g), 0:D], H[0:rows_of(g), g, :], ALU.add)\
                    .then_inc(sem(s + "final"), 1)

        patches = arena[:, 0:PC * TOK].rearrange("p (c n) -> p c n", c=PC)
        w_patch = arena[:, PC * TOK:PC * (TOK + D)].rearrange("p (c n) -> p c n", c=PC)

        def embed_tensor(pe):
            pe.wait_ge(in_patch, 16 * 4)
            for g in range(NT):
                if g >= 2:
                    pe.wait_ge(sem("embedded"), g - 1)
                dst = bank[g % 2][0:rows_of(g), 0:D]
                for k in range(PC):
                    pe.matmul(dst, patches[:, k, tile(g)], w_patch[:, k, :], start=(k == 0), stop=False)
                pe.matmul(dst, place[:, tile(g)], posA, start=False, stop=True).then_inc(sem("embed"), 1)

        def embed_vector(v):
            for g in range(NT):
                v.wait_ge(sem("embed"), g + 1)
                v.tensor_copy(H[0:rows_of(g), g, :], bank[g % 2][0:rows_of(g), 0:D]).then_inc(sem("embedded"), 1)
            v.wait_ge(sem("embedded"), NT)

        n_small = 5
        block = ctx.enter_context(nc.Block())

        @block.sync
        def _(sp):
            sp.dma_start(posA, t["pos"]).then_inc(in_patch, 16)
            sp.dma_start(place, t["place"]).then_inc(in_patch, 16)
            sp.dma_start(w_patch, t["w_patch"]).then_inc(in_patch, 16)
            sp.dma_start(patches, t["patches"]).then_inc(in_patch, 16)
            sp.dma_start(rows[:, :], t["rows"]).then_inc(in_small, 16)
            sp.dma_start(cols[:, :], t["cols"]).then_inc(in_small, 16)
            sp.dma_start(gates[:, :, :, :], t["gates"]).then_inc(in_small, 16)
            sp.dma_start(tab[:, :, :], t["tab"]).then_inc(in_small, 16)
            sp.dma_start(lam_in[0:GT], t["lam"]).then_inc(in_small, 16)
            sp.wait_ge(sem("proj_clear"), 1)
            for h in range(8):
                sp.dma_start(proj8[16 * h:16 * h + 16, h // 4, h % 4, :], t["proj"]).then_inc(in_proj, 16)
            sp.dma_start(wA[0][:, :], t["attn0"]).then_inc(in_attn[0], 16)
            sp.dma_start(wA[1][:, :], t["attn1"]).then_inc(in_attn[1], 16)
            sp.wait_ge(sem("L0_sim"), 4 * G)
            sp.dma_start(wE[0][:, 0:EXP1], t["mlp0"]).then_inc(in_exp[0], 16)
            sp.dma_start(wE[1][:, 0:EXP0], t["ffn0"][1]).then_inc(in_exp[1], 16)

            def stream(dram, size, used, per_expert, before=0, rounds=E // 2):
                with sp.Fori(1, rounds) as i:
                    for b in range(2):
                        sp.wait_ge(used, before + (2 * i + b - 1) * per_expert)
                        sp.dma_start(wE[b][:, 0:size], dram[bass.ds(2 * i + b, 1)].rearrange("e p n -> (e p) n"))\
                            .then_inc(in_exp[b], 16)

            sp.wait_ge(f_y, F1)
            sp.dma_start(wE[0][:, 0:EXP0], t["ffn0"][0]).then_inc(in_exp[0], 16)
            sp.dma_start(wA[0][:, :], t["attn2"]).then_inc(in_attn[0], 16)
            stream(t["ffn0"], EXP0, f_y, F0, UNITS_BEFORE["L0f_"])
            sp.wait_ge(sem("L1_score"), G)
            for b in range(2):
                sp.dma_start(wE[b][:, 0:EXP1], t["ffn1"][b]).then_inc(in_exp[b], 16)
            sp.wait_ge(sem("L1_added"), NT)
            sp.dma_start(wA[1][:, :], t["attn3"]).then_inc(in_attn[1], 16)
            stream(t["ffn1"], EXP1, f_y, F1, UNITS_BEFORE["L1f_"])
            sp.wait_ge(sem("L2_outer"), IMAGES)
            for b in range(2):
                sp.dma_start(wE[b][:, 0:EXP2], t["ffn2"][b]).then_inc(in_exp[b], 16)
            stream(t["ffn2"], EXP2, sem("L2f_y"), 2)
            sp.dma_start(b2all[0:CAP], t["b2"]).then_inc(in_attn[0], 16)
            written = 0
            for g in range(G):
                sp.wait_ge(sem("L3_o"), g + 1)
                for i in range(g * PER, min((g + 1) * PER, IMAGES)):
                    q = (i - g * PER) * SEQ
                    sp.dma_start(by_head[i].rearrange("h q d -> q h d"),
                                 O[q:q + SEQ, g, :].rearrange("p (h d) -> p h d", h=16))\
                        .then_inc(sem("L3_heads_out"), 16)
                    written += 16
                for j in range(NT):
                    if groups_for(j) == g + 1:
                        sp.wait_ge(sem("L3_heads_out"), written)
                        if j:
                            sp.wait_ge(sem("L3_regrouped"), 16 * j)
                        sp.dma_start(X[0:rows_of(j), j, :], by_token[tile(j), :])\
                            .then_inc(sem("L3_regrouped"), 16)
            CUT = C * F1 * P + F1

            def first_w(e, b):
                sp.dma_start(wE[b][:, 0:CUT], t["ffn3"][bass.ds(e, 1), :, 0:CUT].rearrange("e p n -> (e p) n"))\
                    .then_inc(in_exp[b], 16)

            def second_w(e, b):
                sp.dma_start(wE[b][:, CUT:EXP1], t["ffn3"][bass.ds(e, 1), :, CUT:EXP1].rearrange("e p n -> (e p) n"))\
                    .then_inc(in_out[b], 16)

            for b in range(2):
                first_w(b, b)
            for b in range(2):
                second_w(b, b)
            def next_first(e, b):
                sp.wait_ge(sem("L3f_hid"), 2 * (e - 1))
                sp.wait_ge(sem("L3f_b1s"), e - 1)
                first_w(e, b)

            def body(i, more):
                for b in range(2):
                    if b == 0 or more:
                        next_first(2 * i + b + 3, 1 - b)
                    sp.wait_ge(sem("L3f_ys"), 2 * i + b + 1)
                    second_w(2 * i + b + 2, b)

            next_first(2, 0)
            rounds_of(sp, E // 2 - 1, body)
            sp.wait_ge(sem("finished"), 1)
            full = TOK // P
            sp.dma_start(t["out"][0:full * P, :].rearrange("(g p) d -> p g d", p=P), H[:, 0:full, :])\
                .then_inc(stored, 16)
            sp.dma_start(t["out"][full * P:TOK, :], H[0:TOK - full * P, full, :]).then_inc(stored, 16)
            sp.wait_ge(stored, 32)

        @block.gpsimd
        def _(p):
            def L(ins):
                pchain.link(p, ins)

            def keep(x, pattern, base, mult, fill, op=ALU.is_ge):
                L(p.affine_select(out=x, in_=x, pattern=pattern, compare_op=op, fill=fill, base=base,
                                  channel_multiplier=mult))

            def same_block(x, n, size, value_in, fill):
                inner = x.shape[1] // n
                xv = x if inner == 1 else x.rearrange("p (b n) -> p b n", b=n)
                pat = [[-size, n]] if inner == 1 else [[-size, n], [0, inner]]
                keep(xv, pat, 0, 1, fill)
                pat = [[size, n]] if inner == 1 else [[size, n], [0, inner]]
                keep(xv, pat, size - 1, -1, fill)

            p.memset(hT[:, 2:4, 0:4 * P], 0.0).then_inc(sem("proj_clear"), 1)
            L(p.memset(eps[:, 0:1], EPS))
            L(p.memset(mv[:, :, :], 1.0))
            L(p.memset(ident[:, :], 0.0))
            keep(ident[:, :], [[-1, P]], 0, 1, 1.0, ALU.not_equal)
            L(p.memset(ones[:, :], 1.0))
            L(p.memset(tri[:, :], 1.0))
            keep(tri[:, :], [[1, P]], 0, -1, 0.0)
            L(p.memset(same[:, :], 1.0))
            same_block(same[:, :], PER, SEQ, 1.0, 0.0)
            L(p.memset(far[:, :], 0.0))
            same_block(far[:, :], PER, SEQ, 0.0, NEG)
            L(p.memset(causal[:, :], 0.0))
            same_block(causal[:, :], PER, SEQ, 0.0, NEG)
            keep(causal[:, :], [[-1, GT]], 0, 1, NEG)
            L(p.memset(valid[:, :], 1.0))
            keep(valid[:, :], [[0, 1]], TOK - (NT - 1) * P - 1, -1, 0.0)
            L(p.memset(head16[:, :], 1.0))
            same_block(head16[:, :], 8, 16, 1.0, 0.0)
            for n in range(2):
                h = head16[:, n:8:2]
                L(p.tensor_tensor(parity[:, n:n + 1], h[:, 0:1], h[:, 1:2], ALU.add))
                L(p.tensor_tensor(parity[:, n:n + 1], parity[:, n:n + 1], h[:, 2:3], ALU.add))
                L(p.tensor_tensor(parity[:, n:n + 1], parity[:, n:n + 1], h[:, 3:4], ALU.add))
            L(p.memset(block8[:, :], 1.0))
            same_block(block8[:, :], 16, 8, 1.0, 0.0)
            L(p.iota(i32[:, 0:E], [[1, E]], base=0, channel_multiplier=0))
            L(p.tensor_copy(iotaE[:, :], i32[:, 0:E]))
            L(p.iota(i32[:, 0:E], [[-1, E]], base=E, channel_multiplier=0))
            L(p.tensor_copy(revE[:, :], i32[:, 0:E]))
            L(p.iota(i32[:, 0:E], [[CAP, E]], base=0, channel_multiplier=1))
            L(p.tensor_copy(slot_own[:, :], i32[:, 0:E]))
            L(p.iota(i32[:, :], [[1, TOK]], base=0, channel_multiplier=0))
            L(p.tensor_copy(slot_id[:, :], i32[:, :]))
            L(p.memset(eps[:, 1:2], 1.5707963))
            p.memset(XT[:, :, TOK:SLOTS], 0.0).then_inc(consts, 1)
        @block.tensor
        def _(pe):
            embed_tensor(pe)
            pe.wait_ge(consts, 1)
            s = "L0_"
            turn_tensor(pe, s, X, normed_of(s))
            qk_tensor(pe, s, 0, (0, 1))
            v_tensor(pe, s, 0, row("L0_bv"))
            pe.wait_ge(sem("proj_scaled"), 1)
            pe.wait_ge(sem(s + "qk_out"), 8)
            for n in range(LEAD):
                phase_tensor(pe, *divmod(n, 4))
            for n in range(4 * G):
                if n + LEAD < 4 * G:
                    phase_tensor(pe, *divmod(n + LEAD, 4))
                similar_tensor(pe, *divmod(n, 4))
                if n:
                    values_tensor(pe, *divmod(n - 1, 4))
            values_tensor(pe, G - 1, 3)
            turn_tensor(pe, "L0o_", O, lambda g: (sem("L0_o"), g + 1))
            proj_tensor(pe, "L0a_", 0, lambda g: (xt_done, xt_count("L0o_", groups_for(g))), row("L0_bo"))
            s = "L0m_"
            turn_tensor(pe, s, X, normed_of(s))
            pe.wait_ge(xt_done, xt_all(s))
            for g in range(NT):
                pe.matmul(y_bank(g), ones[0:1, 0:rows_of(g)], row("L0_b2"), start=True, stop=True)\
                    .then_inc(sem(s + "bias"), 1)
            ffn_tensor(pe, s, "relu", F1, [0], 1)
            s = "L0f_"
            turn_tensor(pe, s, X, normed_of(s))
            gate_tensor(pe, s, 0, None)
            ffn_tensor(pe, s, "silu", F0, [0, 1], E // 2)
            s = "L1_"
            turn_tensor(pe, s, X, normed_of(s))
            qk_tensor(pe, s, 1, (0, 1))
            v_tensor(pe, s, 1, row("L1_bv"))
            for g in range(2):
                score_tensor(pe, s, g, 8)
            for g in range(G):
                if g + 2 < G:
                    score_tensor(pe, s, g + 2, 8)
                pv_tensor(pe, s, g, 8, 32, 4)
            turn_tensor(pe, "L1o_", X, normed_of("L1o_"))
            proj_tensor(pe, s, 1, lambda g: (xt_done, xt_count("L1o_", groups_for(g))), row("L1_bo"))
            s = "L1f_"
            turn_tensor(pe, s, X, normed_of(s))
            gate_tensor(pe, s, 1, None)
            ffn_tensor(pe, s, "relu", F1, [0, 1], E // 2)
            pe.wait_ge(f_y_added, 2 * (E + 1) * NT)
            bias_tensor(pe, s, 0)
            s = "L2_"
            turn_tensor(pe, s, X, normed_of(s))
            qk_tensor(pe, s, 2, (0,))
            linear_tensor(pe)
            proj_tensor(pe, s, 2, lambda g: (sem("L2_image"), IMAGES), row("L2_bo"))
            s = "L2f_"
            turn_tensor(pe, s, X, normed_of(s))
            gate_tensor(pe, s, 2, rows[0:1, 7 * D:7 * D + E])
            bias_tensor(pe, s, 1)
            deep_tensor(pe, s, 8)
            s = "L3_"
            turn_tensor(pe, s, X, normed_of(s))
            qk_tensor(pe, s, 3, (0, 1))
            v_tensor(pe, s, 3, None)
            for g in range(2):
                score_tensor(pe, s, g, 16)
            for g in range(G):
                if g + 2 < G:
                    score_tensor(pe, s, g + 2, 16)
                pv_tensor(pe, s, g, 16, 16, 16)
            turn_tensor(pe, "L3o_", X, lambda g: (sem("L3_regrouped"), 16 * (g + 1)))
            proj_tensor(pe, s, 3, lambda g: (xt_done, xt_count("L3o_", g + 1)), row("L3_bo"))
            s = "L3f_"
            turn_tensor(pe, s, X, normed_of(s))
            gate_tensor(pe, s, 3, rows[0:1, 7 * D + E:7 * D + 2 * E])
            switch_tensor(pe, 12)

        @block.vector
        def _(v):
            embed_vector(v)
            v.wait_ge(consts, 1)
            v.wait_ge(in_proj, 16 * 8)
            v.tensor_scalar(hT[:, 2:4, 0:4 * P], hT[:, 2:4, 0:4 * P], 0.25 / (2 * 3.141592653589793), None, ALU.mult)\
                .then_inc(sem("proj_scaled"), 1)
            norm_vector(v, "L0i_", H, R0)
            v.wait_ge(normed, NT)
            s = "L0_"
            norm_vector(v, s, R0, X)
            v_vector(v, s, 16, 16)
            for n in range(LEAD):
                phase_vector(v, *divmod(n, 4))
            for n in range(4 * G):
                if n + LEAD < 4 * G:
                    phase_vector(v, *divmod(n + LEAD, 4))
                similar_vector(v, *divmod(n, 4))
                if n % 4 == 0 and n:
                    values_out_vector(v, n // 4 - 1)
            values_out_vector(v, G - 1)
            proj_vector(v, "L0a_", R0, R0)
            s = "L0m_"
            norm_vector(v, s, R0, X)
            split_vector(v, s)
            bias_vector(v, s, R0, f_y_added)
            ffn_vector(v, s, "relu", F1, [0], 1)
            v.wait_ge(f_y_added, 2 * NT)
            for g in range(NT):
                n = rows_of(g)
                last = v.tensor_tensor(H[0:n, g, :], H[0:n, g, :], R0[0:n, g, :], ALU.add)
            vchain.link(v, last)
            s = "L0f_"
            norm_vector(v, s, H, X)
            split_vector(v, s)
            route0_vector(v)
            ffn_vector(v, s, "silu", F0, [0, 1], E // 2)
            v.wait_ge(f_y_added, (E + 2) * NT)
            s = "L1_"
            for j in range(2):
                last = v.tensor_tensor_reduce(lam_in[0:GT, 2 * j, :], lam_in[0:GT, 2 * j, :],
                                              lam_in[0:GT, 2 * j + 1, :], 1.0, 0.0, ALU.mult, ALU.add,
                                              lam[0:GT, j:j + 1])
            last.then_inc(sem(s + "lam"), 1)
            v.wait_ge(sem(s + "lam_exp"), 1)
            vchain.link(v, v.tensor_tensor(lam[0:GT, 4:5], lam[0:GT, 3:4], lam[0:GT, 2:3], ALU.subtract))
            vchain.link(v, v.tensor_scalar(lam[0:GT, 5:6], lam[0:GT, 4:5], -0.8, None, ALU.add))
            norm_vector(v, s, H, X)
            v_ones(v, s, 4, 32)
            for g in range(G):
                v.wait_ge(sem(s + "v"), g + 1)
                b = bank[6 + g % 2]
                vchain.link(v, v.tensor_scalar(O[0:GT, g, 0:P], b[0:GT, P:D], lam[0:GT, 5:6], None, ALU.mult))
                v.tensor_tensor(V[0:GT, g, 0:4 * 33].rearrange("p (h d) -> p h d", h=4)[:, :, 0:32],
                                b[0:GT, 0:P].rearrange("p (h d) -> p h d", h=4),
                                O[0:GT, g, 0:P].rearrange("p (h d) -> p h d", h=4), ALU.add)\
                    .then_inc(sem(s + "v_out"), 1)
            for g in range(2):
                score_vector(v, s, g, 8, far)
            for g in range(G):
                if g + 2 < G:
                    score_vector(v, s, g + 2, 8, far)
                out_vector(v, s, g, 8, 32)
            v.wait_ge(sem(s + "o"), G)
            norm_vector(v, "L1o_", O, X)
            proj_vector(v, s, H, H)
            s = "L1f_"
            norm_vector(v, s, H, X)
            split_vector(v, s)
            route1_vector(v)
            ffn_vector(v, s, "relu", F1, [0, 1], E // 2)
            v.wait_ge(f_y_added, 2 * (E + 1) * NT)
            bias_vector(v, s, H, sem(s + "biased"))
            v.wait_ge(sem(s + "biased"), NT)
            s = "L2_"
            norm_vector(v, s, H, X)
            linear_vector(v)
            proj_vector(v, s, H, H)
            s = "L2f_"
            norm_vector(v, s, H, X)
            free_banks(v, s, 0, 2)
            free_banks(v, s, 1, 2)
            route2_vector(v)
            bias_vector(v, s, H, sem(s + "y_added"))
            deep_vector(v, s)
            v.wait_ge(sem(s + "y_added"), (E + 1) * NT)
            s = "L3_"
            norm_vector(v, s, H, X)
            v_ones(v, s, 16, 16)
            v_vector(v, s, 16, 16)
            for g in range(2):
                score_vector(v, s, g, 16, causal)
            for g in range(G):
                if g + 2 < G:
                    score_vector(v, s, g + 2, 16, causal)
                out_vector(v, s, g, 16, 16)
            proj_vector(v, s, H, H)
            s = "L3f_"
            norm_vector(v, s, H, X)
            v.sem_inc(sem(s + "gelu"), 2)
            v.sem_inc(sem(s + "ys_free"), 2)
            switch_vector(v)
            switch_loop_vector(v, 12)
            v.wait_ge(sem(s + "final"), NT)
            v.memset(r_mx[0:1, 0, 0:1], 0.0).then_inc(sem("finished"), 1)

        @block.scalar
        def _(a):
            a.wait_ge(consts, 1)
            a.wait_ge(in_small, 16 * n_small)
            norm_scalar(a, "L0i_")
            s = "L0_"
            norm_scalar(a, s)
            turn_scalar(a, s, lambda c: col("L0_g1", c), lambda c: col("L0_n1", c))
            qk_scalar(a, s, (0, 1), ACT.Identity, lambda w, c: col(("L0_bq", "L0_bk")[w], c))
            for n in range(4 * G):
                fourier_scalar(a, *divmod(n, 4))
            turn_scalar(a, "L0o_")
            s = "L0m_"
            norm_scalar(a, s)
            turn_scalar(a, s, lambda c: col("L0_g2", c), lambda c: col("L0_n2", c), split=True)
            ffn_scalar(a, s, "relu", F1, -1, [0], 1)
            s = "L0f_"
            norm_scalar(a, s)
            turn_scalar(a, s, split=True)
            route0_scalar(a)
            ffn_scalar(a, s, "silu", F0, 0, [0, 1], E // 2)
            s = "L1_"
            a.wait_ge(sem(s + "lam"), 1)
            a.activation(lam[0:GT, 2:4], lam[0:GT, 0:2], ACT.Exp).then_inc(sem(s + "lam_exp"), 1)
            norm_scalar(a, s)
            turn_scalar(a, s)
            qk_scalar(a, s, (0, 1), ACT.Identity, lambda w, c: col(("L1_bq", "L1_bk")[w], c))
            for g in range(G):
                soft_scalar(a, s, g, 8, 1.0 / 32 ** 0.5)
            norm_scalar(a, "L1o_")
            last = a.activation(aff[:, :], cols[:, 2 * COL.index("L1_g"):2 * COL.index("L1_g") + 4], ACT.Copy,
                                scale=0.2)
            last.then_inc(sem("aff"), 1)
            a.wait_ge(sem("aff"), 1)
            turn_scalar(a, "L1o_", lambda c: aff[:, c:c + 1], lambda c: aff[:, 2 + c:3 + c])
            s = "L1f_"
            norm_scalar(a, s)
            turn_scalar(a, s, split=True)
            exp_on_scalar(a, s, 1, R(2), R(2))
            ffn_scalar(a, s, "relu", F1, 4, [0, 1], E // 2)
            bias_scalar(a, s)
            s = "L2_"
            norm_scalar(a, s)
            turn_scalar(a, s)
            qk_scalar(a, s, (0,), ACT.Relu, lambda w, c: None)
            linear_scalar(a)
            s = "L2f_"
            norm_scalar(a, s)
            turn_scalar(a, s)
            exp_on_scalar(a, s, 1, R(2), R(2))
            bias_scalar(a, s)
            deep_scalar(a, s)
            s = "L3_"
            norm_scalar(a, s)
            turn_scalar(a, s)
            qk_scalar(a, s, (0, 1), ACT.Identity, lambda w, c: None)
            for g in range(G):
                soft_scalar(a, s, g, 16, 0.25)
            turn_scalar(a, "L3o_")
            s = "L3f_"
            norm_scalar(a, s)
            turn_scalar(a, s)
            switch_scalar(a)


def _layout(x):
    import numpy as np

    def chunked(w):
        k, n = w.shape
        return w.reshape(k // P, P, n).transpose(1, 0, 2).reshape(P, -1)

    side = 6
    pt = x["x"].reshape(IMAGES, 3, side, 16, side, 16).transpose(1, 3, 5, 0, 2, 4).reshape(PD, IMAGES, PATCHES)
    full = np.zeros((PD, IMAGES, SEQ), pt.dtype)
    full[:, :, 2:] = pt
    t = {"patches": full.reshape(PC, P, TOK).transpose(1, 0, 2),
         "w_patch": x["L0_tok_W"].T.reshape(PC, P, D).transpose(1, 0, 2)}
    pos = np.zeros((2, SEQ, D), pt.dtype)
    pos[0, 0] = x["cls_tok"][0, 0]
    pos[0, 1:] = x["L0_tok_pos_embed"][0]
    pos[1, 1] = x["L0_tok_cls_token"][0, 0]
    pos[1, 2:] = x["L0_tok_b"]
    t["pos"] = pos.reshape(2 * SEQ, D)
    t["place"] = np.tile(np.eye(SEQ, dtype=pt.dtype), (2, IMAGES))
    gb = np.zeros(D, pt.dtype)
    gb[:E], gb[E:2 * E] = x["L2_ffn_gate_b"], x["L3_ffn_b_sw"]
    t["rows"] = np.concatenate([x["L0_attn_bv"], x["L0_attn_bo"], x["L0_attn_b2"], x["L1_attn_bv"], x["L1_attn_bo"],
                                x["L2_attn_proj_bias"], x["L3_attn_bo"], gb])[None]
    names = ["L0_attn_bq", "L0_attn_bk", "L0_attn_ln1_g", "L0_attn_ln1_b", "L0_attn_ln2_g", "L0_attn_ln2_b",
             "L1_attn_bq", "L1_attn_bk", "L1_attn_ln_w", "L1_attn_ln_b"]
    t["cols"] = np.concatenate([x[n].reshape(C, P).T for n in names], 1)
    t["gates"] = np.stack([w.reshape(C, P, E).transpose(1, 0, 2) for w in (
        x["L0_ffn_gate_w"].T, x["L1_ffn_W_gate"], x["L2_ffn_gate_w"].T, x["L3_ffn_W_sw"])], 1)
    t["tab"] = np.stack([x["L1_ffn_b2"], x["L2_ffn_b3"]], 1)
    t["lam"] = np.tile(np.stack([x["L1_attn_lambda_" + n] for n in ("q1", "k1", "q2", "k2")])[None], (GT, 1, 1))
    t["b2"] = np.tile(x["L3_ffn_b2"][None], (CAP, 1, 1))
    t["proj"] = x["L0_attn_proj_mat"]
    t["attn0"] = np.concatenate([chunked(x["L0_attn_w" + n]) for n in "qkvo"], 1)
    t["attn1"] = np.concatenate([chunked(x["L1_attn_W" + n]) for n in "qkvo"], 1)
    qkv = x["L2_attn_qkv_weight"].T
    t["attn2"] = np.concatenate([chunked(qkv[:, :D]), chunked(qkv[:, D:]), chunked(x["L2_attn_proj_weight"].T)], 1)
    t["attn3"] = np.concatenate([chunked(x["L3_attn_W" + n]) for n in "qkvo"], 1)

    def expert(*parts):
        return np.concatenate(parts, 1)

    def bias(b):
        return b.reshape(-1, P).T

    t["mlp0"] = expert(chunked(x["L0_attn_w1"]), chunked(x["L0_attn_w2"]), bias(x["L0_attn_b1"]))
    t["ffn0"] = np.stack([expert(chunked(x["L0_ffn_w1"][e].T), chunked(x["L0_ffn_w3"][e].T),
                                 chunked(x["L0_ffn_w2"][e].T)) for e in range(E)])
    n = "L1_ffn_"
    t["ffn1"] = np.stack([expert(chunked(x[n + "W1"][e]), chunked(x[n + "W2"][e]), bias(x[n + "b1"][e]))
                          for e in range(E)])
    n = "L3_ffn_"
    t["ffn3"] = np.stack([expert(chunked(x[n + "W1"][e]), bias(x[n + "b1"][e]), chunked(x[n + "W2"][e]))
                          for e in range(E)])
    n = "L2_ffn_"
    t["ffn2"] = np.stack([expert(chunked(x[n + "w1"][e]), chunked(x[n + "w2"][e]), chunked(x[n + "w3"][e]),
                                 bias(x[n + "b1"][e]), bias(x[n + "b2"][e])) for e in range(E)])
    return {k: np.ascontiguousarray(v) for k, v in t.items()}


def kernel(**inputs):
    import numpy as np
    import concourse.bacc as bacc
    from concourse.bass_utils import run_bass_kernel_spmd

    nc = bacc.Bacc("TRN2", target_bir_lowering=False, num_devices=1)
    arrays = _layout({k: np.asarray(v) for k, v in inputs.items()})
    t = {k: nc.dram_tensor(k + "_dram", v.shape, mybir.dt.from_np(v.dtype), kind="ExternalInput").ap()
         for k, v in arrays.items()}
    t["out"] = nc.dram_tensor("out_dram", (TOK, D), F32, kind="ExternalOutput").ap()
    build(nc, t)
    r = run_bass_kernel_spmd(nc, [{k + "_dram": v for k, v in arrays.items()}], core_ids=[0])
    return r.results[0]["out_dram"].reshape(IMAGES, SEQ, D)
```

```python
from contextlib import ExitStack

import concourse.bass as bass
from concourse import mybir

F32 = mybir.dt.float32
F32R = mybir.dt.float32r
ALU = mybir.AluOpType
ACT = mybir.ActivationFunctionType
AX = mybir.AxisListType.X

P = 128
IMAGES, PATCHES, D = 16, 36, 256
SEQ = PATCHES + 2
TOK = IMAGES * SEQ
PER = 3
GT = PER * SEQ
G = -(-IMAGES // PER)
NT = -(-TOK // P)
SLOTS = G * GT
C = D // P
HT = TOK // 2
FIRST_HALF = -(-HT // P)
PD = 768
PC = PD // P
E = 8
CAP = TOK // E
EPS = 1e-5
NEG = -1e30
MAGIC = 12582912.0
TWO_PI = 6.2831850
F0, F1 = 7, 8
ROW = ["L0_bv", "L0_bo", "L0_b2", "L1_bv", "L1_bo", "L2_bo", "L3_bo", "gate_b"]
COL = ["L0_bq", "L0_bk", "L0_g1", "L0_n1", "L0_g2", "L0_n2", "L1_bq", "L1_bk", "L1_g", "L1_n"]


def build(nc, t):
    ctx = ExitStack()
    with ctx:
        def sb(name, shape, dt=F32):
            return ctx.enter_context(nc.sbuf_tensor(name, shape, dt))

        sems = {}

        def sem(name):
            if name not in sems:
                sems[name] = ctx.enter_context(nc.semaphore(name))
            return sems[name]

        bank = [ctx.enter_context(nc.psum_tensor(f"bank{i}", [P, 512], F32)) for i in range(8)]

        H = sb("H", [P, NT, D])
        RO = sb("RO", [P, 2, G, D])
        R0 = RO[:, 0]
        X = sb("X", [P, G, D])
        O = RO[:, 1]
        feat = sb("feat", [P, 3, C, SLOTS])
        XT = feat[:, 0]
        QT = feat[:, 1]
        KT = feat[:, 2]
        parts = sb("parts", [P, 8 * TOK + 6 * 4 * P], F32R)

        def part(at, n, form, **sizes):
            return parts[:, at:at + n].rearrange(form, **sizes)

        XH, XL = [part(i * 2 * TOK, 2 * TOK, "p (c n) -> p c n", c=C) for i in (0, 1)]
        HH, HL = [part(i * 2 * TOK, 2 * TOK, "p (k n) -> p k n", k=2) for i in (2, 3)]
        UH, UL = [part(8 * TOK + i * 8 * P, 8 * P, "p (k c n) -> p k c n", k=2, c=4) for i in (0, 1)]
        DH, DL = [part(8 * TOK + (4 + i) * 4 * P, 4 * P, "p (k n) -> p k n", k=2) for i in (0, 1)]
        parts2 = sb("parts2", [P, 4 * TOK], F32R)
        H2H, H2L = [parts2[:, i * 2 * TOK:(i + 1) * 2 * TOK].rearrange("p (k n) -> p k n", k=2) for i in (0, 1)]
        V = sb("V", [P, G, 16 * 17])
        stats = sb("stats", [P, G, 6])
        mv = sb("mv", [P, G, 2])
        sd = sb("sd", [P, G])
        own = sb("own", [P, 2])
        warm = sb("warm", [P, 11])
        rs = sb("rs", [P, G])
        wA = [sb(f"wA{i}", [P, 4 * C * D]) for i in range(2)]
        EXP0 = C * F0 * P * 2 + F0 * D
        EXP1 = C * F1 * P + F1 * D + F1
        EXP2 = 3 * C * D + 4
        arena = sb("arena", [P, 2 * 8 * SLOTS])
        wD = [arena[:, i * EXP2:(i + 1) * EXP2] for i in range(4)]
        wE = [arena[:, i * EXP0:(i + 1) * EXP0] for i in range(2)]
        arena2 = sb("arena2", [P, 3 * 16 * GT])
        MLP = 2
        wE.append(arena2[:, 0:EXP1])
        hT = sb("hT", [P, 4, TOK])
        ident = sb("ident", [P, P])
        ones = sb("ones", [P, P])
        valid = sb("valid", [P, 1])
        tri = sb("tri", [P, P])
        same = sb("same", [P, GT])
        far = sb("far", [P, GT])
        causal = sb("causal", [P, GT])
        parity = sb("parity", [P, 2])
        head16 = sb("head16", [P, 8])
        block8 = sb("block8", [P, P])
        iotaE = sb("iotaE", [P, E])
        revE = sb("revE", [P, E])
        slot_id = sb("slot_id", [P, TOK])
        slot_own = sb("slot_own", [P, E])
        i32 = hT[:, 0, :].bitcast(mybir.dt.int32)
        rows = sb("rows", [1, len(ROW) * D])
        cols = sb("cols", [P, len(COL) * C])
        gates = sb("gates", [P, 4, C, E])
        tab = sb("tab", [E, 2, D])
        lam_in = sb("lam_in", [P, 4, 32])
        lam = sb("lam", [P, 8])
        proj8 = hT[:, 2:4, 0:4 * P].rearrange("p a (h n) -> p a h n", h=4)
        posA = arena[0:2 * SEQ, PC * (TOK + D):PC * (TOK + D) + D]
        place = arena[0:2 * SEQ, PC * (TOK + D) + D:PC * (TOK + D) + D + TOK]
        score = sb("score", [P, NT, E])
        rt = sb("rt", [P, 12, NT, E])
        r1 = sb("r1", [P, 8, NT])
        gate = sb("gate", [P, NT, E])
        gcur = sb("gcur", [P, 2, NT])
        b1s = sb("b1s", [P, 2, F1])
        b2all = wA[0][:, :].rearrange("p (e n) -> p e n", e=E)
        r_mx = sb("r_mx", [P, 4, 16])
        eps = sb("eps", [P, 2])
        aff = sb("aff", [P, 4])
        ksum = arena2[:, 2 * C * D:2 * C * D + 8 * SEQ].rearrange("p (a i n) -> p a i n", a=2, i=2)

        def row(name):
            i = ROW.index(name)
            return rows[0:1, i * D:(i + 1) * D]

        def col(name, c):
            i = COL.index(name)
            return cols[:, i * C + c:i * C + c + 1]

        def a_w(layer, which):
            v = wA[layer % 2][:, which * C * D:(which + 1) * C * D]
            return v.rearrange("p (c n) -> p c n", c=C)

        def width(g):
            return min(GT, TOK - g * GT)

        def tok(g):
            return slice(g * GT, g * GT + width(g))

        def rows_of(g):
            return min(P, TOK - g * P)

        def tile(g):
            return slice(g * P, g * P + rows_of(g))

        def groups_for(g):
            return -(-(g * P + rows_of(g)) // GT)

        GROUPED = ["L1o_", "L0o_"]

        class Chain:

            def __init__(self, name):
                self.s, self.n = sem(name), 0

            def link(self, eng, ins):
                self.n += 1
                ins.then_inc(self.s, 1)
                eng.wait_ge(self.s, self.n)

        vchain = Chain("vector_order")
        pchain = Chain("pool_order")
        heads_dram = nc.dram_tensor("heads_by_image", (IMAGES * 16 * SEQ * 16,), F32, kind="Internal").ap()
        by_head = heads_dram.rearrange("(i h q d) -> i h q d", i=IMAGES, h=16, q=SEQ)
        by_token = heads_dram.rearrange("(n d) -> n d", d=D)
        in_small, in_patch, in_proj = sem("in_small"), sem("in_patch"), sem("in_proj")
        in_attn = [sem("in_attn0"), sem("in_attn1")]
        in_exp = [sem("in_exp0"), sem("in_exp1")]
        in_mlp = sem("in_mlp")
        in_deep = [sem(f"in_deep{j}") for j in range(4)]
        in_out = [sem("in_out0"), sem("in_out1")]
        consts = sem("consts")
        stored = sem("stored")

        NORMS = ["L0i_", "L0_", "L0m_", "L0f_", "L1_", "L1o_", "L1f_", "L2_", "L2f_", "L3_", "L3f_"]
        TURNS = ["L0_", "L0o_", "L0m_", "L0f_", "L1_", "L1o_", "L1f_", "L2_", "L2f_", "L3_", "L3o_", "L3f_"]
        stats_done, var_done, sd_done = sem("stats_done"), sem("var_done"), sem("sd_done")
        turned, xt_done = sem("turned"), sem("xt_done")
        norm_nth = NORMS.index

        def cuts(s):
            return [(width(g), g * GT) for g in range(G)] if s in GROUPED else [(rows_of(g), g * P) for g in range(NT)]

        def norm_count(s, n):
            return sum(len(cuts(x)) for x in NORMS[:norm_nth(s)]) + n

        normed = sem("normed")
        SPLITS = ["L0m_", "L0f_", "L1f_", "L2f_"]
        xl_done = sem("xl_done")

        def normed_of(s):
            return lambda g: (normed, norm_count(s, g + 1))

        def xt_count(s, n):
            return sum(len(cuts(x)) for x in TURNS[:TURNS.index(s)]) + n

        def xt_all(s):
            return xt_count(s, len(cuts(s)))

        def stats_vector(v, src, g):
            n = rows_of(g)
            v.bn_stats(stats[0:n, g, :], src[0:n, g, :]).then_inc(stats_done, 1)

        def norm_vector(v, s, src, dst, taken=False, then=None):
            m = len(cuts(s))
            if not taken:
                for g, (n, _) in enumerate(cuts(s)):
                    v.bn_stats(stats[0:n, g, :], src[0:n, g, :]).then_inc(stats_done, 1)
            for g, (n, _) in enumerate(cuts(s)):
                v.wait_ge(stats_done, norm_count(s, g + 1))
                last = v.bn_aggr(mv[0:n, g, :], stats[0:n, g, :])
            last.then_inc(var_done, 1)
            v.wait_ge(sd_done, norm_nth(s) + 1)
            vchain.link(v, v.reciprocal(rs[:, 0:m], sd[:, 0:m]))
            for g, (n, _) in enumerate(cuts(s)):
                v.tensor_scalar(dst[0:n, g, :], src[0:n, g, :], mv[0:n, g, 0:1], rs[0:n, g:g + 1],
                                ALU.subtract, ALU.mult).then_inc(normed, 1)
                if then and g:
                    v.wait_ge(normed, norm_count(s, g))
                    then(g - 1)
            if then:
                v.wait_ge(normed, norm_count(s, m))
                then(m - 1)

        def norm_scalar(a, s):
            m = len(cuts(s))
            a.activation(warm[:, norm_nth(s):norm_nth(s) + 1], eps[:, 0:1], ACT.Sqrt)
            a.wait_ge(var_done, norm_nth(s) + 1)
            a.activation(sd[:, 0:m], mv[:, 0:m, 1], ACT.Sqrt, bias=eps[:, 0:1]).then_inc(sd_done, 1)

        def turn_bank(s, g):
            return bank[(6 if s in SPLITS else 0) + g % 2]

        def turn_tensor(pe, s, src, ready):
            for g, (n, _) in enumerate(cuts(s)):
                pe.wait_ge(*ready(g))
                if g >= 2:
                    pe.wait_ge(xt_done, xt_count(s, g - 1))
                for c in range(C):
                    last = pe.transpose(turn_bank(s, g)[:, c * P:c * P + n],
                                        src[0:n, g, c * P:(c + 1) * P], ident[0:n, 0:n])
                last.then_inc(turned, 1)

        def turn_scalar(a, s, scale=None, shift=None):
            for g, (n, at) in enumerate(cuts(s)):
                a.wait_ge(turned, xt_count(s, g + 1))
                src = turn_bank(s, g)[:, 0:C * P].rearrange("p (c n) -> p c n", c=C)[:, :, 0:n]
                if scale is None:
                    last = a.activation(XT[:, :, at:at + n], src, ACT.Copy)
                else:
                    for c in range(C):
                        last = a.activation(XT[:, c, at:at + n], src[:, c, :], ACT.Identity, bias=shift(c),
                                            scale=scale(c))
                last.then_inc(xt_done, 1)

        def split_vector(v, s):
            for g in range(NT):
                x = tile(g)
                v.wait_ge(xt_done, xt_count(s, g + 1))
                vchain.link(v, v.tensor_copy(XH[:, :, x], XT[:, :, x]))
                v.tensor_tensor(XL[:, :, x], XT[:, :, x], XH[:, :, x].bitcast(F32), ALU.subtract)\
                    .then_inc(xl_done, 1)

        def qk_tensor(pe, s, layer, which):
            pe.wait_ge(in_attn[layer % 2], 16 * (layer // 2 + 1))
            pe.wait_ge(xt_done, xt_all(s))
            u = 0
            for w in which:
                for c in range(C):
                    for half in range(2):
                        if u >= 4:
                            pe.wait_ge(sem(s + "qk_out"), u - 3)
                        for k in range(C):
                            last = pe.matmul(bank[2 + u % 4][:, 0:HT], a_w(layer, w)[:, k, c * P:(c + 1) * P],
                                             XT[:, k, half * HT:(half + 1) * HT], start=(k == 0), stop=(k == C - 1))
                        last.then_inc(sem(s + "qk"), 1)
                        u += 1

        def qk_scalar(a, s, which, func, bias):
            u = 0
            for w in which:
                for c in range(C):
                    for half in range(2):
                        a.wait_ge(sem(s + "qk"), u + 1)
                        dst = (QT, KT)[w][:, c, half * HT:(half + 1) * HT]
                        b = bias(w, c)
                        if s == "L3_" and w == 1:
                            for n in range(2):
                                last = a.activation(KM[:, c, n, half * HT:(half + 1) * HT], bank[2 + u % 4][:, 0:HT],
                                                    func, scale=parity[:, n:n + 1])
                            last.then_inc(sem(s + "qk_out"), 1)
                        elif b is None:
                            a.activation(dst, bank[2 + u % 4][:, 0:HT], func).then_inc(sem(s + "qk_out"), 1)
                        else:
                            a.activation(dst, bank[2 + u % 4][:, 0:HT], func, bias=b).then_inc(sem(s + "qk_out"), 1)
                        u += 1

        def v_tensor(pe, s, layer, bias):
            for g in range(G):
                if g >= 2:
                    pe.wait_ge(sem(s + "v_out"), g - 1)
                for k in range(C):
                    last = pe.matmul(bank[6 + g % 2][0:width(g), 0:D], XT[:, k, tok(g)], a_w(layer, 2)[:, k, :],
                                     start=(k == 0), stop=(bias is None and k == C - 1))
                if bias is not None:
                    last = pe.matmul(bank[6 + g % 2][0:width(g), 0:D], ones[0:1, 0:width(g)], bias, start=False,
                                     stop=True)
                last.then_inc(sem(s + "v"), 1)

        def v_vector(v, s, heads, hd):
            for g in range(G):
                v.wait_ge(sem(s + "v"), g + 1)
                v.tensor_copy(V[0:width(g), g, 0:heads * (hd + 1)].rearrange("p (h d) -> p h d", h=heads)[:, :, 0:hd],
                              bank[6 + g % 2][0:width(g), 0:D].rearrange("p (h d) -> p h d", h=heads))\
                    .then_inc(sem(s + "v_out"), 1)

        def v_ones(v, s, heads, hd):
            v.memset(V[0:GT, :, 0:heads * (hd + 1)].rearrange("p g (h d) -> p g h d", d=hd + 1)[:, :, :, hd],
                     1.0).then_inc(sem(s + "v_ones"), 1)

        def proj_tensor(pe, s, layer, ready, bias):
            for g in range(NT):
                pe.wait_ge(*ready(g))
                if g >= 2:
                    pe.wait_ge(sem(s + "added"), g - 1)
                for k in range(C):
                    pe.matmul(bank[2 + g % 2][0:rows_of(g), 0:D], XT[:, k, tile(g)], a_w(layer, 3)[:, k, :],
                              start=(k == 0), stop=False)
                pe.matmul(bank[2 + g % 2][0:rows_of(g), 0:D], ones[0:1, 0:rows_of(g)], bias, start=False, stop=True)\
                    .then_inc(sem(s + "proj"), 1)

        def proj_vector(v, s, dst, src):
            for g in range(NT):
                v.wait_ge(sem(s + "proj"), g + 1)
                v.tensor_tensor(dst[0:rows_of(g), g, :], bank[2 + g % 2][0:rows_of(g), 0:D], src[0:rows_of(g), g, :], ALU.add)\
                    .then_inc(sem(s + "added"), 1)
                if g:
                    v.wait_ge(sem(s + "added"), g)
                    stats_vector(v, dst, g - 1)
            v.wait_ge(sem(s + "added"), NT)
            stats_vector(v, dst, NT - 1)

        KM = arena[:, 0:2 * C * SLOTS].rearrange("p (c a n) -> p c a n", c=C, a=2)

        def scores_of(g, heads):
            toks = width(g)
            o = (g % 3) * 16 * GT
            return arena2[0:toks, o:o + heads * toks]

        def score_tensor(pe, s, g, heads):
            toks = width(g)
            if g == 0:
                pe.wait_ge(sem(s + "qk_out"), 8)
            else:
                pe.wait_ge(sem(s + "masked"), g)
            for j in (0, 4, 1, 5, 2, 6, 3, 7):
                c, at = j // 4, slice(j % 4 * 32, j % 4 * 32 + 32)
                n = heads // 8
                keys = KM[at, c, :, tok(g)] if n == 2 else KT[at, c, tok(g)]
                last = pe.matmul(bank[j % 4][0:toks, c * n * toks:(c + 1) * n * toks], QT[at, c, tok(g)], keys,
                                 start=True, stop=True)
            last.then_inc(sem(s + "score"), 1)

        def score_vector(v, s, g, heads, mask):
            toks = width(g)
            S = scores_of(g, heads).rearrange("p (h n) -> p h n", h=heads)
            mx = arena2_mx(g, heads)
            v.wait_ge(sem(s + "score"), g + 1)
            if g >= 3:
                v.wait_ge(sem(s + "pT"), (g - 2) * (heads // 4))
            n = heads // 8
            by_bank = S.rearrange("p (c r a) n -> p c r a n", c=C, r=4)
            for r in range(4):
                scores = bank[r][0:toks, 0:C * n * toks]
                if n == 1:
                    last = v.tensor_tensor(by_bank[:, :, r, 0, :], scores.rearrange("p (c n) -> p c n", c=C),
                                           mask[0:toks, 0:toks].unsqueeze(1).to_broadcast([toks, C, toks]), ALU.add)
                else:
                    last = v.tensor_tensor(by_bank[:, :, r], scores.rearrange("p (c a n) -> p c a n", c=C, a=n),
                                           mask[0:toks, 0:toks].unsqueeze(1).unsqueeze(1).to_broadcast([toks, C, n, toks]),
                                           ALU.add)
            last.then_inc(sem(s + "masked"), 1)
            v.wait_ge(sem(s + "masked"), g + 1)
            vchain.link(v, v.tensor_reduce(mx, S, AX, ALU.max))
            v.tensor_tensor(S, S, mx.unsqueeze(2).to_broadcast([toks, heads, toks]), ALU.subtract)\
                .then_inc(sem(s + "shifted"), 1)

        def arena2_mx(g, heads):
            return r_mx[0:width(g), g % 3, 0:heads]

        def turned_p(g, heads):
            toks = width(g)
            o = 2 * C * SLOTS + (g % 2) * 16 * GT
            return arena[0:toks, o:o + heads * toks].rearrange("p (h n) -> p h n", h=heads)

        def exp_scalar(a, s, g, heads, scale):
            S = scores_of(g, heads)
            a.wait_ge(sem(s + "shifted"), g + 1)
            a.activation(S, S, ACT.Exp, scale=scale).then_inc(sem(s + "exp"), 1)

        def turned_scalar(a, s, g, heads):
            toks = width(g)
            PT = turned_p(g, heads)
            if g >= 2:
                a.wait_ge(sem(s + "pv"), g - 1)
            for j in range(heads // 4):
                a.wait_ge(sem(s + "pT"), g * (heads // 4) + j + 1)
                a.activation(PT[:, 4 * j:4 * j + 4, :],
                             bank[4 + j % 2][0:toks, 0:4 * toks].rearrange("p (h n) -> p h n", h=4), ACT.Copy)\
                    .then_inc(sem(s + "pT_out"), 1)

        def soft_scalar(a, s, heads, scale):
            exp_scalar(a, s, 0, heads, scale)
            exp_scalar(a, s, 1, heads, scale)
            turned_scalar(a, s, 0, heads)
            for g in range(1, G):
                turned_scalar(a, s, g, heads)
                if g + 1 < G:
                    exp_scalar(a, s, g + 1, heads, scale)

        def turn_p_tensor(pe, s, g, heads, j):
            toks = width(g)
            S = scores_of(g, heads).rearrange("p (h n) -> p h n", h=heads)
            n = g * (heads // 4) + j
            if j == 0:
                pe.wait_ge(sem(s + "exp"), g + 1)
            if n >= 2:
                pe.wait_ge(sem(s + "pT_out"), n - 1)
            for h in range(4):
                last = pe.transpose(bank[4 + j % 2][0:toks, h * toks:(h + 1) * toks], S[:, 4 * j + h, :],
                                    ident[0:toks, 0:toks])
            last.then_inc(sem(s + "pT"), 1)

        def pv_tensor(pe, s, g, heads, hd, shared, j):
            toks = width(g)
            PT = turned_p(g, heads)
            if j == 0:
                if g == 0:
                    pe.wait_ge(sem(s + "v_out"), G)
                    pe.wait_ge(sem(s + "v_ones"), 1)
                else:
                    pe.wait_ge(sem(s + "o"), g)
            pe.wait_ge(sem(s + "pT_out"), g * (heads // 4) + j + 1)
            n = hd + 1
            for h in range(4 * j, 4 * j + 4):
                hv = h % shared
                last = pe.matmul(bank[6][0:toks, h * n:(h + 1) * n], PT[:, h, :], V[0:toks, g, hv * n:(hv + 1) * n],
                                 start=True, stop=True)
            if j == heads // 4 - 1:
                last.then_inc(sem(s + "pv"), 1)

        def softmax_tensor(pe, s, heads, hd, shared):
            for g in range(2):
                score_tensor(pe, s, g, heads)
            for j in range(heads // 4):
                turn_p_tensor(pe, s, 0, heads, j)
            for g in range(G):
                if g + 2 < G:
                    score_tensor(pe, s, g + 2, heads)
                for j in range(heads // 4):
                    if g + 1 < G:
                        turn_p_tensor(pe, s, g + 1, heads, j)
                    pv_tensor(pe, s, g, heads, hd, shared, j)

        def out_vector(v, s, g, heads, hd):
            toks = width(g)
            o = bank[6][0:toks, 0:heads * (hd + 1)].rearrange("p (h d) -> p h d", h=heads)
            den = r_mx[0:toks, 3, 0:heads]
            v.wait_ge(sem(s + "pv"), g + 1)
            if g:
                v.wait_ge(sem(s + "o"), g)
            vchain.link(v, v.reciprocal(den, o[:, :, hd]))
            v.tensor_tensor(O[0:toks, g, :].rearrange("p (h d) -> p h d", h=heads), o[:, :, 0:hd],
                            den.unsqueeze(2).to_broadcast([toks, heads, hd]), ALU.mult).then_inc(sem(s + "o"), 1)


        FE = arena[:, 0:32 * GT].rearrange("p (w h n) -> p w h n", w=2, h=16)
        FS = arena[:, 32 * GT:64 * GT].rearrange("p (w h n) -> p w h n", w=2, h=16)
        FC = arena2[:, 0:32 * GT].rearrange("p (w h n) -> p w h n", w=2, h=16)
        FPT = arena2[0:GT, 32 * GT:48 * GT].rearrange("p (h n) -> p h n", h=16)
        FR = hT[:, 0:2, 0:4 * GT]

        LEAD = 3
        def heads_of(x, w, j, n):
            return x[:, w, 4 * j:4 * j + 4, 0:n]

        def phase_tensor(pe, g, j):
            toks = width(g)
            s = "L0_"
            for w in range(2):
                u = 8 * g + 2 * j + w
                if u >= 4:
                    pe.wait_ge(sem(s + "phase_out"), u - 3)
                for h in range(4):
                    last = pe.matmul(bank[u % 4][:, h * toks:(h + 1) * toks], proj8[:, j % 2, h, :],
                                     (QT, KT)[w][:, j // 2, tok(g)], start=True, stop=True)
                last.then_inc(sem(s + "phase"), 1)

        def similar_tensor(pe, g, j):
            toks = width(g)
            s = "L0_"
            n = g * 4 + j
            pe.wait_ge(sem(s + "cos"), n + 1)
            if n >= 2:
                pe.wait_ge(sem(s + "sim_out"), n - 1)
            for h in range(4):
                for k, f in enumerate((FS, FC)):
                    last = pe.matmul(bank[4 + j % 2][0:toks, h * toks:(h + 1) * toks], f[:, 1, 4 * j + h, 0:toks],
                                     f[:, 0, 4 * j + h, 0:toks], start=(k == 0), stop=(k == 1))
            last.then_inc(sem(s + "sim"), 1)

        def values_tensor(pe, g, j):
            toks = width(g)
            s = "L0_"
            pe.wait_ge(sem(s + "sim_out"), 4 * g + j + 1)
            if g == 0 and j == 0:
                pe.wait_ge(sem(s + "v_out"), G)
            if g and j == 0:
                pe.wait_ge(sem(s + "o"), g)
            for h in range(4 * j, 4 * j + 4):
                last = pe.matmul(bank[6][0:toks, h * 16:(h + 1) * 16], FPT[0:toks, h, 0:toks], V[0:toks, g, h * 17:h * 17 + 16],
                                 start=True, stop=True)
            last.then_inc(sem(s + "pv"), 1)

        def phase_vector(v, g, j):
            toks = width(g)
            s = "L0_"
            for w in range(2):
                u = 8 * g + 2 * j + w
                v.wait_ge(sem(s + "phase"), u + 1)
                if u >= 2:
                    v.wait_ge(sem(s + "phase_out"), u - 1)
                if g and w == 0:
                    v.wait_ge(sem(s + "sin"), 4 * (g - 1) + j + 1)
                vchain.link(v, v.tensor_scalar(FR[:, u % 2, 0:4 * toks], bank[u % 4][:, 0:4 * toks], MAGIC, -MAGIC,
                                               ALU.add, ALU.add))
                v.tensor_tensor(heads_of(FE, w, j, toks), bank[u % 4][:, 0:4 * toks].rearrange("p (h n) -> p h n", h=4),
                                FR[:, u % 2, 0:4 * toks].rearrange("p (h n) -> p h n", h=4), ALU.subtract)\
                    .then_inc(sem(s + "phase_out"), 1)

        def similar_vector(v, g, j):
            toks = width(g)
            s = "L0_"
            v.wait_ge(sem(s + "sim"), 4 * g + j + 1)
            if g:
                v.wait_ge(sem(s + "pv"), 4 * (g - 1) + j + 1)
            v.scalar_tensor_tensor(FPT[0:toks, 4 * j:4 * j + 4, 0:toks],
                                   bank[4 + j % 2][0:toks, 0:4 * toks].rearrange("p (h n) -> p h n", h=4),
                                   1.0 / 128, same[0:toks, 0:toks].unsqueeze(1).to_broadcast([toks, 4, toks]),
                                   ALU.mult, ALU.mult).then_inc(sem(s + "sim_out"), 1)

        def values_out_vector(v, g):
            toks = width(g)
            v.wait_ge(sem("L0_pv"), 4 * g + 4)
            v.tensor_copy(O[0:toks, g, :], bank[6][0:toks, 0:D]).then_inc(sem("L0_o"), 1)

        def fourier_scalar(a, g, j):
            toks = width(g)
            s = "L0_"
            n = 4 * g + j
            a.wait_ge(sem(s + "phase_out"), 2 * n + 2)
            if g:
                a.wait_ge(sem(s + "sim"), n - 3)
            a.activation(FC[:, :, 4 * j:4 * j + 4, 0:toks], FE[:, :, 4 * j:4 * j + 4, 0:toks], ACT.Abs)\
                .then_inc(sem(s + "abs"), 1)
            a.activation(FS[:, :, 4 * j:4 * j + 4, 0:toks], FE[:, :, 4 * j:4 * j + 4, 0:toks], ACT.Sin, scale=TWO_PI)\
                .then_inc(sem(s + "sin"), 1)
            a.wait_ge(sem(s + "abs"), n + 1)
            a.activation(FC[:, :, 4 * j:4 * j + 4, 0:toks], FC[:, :, 4 * j:4 * j + 4, 0:toks], ACT.Sin, scale=-TWO_PI,
                         bias=eps[:, 1:2]).then_inc(sem(s + "cos"), 1)

        KI = arena[0:GT, 0:IMAGES * D].rearrange("p (i n) -> p i n", i=IMAGES)
        VC = arena[0:GT, IMAGES * D:IMAGES * D + G * C * (P + 1)].rearrange("p (g c n) -> p g c n", g=G, c=C)
        KVM = arena2[:, 0:2 * C * 2 * P].rearrange("p (b c n) -> p b c n", b=2, c=C)

        def linear_tensor(pe):
            s = "L2_"
            pe.wait_ge(sem(s + "qk_out"), 4)
            pe.wait_ge(sem(s + "v_ones"), 1)
            linear_kv(pe, 0)
            for g in range(G):
                if g + 1 < G:
                    linear_kv(pe, g + 1)
                pe.wait_ge(sem(s + "kv_out"), g + 1)
                for i in range(g * PER, min((g + 1) * PER, IMAGES)):
                    if i >= 2:
                        pe.wait_ge(sem(s + "outer_out"), i - 1)
                    for c in range(C):
                        last = pe.matmul(bank[i % 2][:, c * (P + 1):(c + 1) * (P + 1)], KI[0:width(g), i, c * P:(c + 1) * P],
                                         VC[0:width(g), g, c, :], start=True, stop=True)
                    last.then_inc(sem(s + "outer"), 1)
                    if i:
                        linear_apply(pe, i - 1)
            linear_apply(pe, IMAGES - 1)

        def linear_kv(pe, g):
            s = "L2_"
            if g >= 2:
                pe.wait_ge(sem(s + "kv_out"), g - 1)
            for k in range(C):
                last = pe.matmul(bank[6 + g % 2][0:width(g), :], XT[:, k, tok(g)],
                                 wA[0][:, D * C:3 * D * C].rearrange("p (c n) -> p c n", c=C)[:, k, :],
                                 start=(k == 0), stop=(k == C - 1))
            last.then_inc(sem(s + "kv"), 1)

        def linear_apply(pe, i):
            s = "L2_"
            pe.wait_ge(sem(s + "outer_out"), i + 1)
            if i >= 4:
                pe.wait_ge(sem(s + "pair"), i // 2 - 1)
            for half in range(2):
                for c in range(C):
                    o = ((i % 2 * 2 + half) * C + c) * SEQ
                    last = pe.matmul(bank[4 + i // 2 % 2][:, o:o + SEQ], KVM[:, i % 2, c, half * P:(half + 1) * P],
                                     QT[:, c, i * SEQ:(i + 1) * SEQ], start=True, stop=True)
            last.then_inc(sem(s + "applied"), 1)

        def linear_vector(v):
            s = "L2_"
            v.memset(VC[:, :, :, P], 1.0).then_inc(sem(s + "v_ones"), 1)
            block = block8[:, :].unsqueeze(1).to_broadcast([P, C, P])
            for i in range(IMAGES):
                v.wait_ge(sem(s + "outer"), i + 1)
                if i >= 2:
                    v.wait_ge(sem(s + "applied"), i - 1)
                b = bank[i % 2][:, 0:C * (P + 1)].rearrange("p (c n) -> p c n", c=C)
                v.tensor_tensor(KVM[:, i % 2, :, 0:P], b[:, :, 0:P], block, ALU.mult)
                v.tensor_tensor(KVM[:, i % 2, :, P:2 * P], block, b[:, :, P:P + 1].to_broadcast([P, C, P]), ALU.mult)\
                    .then_inc(sem(s + "outer_out"), 1)
                if i and i % 2 == 0:
                    linear_divide(v, i // 2 - 1)
            linear_divide(v, IMAGES // 2 - 1)

        def linear_divide(v, pair):
            s = "L2_"
            v.wait_ge(sem(s + "applied"), 2 * pair + 2)
            b = bank[4 + pair % 2][:, 0:2 * 4 * SEQ].rearrange("p (i h n) -> p i h n", i=2, h=2)
            vchain.link(v, v.tensor_scalar(ksum[:, 0], b[:, :, 1, :], 1e-15, None, ALU.add))
            vchain.link(v, v.reciprocal(ksum[:, 1], ksum[:, 0]))
            v.tensor_tensor(XT[:, :, 2 * pair * SEQ:2 * (pair + 1) * SEQ].rearrange("p c (i n) -> p i c n", i=2),
                            b[:, :, 0, :].rearrange("p i (c n) -> p i c n", c=C),
                            ksum[:, 1].rearrange("p i (c n) -> p i c n", c=C), ALU.mult)\
                .then_inc(sem(s + "pair"), 1)

        def linear_scalar(a):
            s = "L2_"
            for g in range(G):
                a.wait_ge(sem(s + "kv"), g + 1)
                kv = bank[6 + g % 2][0:width(g), :]
                for i in range(g * PER, min((g + 1) * PER, IMAGES)):
                    j = (i - g * PER) * SEQ
                    a.activation(KI[0:width(g), i, :], kv[:, 0:D], ACT.Relu, scale=same[0:width(g), j:j + 1])
                a.activation(VC[0:width(g), g, :, 0:P], kv[:, D:2 * D].rearrange("p (c n) -> p c n", c=C), ACT.Relu)\
                    .then_inc(sem(s + "kv_out"), 1)

        def half_of(h):
            return slice(h * HT, (h + 1) * HT)

        def y_bank(g):
            return bank[4 + g // 2][0:rows_of(g), (g % 2) * D:(g % 2) * D + D]

        UNITS_BEFORE = {"L0m_": 0, "L0f_": F1, "L1f_": F1 + E * F0}
        EXPERTS_BEFORE = {"L0m_": 0, "L0f_": 1, "L1f_": 1 + E}
        f_h, f_silu, f_t, f_hh, f_hl = ([sem(f"ffn_{x}{half}") for half in range(2)] for x in (
            "product", "silu", "activations", "hidden_high", "hidden_low"))
        f_uh, f_ul, f_dh, f_dl, f_y, f_y_added, f_gcur = [sem("ffn_" + x) for x in (
            "up_high", "up_low", "down_high", "down_low", "outputs", "outputs_added", "gate_column")]
        act1 = QT[:, 0, 0:TOK]

        def unit(bufs, nf, k):
            k %= len(bufs) * nf
            return bufs[k // nf], k % nf

        def up_w(kind, nf, b, f):
            n = 2 * C if kind == "silu" else C
            return wE[b][:, 0:n * nf * P].rearrange("p (c n) -> p c n", c=n)[:, :, f * P:(f + 1) * P]

        def down_w(kind, nf, b, f):
            o = (2 * C if kind == "silu" else C) * nf * P
            return wE[b][:, o + f * D:o + (f + 1) * D]

        def three(high_a, low_a, high_b, low_b):
            return (high_a, high_b), (high_a, low_b), (low_a, high_b)

        def rounds_of(eng, rounds, body, first=0):
            for i in range(first):
                body(i, True)
            if rounds > first + 1:
                with eng.Fori(first, rounds - 1) as i:
                    body(i, True)
            body(rounds - 1, False)

        def is_first(i, rounds):
            return isinstance(i, int) and i == 0 and rounds > 1

        def ffn_tensor(pe, s, kind, nf, bufs, rounds, gate=None):
            units, base = len(bufs) * nf, UNITS_BEFORE[s]
            blocks = 2 * C if kind == "silu" else C

            def h(u, k):
                pe.wait_ge(f_ul, u + 1)
                for half in range(2):
                    if k == 0:
                        pe.wait_ge(xl_done, SPLITS.index(s) * NT + (NT if half else FIRST_HALF))
                    if kind == "silu":
                        if k:
                            pe.wait_ge(f_t[half], u - base)
                        dst = (bank[2 * half], bank[2 * half + 1])
                    else:
                        if k >= 2:
                            pe.wait_ge(f_hh[half], u - 1)
                        dst = (bank[2 * (k % 2) + half],)
                    x = half_of(half)
                    for j in range(blocks // C):
                        for c in range(C):
                            for n, (w, xx) in enumerate(three(UH, UL, XH, XL)):
                                last = pe.matmul(dst[j][:, 0:HT], w[:, k % 2, j * C + c, :], xx[:, c, x],
                                                 start=(c == 0 and n == 0), stop=(c == C - 1 and n == 2))
                    last.then_inc(f_h[half], 1)

            def y(u, e, k):
                f = k % nf
                for half in range(2):
                    pe.wait_ge(f_hl[half], u + 1)
                pe.wait_ge(f_dl, u + 1)
                for g in range(NT):
                    if f == 0 and g % 2 == 0:
                        pe.wait_ge(f_y_added, (EXPERTS_BEFORE[s] + e) * NT + min(g + 2, NT))
                    for p, (hid, w) in enumerate(three(HH, HL, DH, DL)):
                        last = pe.matmul(y_bank(g), hid[:, k % 2, tile(g)], w[:, k % 2, :],
                                         start=(f == 0 and g % 2 == 0 and p == 0), stop=(f == nf - 1 and p == 2),
                                         skip_group_check=True)
                last.then_inc(f_y, 1)

            def body(i, more):
                for k in range(units):
                    if k + 1 < units or more:
                        h(base + i * units + k + 1, k + 1)
                    if s in BIASED and not more and k < BIAS_STEPS:
                        bias_tensor(pe, s, k)
                    y(base + i * units + k, len(bufs) * i + k // nf, k)

            h(base, 0)
            if gate:
                gate()
            rounds_of(pe, rounds, body, int(rounds > 1))

        def ffn_scalar(a, s, kind, nf, wave, bufs, rounds, route=None):
            units, base = len(bufs) * nf, UNITS_BEFORE[s]

            def up_high(i, k):
                b, f = unit(bufs, nf, k)
                if b == MLP:
                    a.wait_ge(in_mlp, 16)
                elif f == 0:
                    a.wait_ge(in_exp[b], 16 * (i + k // units + wave + 1))
                w = up_w(kind, nf, b, f)
                a.activation(UH[:, k % 2, 0:w.shape[1], :], w, ACT.Copy).then_inc(f_uh, 1)

            def down_high(i, k, first=False):
                b, f = unit(bufs, nf, k)
                if not first or base:
                    a.wait_ge(f_y, base + i * units + k - 1)
                a.activation(DH[:, k % 2, :], down_w(kind, nf, b, f), ACT.Copy).then_inc(f_dh, 1)

            def body(i, more):
                for k in range(units):
                    b, f = unit(bufs, nf, k)
                    u = base + i * units + k
                    if kind == "silu":
                        for half in range(2):
                            a.wait_ge(f_h[half], u + 1)
                            a.activation(act1[:, half_of(half)], bank[2 * half][:, 0:HT], ACT.Silu)\
                                .then_inc(f_silu[half], 1)
                        if k + 2 < units or more:
                            up_high(i, k + 2)
                        for half in range(2):
                            a.wait_ge(f_t[half], u - base + 1)
                            a.activation(HH[:, k % 2, half_of(half)], KT[:, k % 2, half_of(half)], ACT.Copy)\
                                .then_inc(f_hh[half], 1)
                    else:
                        b1 = wE[b][:, nf * (C * P + D) + f:nf * (C * P + D) + f + 1]
                        for half in range(2):
                            a.wait_ge(f_h[half], u + 1)
                            if k >= 2 or base:
                                a.wait_ge(f_hl[half], u - 1)
                            src = bank[2 * (k % 2) + half][:, 0:HT]
                            a.activation(KT[:, k % 2, half_of(half)], src, ACT.Relu, bias=b1)
                            a.activation(HH[:, k % 2, half_of(half)], src, ACT.Relu, bias=b1)\
                                .then_inc(f_hh[half], 1)
                        if k + 2 < units or more:
                            up_high(i, k + 2)
                    if k + 1 < units or more:
                        down_high(i, k + 1, base == 0 and k == 0)
                    if is_first(i, rounds):
                        route(k)
                    if s in BIASED and not more and k < BIAS_STEPS:
                        bias_scalar(a, s, k)

            def start():
                up_high(0, 0)
                up_high(0, 1)
                down_high(0, 0, True)

            return start, lambda: rounds_of(a, rounds, body, int(rounds > 1))

        def ffn_vector(v, s, kind, nf, bufs, rounds, route=None):
            units, base = len(bufs) * nf, UNITS_BEFORE[s]
            gated = s != "L0m_"

            def up_low(i, k):
                b, f = unit(bufs, nf, k)
                w = up_w(kind, nf, b, f)
                n = w.shape[1]
                v.wait_ge(f_uh, base + i * units + k + 1)
                v.tensor_tensor(UL[:, k % 2, 0:n, :], w, UH[:, k % 2, 0:n, :].bitcast(F32), ALU.subtract)\
                    .then_inc(f_ul, 1)

            def down_low(i, k):
                b, f = unit(bufs, nf, k)
                v.wait_ge(f_dh, base + i * units + k + 1)
                v.tensor_tensor(DL[:, k % 2, :], down_w(kind, nf, b, f), DH[:, k % 2, :].bitcast(F32), ALU.subtract)\
                    .then_inc(f_dl, 1)

            def hidden(i, k):
                u = base + i * units + k
                if kind == "silu":
                    for half in range(2):
                        v.wait_ge(f_silu[half], u - base + 1)
                        v.wait_ge(f_hl[half], u - 1)
                        v.tensor_tensor(KT[:, k % 2, half_of(half)], bank[2 * half + 1][:, 0:HT],
                                        act1[:, half_of(half)], ALU.mult).then_inc(f_t[half], 1)
                for half in range(2):
                    v.wait_ge(f_hh[half], u + 1)
                    x = half_of(half)
                    v.tensor_tensor(HL[:, k % 2, x], KT[:, k % 2, x], HH[:, k % 2, x].bitcast(F32), ALU.subtract)\
                        .then_inc(f_hl[half], 1)

            def add(i, k, last):
                e, b = len(bufs) * i + k // nf, k // nf
                before = (EXPERTS_BEFORE[s] + e) * NT
                if gated:
                    v.wait_ge(f_y_added, before + NT)
                    v.tensor_copy(gcur[0:P, b, :], gate[0:P, :, bass.ds(e, 1)].rearrange("p g e -> p (g e)"))\
                        .then_inc(f_gcur, 1)
                v.wait_ge(f_y, base + i * units + k + 1)
                if gated:
                    v.wait_ge(f_gcur, EXPERTS_BEFORE[s] + e)
                for g in range(NT):
                    v.wait_ge(f_y_added, before + g + 1)
                    if gated:
                        v.scalar_tensor_tensor(H[0:rows_of(g), g, :], y_bank(g), gcur[0:rows_of(g), b, g:g + 1], H[0:rows_of(g), g, :],
                                               ALU.mult, ALU.add).then_inc(f_y_added, 1)
                    else:
                        v.tensor_tensor(H[0:rows_of(g), g, :], y_bank(g), H[0:rows_of(g), g, :], ALU.add)\
                            .then_inc(f_y_added, 1)
                    if last and g:
                        v.wait_ge(f_y_added, before + NT + g)
                        stats_vector(v, H, g - 1)
                if last:
                    v.wait_ge(f_y_added, before + 2 * NT)
                    stats_vector(v, H, NT - 1)

            def body(i, more):
                for k in range(units):
                    if k + 1 < units or more:
                        hidden(i, k + 1)
                    if is_first(i, rounds):
                        next(route, None)
                    if s in BIASED and not more and k < BIAS_STEPS:
                        bias_vector(v, s, k, (EXPERTS_BEFORE[s] + E - 2) * NT)
                    if k % nf == nf - 1:
                        add(i, k, not more and k == units - 1)
                    if k + 3 < units or more:
                        up_low(i, k + 3)
                    if k + 2 < units or more:
                        down_low(i, k + 2)

            def start():
                up_low(0, 0)
                up_low(0, 1)
                down_low(0, 0)

            def run():
                hidden(0, 0)
                up_low(0, 2)
                down_low(0, 1)
                rounds_of(v, rounds, body, int(rounds > 1))

            return start, run

        DONE = F1 + E * F0 + E * F1
        f_mh, f_ml = sem("deep_middle_high"), sem("deep_middle_low")
        f_t = f_t + [sem("deep_t1")]
        HIDDEN = ((HH, HL, KT), (H2H, H2L, QT))

        def deep_w(j, layer):
            return wD[j][:, layer * C * D:(layer + 1) * C * D]

        def deep_split(layer):
            high, low = (UH, UL) if layer < 2 else (DH, DL)
            if layer < 2:
                return [x[:, layer].rearrange("p c n -> p (c n)") for x in (high, low)]
            return [x.rearrange("p c n -> p (c n)") for x in (high, low)]

        def deep_bias(j, layer, f):
            o = 3 * C * D + 2 * layer + f
            return wD[j][:, o:o + 1]

        def deep_rounds(step):
            for e in range(E):
                step(e, e % 4, lambda n, e=e: e + n < E)

        def deep_tensor(pe, s, gate):
            def hidden(e, j, layer):
                if layer == 0:
                    pe.wait_ge(f_ul, DONE + e + 1)
                else:
                    pe.wait_ge(f_ml, e + 1)
                for f in range(2):
                    n = 4 * e + 2 * layer + f
                    for half in range(2):
                        if e == 0 and layer == 0 and f == 0:
                            pe.wait_ge(xl_done, SPLITS.index(s) * NT + (NT if half else FIRST_HALF))
                        pe.wait_ge(f_hh[half], DONE + n - 1)
                        if layer == 1:
                            pe.wait_ge(f_hl[half], DONE + 4 * e + 2)
                        x = half_of(half)
                        w = [x_.rearrange("p (c n) -> p c n", c=C) for x_ in deep_split(layer)]
                        src = (XH, XL) if layer == 0 else (HH, HL)
                        for c in range(C):
                            for p, (ww, xx) in enumerate(three(w[0], w[1], src[0], src[1])):
                                last = pe.matmul(bank[2 * f + half][:, 0:HT], ww[:, c, f * P:(f + 1) * P], xx[:, c, x],
                                                 start=(c == 0 and p == 0), stop=(c == C - 1 and p == 2))
                        last.then_inc(f_h[half], 1)

            def step(e, j, ahead):
                hidden(e, j + 1, 1)
                bias_step(ahead, j, 0)
                if ahead(1):
                    hidden(e + 1, j + 1, 0)
                for half in range(2):
                    pe.wait_ge(f_hl[half], DONE + 4 * e + 4)
                pe.wait_ge(f_dl, DONE + e + 1)
                for f in range(2):
                    for g in range(NT):
                        if f == 0 and g % 2 == 0:
                            pe.wait_ge(f_y_added, (2 * (E + 1) + e - 1) * NT + min(g + 2, NT))
                        for p, (hid, w) in enumerate(three(H2H, H2L, DH, DL)):
                            last = pe.matmul(y_bank(g), hid[:, f, tile(g)], w[:, f, :],
                                             start=(f == 0 and g % 2 == 0 and p == 0), stop=(f == 1 and p == 2),
                                             skip_group_check=True)
                last.then_inc(f_y, 1)
                bias_step(ahead, j, 1)

            def bias_step(ahead, j, n):
                if not ahead(4) and 2 * j + n < BIAS_STEPS:
                    bias_tensor(pe, s, 2 * j + n)

            hidden(0, 0, 0)
            gate()
            deep_rounds(step)

        def deep_scalar(a, s):
            def high(e, j, layer):
                j %= 4
                if layer == 0:
                    a.wait_ge(in_deep[j], 16 * (e // 4 + 1))
                if layer == 2 and e:
                    a.wait_ge(f_y, DONE + e)
                a.activation(deep_split(layer)[0], deep_w(j, layer), ACT.Copy)\
                    .then_inc((f_uh, f_mh, f_dh)[layer], 1)

            def hidden(e, j, layer):
                j %= 4
                hh, _, t_ = HIDDEN[layer]
                for f in range(2):
                    n = 4 * e + 2 * layer + f
                    for half in range(2):
                        a.wait_ge(f_h[half], DONE + n + 1)
                        dst = hh[:, f, half_of(half)]
                        if half == 0:
                            src, b = bank[2 * f][:, 0:HT], deep_bias(j, layer, f)
                            a.activation(t_[:, f, half_of(0)], src, ACT.Relu, bias=b)
                            a.activation(dst, src, ACT.Relu, bias=b).then_inc(f_hh[0], 1)
                        else:
                            a.wait_ge(f_t[2], n + 1)
                            a.activation(dst, t_[:, f, half_of(1)], ACT.Copy).then_inc(f_hh[1], 1)

            def bias_step(ahead, j, n):
                if not ahead(4) and 2 * j + n < BIAS_STEPS:
                    bias_scalar(a, s, 2 * j + n)

            def step(e, j, ahead):
                hidden(e, j, 1)
                bias_step(ahead, j, 0)
                if e == 0:
                    exp_on_scalar(a, s, 1, R(2), R(2))
                if ahead(1):
                    high(e + 1, j + 1, 1)
                    hidden(e + 1, j + 1, 0)
                if ahead(2):
                    high(e + 2, j + 2, 0)
                if ahead(1):
                    high(e + 1, j + 1, 2)
                bias_step(ahead, j, 1)

            def start():
                for layer in range(3):
                    high(0, 0, layer)

            def run():
                hidden(0, 0, 0)
                high(1, 1, 0)
                deep_rounds(step)

            return start, run

        def deep_vector(v, s, route):
            def low(e, j, layer):
                j %= 4
                done, ready, base = ((f_uh, f_ul, DONE), (f_mh, f_ml, 0), (f_dh, f_dl, DONE))[layer]
                v.wait_ge(done, base + e + 1)
                hi, lo = deep_split(layer)
                v.tensor_tensor(lo, deep_w(j, layer), hi.bitcast(F32), ALU.subtract).then_inc(ready, 1)

            def hidden(e, j, layer):
                j %= 4
                hh, hl, t_ = HIDDEN[layer]
                for f in range(2):
                    n = 4 * e + 2 * layer + f
                    v.wait_ge(f_h[1], DONE + n + 1)
                    v.wait_ge(f_hl[1], DONE + n - 3)
                    v.tensor_scalar(t_[:, f, half_of(1)], bank[2 * f + 1][:, 0:HT], deep_bias(j, layer, f), 0.0,
                                    ALU.add, ALU.max).then_inc(f_t[2], 1)
                    for half in range(2):
                        x = half_of(half)
                        v.wait_ge(f_hh[half], DONE + n + 1)
                        if half == 1:
                            v.wait_ge(f_t[2], n + 1)
                        v.tensor_tensor(hl[:, f, x], t_[:, f, x], hh[:, f, x].bitcast(F32), ALU.subtract)\
                            .then_inc(f_hl[half], 1)

            def add(e, last):
                before = (2 * (E + 1) - 1 + e) * NT
                v.wait_ge(f_y_added, before + NT)
                v.tensor_copy(gcur[:, 0, :], gate[:, :, bass.ds(e, 1)].rearrange("p g e -> p (g e)"))\
                    .then_inc(f_gcur, 1)
                v.wait_ge(f_y, DONE + e + 1)
                v.wait_ge(f_gcur, 2 * E + e + 1)
                for g in range(NT):
                    n = rows_of(g)
                    v.wait_ge(f_y_added, before + g + 1)
                    v.scalar_tensor_tensor(H[0:n, g, :], y_bank(g), gcur[0:n, 0, g:g + 1], H[0:n, g, :],
                                           ALU.mult, ALU.add).then_inc(f_y_added, 1)
                    if last and g:
                        v.wait_ge(f_y_added, before + NT + g)
                        stats_vector(v, H, g - 1)
                if last:
                    v.wait_ge(f_y_added, before + 2 * NT)
                    stats_vector(v, H, NT - 1)

            def bias_step(ahead, j, n, sums):
                if not ahead(4) and 2 * j + n < BIAS_STEPS:
                    bias_vector(v, s, 2 * j + n, sums)

            def step(e, j, ahead):
                hidden(e, j, 1)
                bias_step(ahead, j, 0, (2 * (E + 1) + e) * NT)
                if ahead(1):
                    low(e + 1, j + 1, 1)
                    hidden(e + 1, j + 1, 0)
                if ahead(2):
                    low(e + 2, j + 2, 0)
                if e == 0:
                    next(route)
                add(e, not ahead(1))
                if ahead(1):
                    low(e + 1, j + 1, 2)
                bias_step(ahead, j, 1, (2 * (E + 1) + e + 1) * NT)

            def start():
                for layer in range(3):
                    low(0, 0, layer)

            def run():
                hidden(0, 0, 0)
                low(1, 1, 0)
                next(route)
                deep_rounds(step)

            return start, run

        def gate_tensor(pe, s, which, bias):
            pe.wait_ge(xt_done, xt_all(s))
            for g in range(NT):
                for k in range(C):
                    last = pe.matmul(bank[7][0:P, g * E:(g + 1) * E], XT[:, k, g * P:(g + 1) * P], gates[:, which, k, :],
                                     start=(k == 0), stop=(bias is None and k == C - 1))
                if bias is not None:
                    last = pe.matmul(bank[7][0:P, g * E:(g + 1) * E], ones[0:1, 0:P], bias, start=False, stop=True)
            last.then_inc(sem(s + "gate_mm"), 1)

        def wide(x):
            return x.unsqueeze(2).to_broadcast([P, NT, E])

        def over_groups(x):
            return x[0:P, :].unsqueeze(1).to_broadcast([P, NT, E])

        def first_of(v, values, best, hot, tmp, one):
            vchain.link(v, v.tensor_tensor(tmp, values, wide(best), ALU.is_equal))
            vchain.link(v, v.tensor_tensor(tmp, tmp, over_groups(revE), ALU.mult))
            vchain.link(v, v.tensor_reduce(one, tmp, AX, ALU.max))
            vchain.link(v, v.tensor_tensor(hot, tmp, wide(one), ALU.is_equal))

        def R(i):
            return rt[0:P, i]

        def r(i):
            return r1[0:P, i]

        def get_scores(v, s):
            v.wait_ge(sem(s + "gate_mm"), 1)
            vchain.link(v, v.tensor_copy(score[0:P], bank[7][0:P, 0:NT * E].rearrange("p (g e) -> p g e", g=NT)))

        def exp_on_scalar(a, s, n, src, dst):
            a.wait_ge(sem(s + "to_exp"), n)
            a.activation(dst, src, ACT.Exp).then_inc(sem(s + "exped"), 1)

        def route0_vector(v):
            s = "L0f_"
            get_scores(v, s)
            S = score[0:P]
            L = lambda ins: vchain.link(v, ins)
            L(v.tensor_reduce(r(0), S, AX, ALU.max))
            first_of(v, S, r(0), R(0), R(1), r(1))
            L(v.scalar_tensor_tensor(R(2), R(0), NEG, S, ALU.mult, ALU.add))
            yield
            L(v.tensor_reduce(r(2), R(2), AX, ALU.max))
            first_of(v, R(2), r(2), R(3), R(1), r(1))
            L(v.scalar_tensor_tensor(R(4), S, -1.0, S, ALU.mult, ALU.max))
            yield
            for n, (top, src, d, keep) in enumerate(((r(0), S, R(5), R(6)), (r(2), R(2), R(7), R(8)))):
                L(v.tensor_tensor(R(9), R(4), wide(top), ALU.max))
                L(v.tensor_tensor(R(10), S, wide(top), ALU.subtract))
                L(v.scalar_tensor_tensor(R(11), R(9), 0.02, R(10), ALU.mult, ALU.add))
                L(v.tensor_scalar(keep, R(11), 0.0, None, ALU.is_ge))
                v.tensor_tensor(d, src, wide(top), ALU.subtract).then_inc(sem(s + "to_exp"), 1)
            yield
            for n, (d, keep, hot) in enumerate(((R(5), R(6), R(0)), (R(7), R(8), R(3)))):
                v.wait_ge(sem(s + "exped"), n + 1)
                L(v.tensor_tensor(keep, keep, d, ALU.mult))
                L(v.tensor_reduce(r(3), keep, AX, ALU.add))
                L(v.reciprocal(r(4), r(3)))
                L(v.tensor_tensor(hot, hot, wide(r(4)), ALU.mult))
            v.tensor_tensor(gate[0:P], R(0), R(3), ALU.add).then_inc(sem(s + "gate"), 1)
            v.wait_ge(sem(s + "gate"), 1)
            yield

        def route0_scalar(a):
            exp_on_scalar(a, "L0f_", 1, R(5), R(5))
            exp_on_scalar(a, "L0f_", 2, R(7), R(7))

        def route1_vector(v):
            s = "L1f_"
            get_scores(v, s)
            S = score[0:P]
            L = lambda ins: vchain.link(v, ins)
            for g in range(NT):
                last = v.max(R(0)[:, g, :], S[:, g, :])
            L(last)
            L(v.tensor_tensor(R(1), S, wide(R(0)[:, :, 1]), ALU.is_ge))
            v.tensor_tensor(R(2), S, wide(R(0)[:, :, 0]), ALU.subtract).then_inc(sem(s + "to_exp"), 1)
            yield
            v.wait_ge(sem(s + "exped"), 1)
            L(v.tensor_tensor(R(3), R(1), R(2), ALU.mult))
            L(v.tensor_reduce(r(0), R(3), AX, ALU.add))
            L(v.reciprocal(r(1), r(0)))
            v.scalar_tensor_tensor(gate[0:P], R(3), 1.0 / E, wide(r(1)), ALU.mult, ALU.mult)\
                .then_inc(sem(s + "gate"), 1)
            v.wait_ge(sem(s + "gate"), 1)
            yield

        def probs_vector(v, s):
            get_scores(v, s)
            S = score[0:P]
            L = lambda ins: vchain.link(v, ins)
            L(v.tensor_reduce(r(0), S, AX, ALU.max))
            v.tensor_tensor(R(2), S, wide(r(0)), ALU.subtract).then_inc(sem(s + "to_exp"), 1)
            yield
            v.wait_ge(sem(s + "exped"), 1)
            L(v.tensor_reduce(r(1), R(2), AX, ALU.add))
            L(v.reciprocal(r(2), r(1)))
            L(v.tensor_tensor(R(3), R(2), wide(r(2)), ALU.mult))
            L(v.tensor_reduce(r(3), R(3), AX, ALU.max))
            first_of(v, R(3), r(3), R(4), R(5), r(4))

        def route2_vector(v):
            s = "L2f_"
            yield from probs_vector(v, s)
            L = lambda ins: vchain.link(v, ins)
            L(v.scalar_tensor_tensor(R(6), R(4), -2.0, R(3), ALU.mult, ALU.add))
            L(v.tensor_reduce(r(5), R(6), AX, ALU.max))
            first_of(v, R(6), r(5), R(7), R(5), r(4))
            L(v.tensor_tensor(R(8), R(4), wide(R(3)[:, :, 0]), ALU.mult))
            L(v.tensor_tensor(R(9), R(7), wide(R(3)[:, :, 1]), ALU.mult))
            v.tensor_tensor(gate[0:P], R(8), R(9), ALU.add).then_inc(sem(s + "gate"), 1)
            v.wait_ge(sem(s + "gate"), 1)
            yield

        gateT = hT[0:E, 0:2, :].rearrange("p a n -> p (a n)")[:, 0:NT * P].rearrange("p (g n) -> p g n", g=NT)
        BIAS_STEPS = 5
        gate_turned, gate_out, bias_made, biased = [sem("bias_" + n) for n in ("turned", "out", "made", "added")]
        BIASED = ["L1f_", "L2f_"]

        def bias_tensor(pe, s, n):
            m = BIASED.index(s)
            if n == 0:
                pe.wait_ge(sem(s + "gate"), 1)
            if n < 2:
                if n == 1:
                    pe.wait_ge(gate_out, 2 * m + 1)
                elif m:
                    pe.wait_ge(biased, m * NT)
                for g in (range(4) if n == 0 else (4,)):
                    last = pe.transpose(bank[7][0:E, g % 4 * P:(g % 4 + 1) * P], gate[:, g, :], ident[:, :])
                last.then_inc(gate_turned, 1)
            else:
                pe.wait_ge(gate_out, 2 * m + 2)
                if n > 2:
                    pe.wait_ge(biased, m * NT + 2 * (n - 2))
                for g in range(2 * (n - 2), min(2 * (n - 1), NT)):
                    last = pe.matmul(bank[7][0:rows_of(g), g % 2 * D:(g % 2 + 1) * D], gateT[:, g, 0:rows_of(g)],
                                     tab[:, m, :], start=True, stop=True)
                last.then_inc(bias_made, 1)

        def bias_scalar(a, s, n):
            if n < 2:
                a.wait_ge(gate_turned, 2 * BIASED.index(s) + n + 1)
                g = slice(4 * n, min(4 * n + 4, NT))
                m = g.stop - g.start
                a.activation(gateT[:, g, :], bank[7][0:E, 0:m * P].rearrange("p (g n) -> p g n", g=m), ACT.Copy)\
                    .then_inc(gate_out, 1)

        def bias_vector(v, s, n, sums):
            m = BIASED.index(s)
            if n >= 2:
                v.wait_ge(bias_made, 3 * m + n - 1)
                v.wait_ge(f_y_added, sums)
                for g in range(2 * (n - 2), min(2 * (n - 1), NT)):
                    k = rows_of(g)
                    v.tensor_tensor(H[0:k, g, :], bank[7][0:k, g % 2 * D:(g % 2 + 1) * D], H[0:k, g, :], ALU.add)\
                        .then_inc(biased, 1)
            if n == BIAS_STEPS - 1:
                v.wait_ge(biased, (m + 1) * NT)

        DSP = part(0, NT * TOK, "p (g n) -> p g n", g=NT)
        XP = [part(8 * TOK + i * NT * D, NT * D, "p (g n) -> p g n", g=NT) for i in range(2)]
        DST = part(0, 2 * NT * P, "p (b g n) -> p b g n", b=2, g=NT)[0:CAP]
        YP = [part(8 * TOK + i * 2 * D, 2 * D, "p (b n) -> p b n", b=2)[0:CAP] for i in range(2)]
        SL = arena2[:, 0:C * TOK].rearrange("p (c n) -> p c n", c=C)
        YS = arena2[0:CAP, C * TOK:C * TOK + 2 * D].rearrange("p (b n) -> p b n", b=2)
        diag = arena2[0:P, C * TOK + E * D:C * TOK + E * D + 2 * P].rearrange("p (b n) -> p b n", b=2)
        destB = V[0:CAP].rearrange("p g n -> p (g n)")[:, 0:NT * P]
        GELU_IN = 2.0 ** 0.5 / 1.41421

        def switch_w(b):
            w, n = wE[b], C * F1 * P
            return (w[:, 0:n].rearrange("p (c n) -> p c n", c=C), w[:, n:n + F1],
                    w[:, n + F1:n + F1 + F1 * D].rearrange("p (f n) -> p f n", f=F1))

        def switch_vector(v):
            s = "L3f_"
            for _ in probs_vector(v, s):
                pass
            L = lambda ins: vchain.link(v, ins)
            L(v.tensor_scalar(R(4)[:, NT - 1, :], R(4)[:, NT - 1, :], valid[:, 0:1], None, ALU.mult))
            v.tensor_copy(R(6), R(4)).then_inc(sem(s + "hot"), 1)
            L(v.reciprocal(r(5), r(3)))
            L(v.tensor_tensor(r(6), r(3), r(5), ALU.mult))
            L(v.scalar_tensor_tensor(R(5), R(4), float(CAP), over_groups(iotaE), ALU.mult, ALU.mult))
            L(v.tensor_reduce(r(0), R(5), AX, ALU.add))
            v.wait_ge(sem(s + "cum"), 1)
            L(v.tensor_tensor(R(7), R(4), bank[7][0:P, 64:64 + NT * E].rearrange("p (g e) -> p g e", g=NT), ALU.mult))
            L(v.tensor_reduce(r(1), R(7), AX, ALU.add))
            v.tensor_scalar(r(2), r(1), float(CAP), None, ALU.is_le)
            L(v.tensor_tensor(r(7), r(0), r(1), ALU.add))
            L(v.tensor_tensor(r(4), r(7), r(2), ALU.mult))
            L(v.tensor_scalar(r(4), r(4), -1.0, None, ALU.add))
            for g in range(NT):
                n = rows_of(g)
                v.tensor_scalar(X[0:n, g, :], X[0:n, g, :], r(6)[0:n, g:g + 1], None, ALU.mult)\
                    .then_inc(sem(s + "xs"), 1)
            L(v.tensor_scalar(r(5), r(2), -1.0, 1.0, ALU.mult, ALU.add))
            for g in range(NT):
                v.tensor_scalar(DSP[:, g, :], slot_id[0:P, :], r(4)[:, g:g + 1], None, ALU.is_equal)\
                    .then_inc(sem(s + "dispatch"), 1)
            for g in range(NT):
                n = rows_of(g)
                v.wait_ge(sem(s + "xs_high"), g + 1)
                v.tensor_tensor(XP[1][0:n, g, :], X[0:n, g, :], XP[0][0:n, g, :].bitcast(F32), ALU.subtract)\
                    .then_inc(sem(s + "xs_low"), 1)
            for g in range(NT):
                if g >= 2:
                    v.wait_ge(sem(s + "dest"), g - 1)
                v.tensor_scalar(diag[:, g % 2, :], ident[0:P, 0:P], r(4)[:, g:g + 1], None, ALU.mult)\
                    .then_inc(sem(s + "diag"), 1)
            for j, n in enumerate((4, 1)):
                v.wait_ge(sem(s + "dest"), 4 * j + n)
                last = v.tensor_copy(destB[:, 4 * j * P:(4 * j + n) * P], bank[4 + j][0:CAP, 0:n * P])
            L(last)
            v.wait_ge(sem(s + "slots"), 4)

        def switch_tensor(pe, wave):
            s = "L3f_"
            pe.wait_ge(sem(s + "hot"), 1)
            for k in range(NT):
                last = pe.matmul(bank[7][0:P, 64 + k * E:64 + NT * E], (ones if k else tri)[:, :],
                                 R(6)[:, 0:NT - k, :], start=(k == 0), stop=(k == NT - 1))
            last.then_inc(sem(s + "cum"), 1)
            pe.wait_ge(sem(s + "dispatch"), NT)
            pe.wait_ge(sem(s + "xs_low"), NT)
            for c in range(C):
                for half in range(2):
                    for g in range(NT):
                        n = rows_of(g)
                        for j in range(2):
                            last = pe.matmul(bank[2 * c + half][:, 0:HT], XP[j][0:n, g, c * P:(c + 1) * P],
                                             DSP[0:n, g, half_of(half)], start=(g == 0 and j == 0),
                                             stop=(g == NT - 1 and j == 1))
                    last.then_inc(sem(s + "slots"), 1)
            for g in range(NT):
                pe.wait_ge(sem(s + "diag"), g + 1)
                pe.matmul(bank[4 + g // 4][0:CAP, g % 4 * P:(g % 4 + 1) * P], ones[0:P, 0:CAP], diag[:, g % 2, :],
                          start=True, stop=True).then_inc(sem(s + "dest"), 1)
            pe.wait_ge(sem(s + "slots_out"), 4)

            def hidden(i, b):
                pe.wait_ge(in_exp[b], 16 * (i + wave + 1))
                pe.wait_ge(sem(s + "gelu"), 2 * i + b + 1)
                for f in range(F1):
                    for c in range(C):
                        last = pe.matmul(bank[2 * b + f // 4][:, f % 4 * CAP:(f % 4 + 1) * CAP],
                                         switch_w(b)[0][:, c, f * P:(f + 1) * P],
                                         SL[:, c, bass.ds((2 * i + b) * CAP, CAP)], start=(c == 0), stop=(c == C - 1))
                    if f % 4 == 3:
                        last.then_inc(sem(s + "hid"), 1)

            def body(i, more):
                for b in range(2):
                    if b == 0 or more:
                        hidden(i + b, 1 - b)
                    pe.wait_ge(in_out[b], 16 * (i + 1))
                    pe.wait_ge(sem(s + "gelu"), 2 * i + b + 3)
                    pe.wait_ge(sem(s + "ys_free"), 2 * i + b + 1)
                    for f in range(F1):
                        last = pe.matmul(bank[7][0:CAP, 0:D], hT[:, b, f * CAP:(f + 1) * CAP],
                                         switch_w(b)[2][:, f, :], start=(f == 0), stop=(f == F1 - 1))
                    last.then_inc(sem(s + "ys"), 1)
                    if b == 1 or not is_first(i, E // 2):
                        gather(2 * i + b - 1, 1 - b)

            def gather(e, b):
                pe.wait_ge(sem(s + "yl"), e + 1)
                pe.wait_ge(sem(s + "combine"), e + 1)
                first = isinstance(e, int) and e == 0
                last_one = isinstance(e, int) and e == E - 1
                for g in range(NT):
                    for j in range(2):
                        last = pe.matmul(y_bank(g), DST[:, b, g, 0:rows_of(g)], YP[j][:, b, :],
                                         start=(first and g % 2 == 0 and j == 0), stop=(last_one and j == 1),
                                         skip_group_check=True)
                last.then_inc(sem(s + "gathered"), 1)

            hidden(0, 0)
            rounds_of(pe, E // 2, body, 1)
            gather(E - 1, 1)

        def switch_scalar(a):
            s = "L3f_"
            exp_on_scalar(a, s, 1, R(2), R(2))
            for g in range(NT):
                n = rows_of(g)
                a.wait_ge(sem(s + "xs"), g + 1)
                a.activation(XP[0][0:n, g, :], X[0:n, g, :], ACT.Copy).then_inc(sem(s + "xs_high"), 1)
            for c in range(C):
                for half in range(2):
                    a.wait_ge(sem(s + "slots"), 2 * c + half + 1)
                    a.activation(SL[:, c, half_of(half)], bank[2 * c + half][:, 0:HT], ACT.Copy)\
                        .then_inc(sem(s + "slots_out"), 1)
            with a.Fori(0, E // 2) as i:
                for b in range(2):
                    a.wait_ge(sem(s + "b1s"), 2 * i + b + 1)
                    for f in range(F1):
                        if f % 4 == 0:
                            a.wait_ge(sem(s + "hid"), 4 * i + 2 * b + f // 4 + 1)
                        last = a.activation(hT[:, b, f * CAP:(f + 1) * CAP],
                                            bank[2 * b + f // 4][:, f % 4 * CAP:(f % 4 + 1) * CAP], ACT.Gelu,
                                            bias=b1s[:, b, f:f + 1], scale=GELU_IN)
                    last.then_inc(sem(s + "gelu"), 1)

        def switch_loop_vector(v, wave):
            s = "L3f_"
            v.wait_ge(in_attn[0], 16 * 3)

            def bias_in(i, b):
                v.wait_ge(in_exp[b], 16 * (i + wave + 1))
                v.tensor_scalar(b1s[:, b, :], switch_w(b)[1], GELU_IN, None, ALU.mult).then_inc(sem(s + "b1s"), 1)

            def body(i, more):
                for b in range(2):
                    e, y = 2 * i + b, YS[:, b, :]
                    v.wait_ge(sem(s + "ys"), e + 1)
                    v.scalar_tensor_tensor(y, bank[7][0:CAP, 0:D], 1.0 / GELU_IN,
                                           b2all[0:CAP, bass.ds(e, 1), :].rearrange("p e n -> p (e n)"),
                                           ALU.mult, ALU.add).then_inc(sem(s + "ys_free"), 1)
                    v.tensor_copy(own[:, b:b + 1], slot_own[:, bass.ds(e, 1)]).then_inc(sem(s + "own"), 1)
                    v.wait_ge(sem(s + "gathered"), e + 1)
                    v.wait_ge(sem(s + "ys_free"), e + 2)
                    v.tensor_copy(YP[0][:, b, :], y).then_inc(sem(s + "yh"), 1)
                    v.wait_ge(sem(s + "own"), e + 1)
                    v.tensor_scalar(DST[:, b], destB[:, 0:NT * P].rearrange("p (g n) -> p g n", g=NT),
                                    own[0:CAP, b:b + 1], None, ALU.is_equal).then_inc(sem(s + "combine"), 1)
                    v.wait_ge(sem(s + "yh"), e + 1)
                    v.tensor_tensor(YP[1][:, b, :], y, YP[0][:, b, :].bitcast(F32), ALU.subtract)\
                        .then_inc(sem(s + "yl"), 1)
                    if more:
                        bias_in(i + 1, b)

            for b in range(2):
                bias_in(0, b)
            for g in range(NT):
                n = rows_of(g)
                v.scalar_tensor_tensor(H[0:n, g, :], X[0:n, g, :], r(5)[0:n, g:g + 1], H[0:n, g, :],
                                       ALU.mult, ALU.add).then_inc(sem(s + "kept"), 1)
            rounds_of(v, E // 2, body)
            v.wait_ge(sem(s + "kept"), NT)
            v.wait_ge(sem(s + "gathered"), E + 2)
            for g in range(NT):
                n = rows_of(g)
                v.tensor_tensor(H[0:n, g, :], y_bank(g), H[0:n, g, :], ALU.add).then_inc(sem(s + "final"), 1)

        patches = arena[:, 0:PC * TOK].rearrange("p (c n) -> p c n", c=PC)
        w_patch = arena[:, PC * TOK:PC * (TOK + D)].rearrange("p (c n) -> p c n", c=PC)

        FIRST = 1

        def embed_tensor(pe):
            pe.wait_ge(in_patch, 16 * 4)
            for g in range(NT):
                if g == FIRST:
                    pe.wait_ge(sem("in_patch_rest"), 16)
                if g >= 2:
                    pe.wait_ge(sem("embedded"), g - 1)
                dst = bank[g % 2][0:rows_of(g), 0:D]
                for k in range(PC):
                    pe.matmul(dst, patches[:, k, tile(g)], w_patch[:, k, :], start=(k == 0), stop=False)
                pe.matmul(dst, place[:, tile(g)], posA, start=False, stop=True).then_inc(sem("embed"), 1)

        def embed_vector(v):
            for g in range(NT):
                v.wait_ge(sem("embed"), g + 1)
                v.tensor_copy(H[0:rows_of(g), g, :], bank[g % 2][0:rows_of(g), 0:D]).then_inc(sem("embedded"), 1)
                if g:
                    v.wait_ge(sem("embedded"), g)
                    stats_vector(v, H, g - 1)
            v.wait_ge(sem("embedded"), NT)
            stats_vector(v, H, NT - 1)

        n_small = 5
        block = ctx.enter_context(nc.Block())

        @block.sync
        def _(sp):
            sp.dma_start(posA, t["pos"]).then_inc(in_patch, 16)
            sp.dma_start(place, t["place"]).then_inc(in_patch, 16)
            sp.dma_start(w_patch, t["w_patch"]).then_inc(in_patch, 16)
            sp.dma_start(patches[:, :, 0:FIRST * P], t["patches"][:, :, 0:FIRST * P]).then_inc(in_patch, 16)
            sp.dma_start(patches[:, :, FIRST * P:TOK], t["patches"][:, :, FIRST * P:TOK])\
                .then_inc(sem("in_patch_rest"), 16)
            sp.dma_start(rows[:, :], t["rows"]).then_inc(in_small, 16)
            sp.dma_start(cols[:, :], t["cols"]).then_inc(in_small, 16)
            sp.dma_start(gates[:, :, :, :], t["gates"]).then_inc(in_small, 16)
            sp.dma_start(tab[:, :, :], t["tab"]).then_inc(in_small, 16)
            sp.dma_start(lam_in[0:GT], t["lam"]).then_inc(in_small, 16)
            sp.wait_ge(sem("proj_clear"), 1)
            for h in range(8):
                sp.dma_start(proj8[16 * h:16 * h + 16, h // 4, h % 4, :], t["proj"]).then_inc(in_proj, 16)
            sp.dma_start(wA[0][:, :], t["attn0"]).then_inc(in_attn[0], 16)
            sp.dma_start(wA[1][:, :], t["attn1"]).then_inc(in_attn[1], 16)
            sp.wait_ge(sem("L0_pv"), 4 * G)
            sp.dma_start(wE[MLP], t["mlp0"]).then_inc(in_mlp, 16)
            for b in range(2):
                sp.dma_start(wE[b], t["ffn0"][b]).then_inc(in_exp[b], 16)

            def stream(dram, size, used, per_expert, before=0, rounds=E // 2):
                with sp.Fori(1, rounds) as i:
                    for b in range(2):
                        sp.wait_ge(used, before + (2 * i + b - 1) * per_expert)
                        sp.dma_start(wE[b][:, 0:size], dram[bass.ds(2 * i + b, 1)].rearrange("e p n -> (e p) n"))\
                            .then_inc(in_exp[b], 16)

            sp.wait_ge(sem("L0a_added"), NT)
            sp.dma_start(wA[0][:, :], t["attn2"]).then_inc(in_attn[0], 16)
            stream(t["ffn0"], EXP0, f_y, F0, UNITS_BEFORE["L0f_"])
            sp.wait_ge(sem("L1_pv"), G)
            for b in range(2):
                sp.dma_start(wE[b][:, 0:EXP1], t["ffn1"][b]).then_inc(in_exp[b], 16)
            sp.wait_ge(sem("L1_added"), NT)
            sp.dma_start(wA[1][:, :], t["attn3"]).then_inc(in_attn[1], 16)
            stream(t["ffn1"], EXP1, f_y, F1, UNITS_BEFORE["L1f_"])
            sp.wait_ge(sem("L2_outer"), IMAGES)
            for j in range(4):
                sp.dma_start(wD[j], t["ffn2"][j]).then_inc(in_deep[j], 16)
            for e in range(4, E):
                sp.wait_ge(f_y, DONE + e - 3)
                sp.dma_start(wD[e % 4], t["ffn2"][e]).then_inc(in_deep[e % 4], 16)
            sp.dma_start(b2all[0:CAP], t["b2"]).then_inc(in_attn[0], 16)
            written = 0
            for g in range(G):
                sp.wait_ge(sem("L3_o"), g + 1)
                for i in range(g * PER, min((g + 1) * PER, IMAGES)):
                    q = (i - g * PER) * SEQ
                    sp.dma_start(by_head[i].rearrange("h q d -> q h d"),
                                 O[q:q + SEQ, g, :].rearrange("p (h d) -> p h d", h=16))\
                        .then_inc(sem("L3_heads_out"), 16)
                    written += 16
                for j in range(NT):
                    if groups_for(j) == g + 1:
                        sp.wait_ge(sem("L3_heads_out"), written)
                        if j:
                            sp.wait_ge(sem("L3_regrouped"), 16 * j)
                        sp.dma_start(X[0:rows_of(j), j, :], by_token[tile(j), :])\
                            .then_inc(sem("L3_regrouped"), 16)
            CUT = C * F1 * P + F1

            def first_w(e, b):
                sp.dma_start(wE[b][:, 0:CUT], t["ffn3"][bass.ds(e, 1), :, 0:CUT].rearrange("e p n -> (e p) n"))\
                    .then_inc(in_exp[b], 16)

            def second_w(e, b):
                sp.dma_start(wE[b][:, CUT:EXP1], t["ffn3"][bass.ds(e, 1), :, CUT:EXP1].rearrange("e p n -> (e p) n"))\
                    .then_inc(in_out[b], 16)

            for b in range(2):
                first_w(b, b)
            for b in range(2):
                second_w(b, b)
            def next_first(e, b):
                sp.wait_ge(sem("L3f_hid"), 2 * (e - 1))
                sp.wait_ge(sem("L3f_b1s"), e - 1)
                first_w(e, b)

            def body(i, more):
                for b in range(2):
                    if b == 0 or more:
                        next_first(2 * i + b + 3, 1 - b)
                    sp.wait_ge(sem("L3f_ys"), 2 * i + b + 1)
                    second_w(2 * i + b + 2, b)

            next_first(2, 0)
            rounds_of(sp, E // 2 - 1, body)
            for g in range(NT):
                sp.wait_ge(sem("L3f_final"), g + 1)
                sp.dma_start(t["out"][tile(g), :], H[0:rows_of(g), g, :]).then_inc(stored, 16)
            sp.wait_ge(stored, 16 * NT)

        @block.gpsimd
        def _(p):
            def L(ins):
                pchain.link(p, ins)

            def keep(x, pattern, base, mult, fill, op=ALU.is_ge):
                L(p.affine_select(out=x, in_=x, pattern=pattern, compare_op=op, fill=fill, base=base,
                                  channel_multiplier=mult))

            def same_block(x, n, size, value_in, fill):
                inner = x.shape[1] // n
                xv = x if inner == 1 else x.rearrange("p (b n) -> p b n", b=n)
                pat = [[-size, n]] if inner == 1 else [[-size, n], [0, inner]]
                keep(xv, pat, 0, 1, fill)
                pat = [[size, n]] if inner == 1 else [[size, n], [0, inner]]
                keep(xv, pat, size - 1, -1, fill)

            p.memset(hT[:, 2:4, 0:4 * P], 0.0).then_inc(sem("proj_clear"), 1)
            L(p.memset(eps[:, 0:1], EPS))
            L(p.memset(mv[:, :, :], 1.0))
            L(p.memset(ident[:, :], 0.0))
            keep(ident[:, :], [[-1, P]], 0, 1, 1.0, ALU.not_equal)
            L(p.memset(ones[:, :], 1.0))
            L(p.memset(tri[:, :], 1.0))
            keep(tri[:, :], [[1, P]], 0, -1, 0.0)
            L(p.memset(same[:, :], 1.0))
            same_block(same[:, :], PER, SEQ, 1.0, 0.0)
            L(p.memset(far[:, :], 0.0))
            same_block(far[:, :], PER, SEQ, 0.0, NEG)
            L(p.memset(causal[:, :], 0.0))
            same_block(causal[:, :], PER, SEQ, 0.0, NEG)
            keep(causal[:, :], [[-1, GT]], 0, 1, NEG)
            L(p.memset(valid[:, :], 1.0))
            keep(valid[:, :], [[0, 1]], TOK - (NT - 1) * P - 1, -1, 0.0)
            L(p.memset(head16[:, :], 1.0))
            same_block(head16[:, :], 8, 16, 1.0, 0.0)
            for n in range(2):
                h = head16[:, n:8:2]
                L(p.tensor_tensor(parity[:, n:n + 1], h[:, 0:1], h[:, 1:2], ALU.add))
                L(p.tensor_tensor(parity[:, n:n + 1], parity[:, n:n + 1], h[:, 2:3], ALU.add))
                L(p.tensor_tensor(parity[:, n:n + 1], parity[:, n:n + 1], h[:, 3:4], ALU.add))
            L(p.memset(block8[:, :], 1.0))
            same_block(block8[:, :], 16, 8, 1.0, 0.0)
            L(p.iota(i32[:, 0:E], [[1, E]], base=0, channel_multiplier=0))
            L(p.tensor_copy(iotaE[:, :], i32[:, 0:E]))
            L(p.iota(i32[:, 0:E], [[-1, E]], base=E, channel_multiplier=0))
            L(p.tensor_copy(revE[:, :], i32[:, 0:E]))
            L(p.iota(i32[:, 0:E], [[CAP, E]], base=0, channel_multiplier=1))
            L(p.tensor_copy(slot_own[:, :], i32[:, 0:E]))
            L(p.iota(i32[:, :], [[1, TOK]], base=0, channel_multiplier=0))
            L(p.tensor_copy(slot_id[:, :], i32[:, :]))
            L(p.memset(eps[:, 1:2], 1.5707963))
            p.memset(XT[:, :, TOK:SLOTS], 0.0).then_inc(consts, 1)
        @block.tensor
        def _(pe):
            embed_tensor(pe)
            pe.wait_ge(consts, 1)
            s = "L0_"
            turn_tensor(pe, s, X, normed_of(s))
            qk_tensor(pe, s, 0, (0, 1))
            v_tensor(pe, s, 0, row("L0_bv"))
            pe.wait_ge(sem("proj_scaled"), 1)
            pe.wait_ge(sem(s + "qk_out"), 8)
            for n in range(LEAD):
                phase_tensor(pe, *divmod(n, 4))
            for n in range(4 * G):
                if n + LEAD < 4 * G:
                    phase_tensor(pe, *divmod(n + LEAD, 4))
                similar_tensor(pe, *divmod(n, 4))
                if n:
                    values_tensor(pe, *divmod(n - 1, 4))
            values_tensor(pe, G - 1, 3)
            turn_tensor(pe, "L0o_", O, lambda g: (sem("L0_o"), g + 1))
            proj_tensor(pe, "L0a_", 0, lambda g: (xt_done, xt_count("L0o_", groups_for(g))), row("L0_bo"))
            s = "L0m_"
            turn_tensor(pe, s, X, normed_of(s))
            pe.wait_ge(xt_done, xt_all(s))
            for g in range(NT):
                pe.matmul(y_bank(g), ones[0:1, 0:rows_of(g)], row("L0_b2"), start=True, stop=True)\
                    .then_inc(sem(s + "bias"), 1)
            ffn_tensor(pe, s, "relu", F1, [MLP], 1)
            s = "L0f_"
            turn_tensor(pe, s, X, normed_of(s))
            ffn_tensor(pe, s, "silu", F0, [0, 1], E // 2, lambda: gate_tensor(pe, "L0f_", 0, None))
            s = "L1_"
            turn_tensor(pe, s, X, normed_of(s))
            qk_tensor(pe, s, 1, (0, 1))
            v_tensor(pe, s, 1, row("L1_bv"))
            softmax_tensor(pe, s, 8, 32, 4)
            turn_tensor(pe, "L1o_", X, normed_of("L1o_"))
            proj_tensor(pe, s, 1, lambda g: (xt_done, xt_count("L1o_", groups_for(g))), row("L1_bo"))
            s = "L1f_"
            turn_tensor(pe, s, X, normed_of(s))
            ffn_tensor(pe, s, "relu", F1, [0, 1], E // 2, lambda: gate_tensor(pe, "L1f_", 1, None))
            s = "L2_"
            turn_tensor(pe, s, X, normed_of(s))
            qk_tensor(pe, s, 2, (0,))
            linear_tensor(pe)
            proj_tensor(pe, s, 2, lambda g: (sem("L2_pair"), IMAGES // 2), row("L2_bo"))
            s = "L2f_"
            turn_tensor(pe, s, X, normed_of(s))
            deep_tensor(pe, s, lambda: gate_tensor(pe, "L2f_", 2, rows[0:1, 7 * D:7 * D + E]))
            s = "L3_"
            turn_tensor(pe, s, X, normed_of(s))
            qk_tensor(pe, s, 3, (0, 1))
            v_tensor(pe, s, 3, None)
            softmax_tensor(pe, s, 16, 16, 16)
            turn_tensor(pe, "L3o_", X, lambda g: (sem("L3_regrouped"), 16 * (g + 1)))
            proj_tensor(pe, s, 3, lambda g: (xt_done, xt_count("L3o_", g + 1)), row("L3_bo"))
            s = "L3f_"
            turn_tensor(pe, s, X, normed_of(s))
            gate_tensor(pe, s, 3, rows[0:1, 7 * D + E:7 * D + 2 * E])
            switch_tensor(pe, 8)

        @block.vector
        def _(v):
            embed_vector(v)
            v.wait_ge(consts, 1)
            v.wait_ge(in_proj, 16 * 8)
            v.tensor_scalar(hT[:, 2:4, 0:4 * P], hT[:, 2:4, 0:4 * P], 0.25 / (2 * 3.141592653589793), None, ALU.mult)\
                .then_inc(sem("proj_scaled"), 1)
            norm_vector(v, "L0i_", H, R0, taken=True, then=lambda g: stats_vector(v, R0, g))
            s = "L0_"
            norm_vector(v, s, R0, X, taken=True)
            v_vector(v, s, 16, 16)
            for n in range(LEAD):
                phase_vector(v, *divmod(n, 4))
            for n in range(4 * G):
                if n + LEAD < 4 * G:
                    phase_vector(v, *divmod(n + LEAD, 4))
                similar_vector(v, *divmod(n, 4))
                if n % 4 == 0 and n:
                    values_out_vector(v, n // 4 - 1)
            values_out_vector(v, G - 1)
            proj_vector(v, "L0a_", R0, R0)
            s = "L0m_"
            norm_vector(v, s, R0, X, taken=True)
            start, run = ffn_vector(v, s, "relu", F1, [MLP], 1)
            start()
            split_vector(v, s)
            v.wait_ge(sem(s + "bias"), NT)
            for g in range(NT):
                n = rows_of(g)
                vchain.link(v, v.tensor_tensor(R0[0:n, g, :], y_bank(g), R0[0:n, g, :], ALU.add))
                v.tensor_tensor(H[0:n, g, :], H[0:n, g, :], R0[0:n, g, :], ALU.add).then_inc(f_y_added, 1)
            run()
            s = "L0f_"
            norm_vector(v, s, H, X, taken=True)
            start, run = ffn_vector(v, s, "silu", F0, [0, 1], E // 2, route0_vector(v))
            start()
            split_vector(v, s)
            run()
            s = "L1_"
            for j in range(2):
                last = v.tensor_tensor_reduce(lam_in[0:GT, 2 * j, :], lam_in[0:GT, 2 * j, :],
                                              lam_in[0:GT, 2 * j + 1, :], 1.0, 0.0, ALU.mult, ALU.add,
                                              lam[0:GT, j:j + 1])
            last.then_inc(sem(s + "lam"), 1)
            v.wait_ge(sem(s + "lam_exp"), 1)
            vchain.link(v, v.tensor_tensor(lam[0:GT, 4:5], lam[0:GT, 3:4], lam[0:GT, 2:3], ALU.subtract))
            vchain.link(v, v.tensor_scalar(lam[0:GT, 5:6], lam[0:GT, 4:5], -0.8, None, ALU.add))
            norm_vector(v, s, H, X, taken=True)
            v_ones(v, s, 4, 32)
            for g in range(G):
                v.wait_ge(sem(s + "v"), g + 1)
                b, n = bank[6 + g % 2], width(g)
                vchain.link(v, v.tensor_scalar(O[0:n, g, 0:P], b[0:n, P:D], lam[0:n, 5:6], None, ALU.mult))
                v.tensor_tensor(V[0:n, g, 0:4 * 33].rearrange("p (h d) -> p h d", h=4)[:, :, 0:32],
                                b[0:n, 0:P].rearrange("p (h d) -> p h d", h=4),
                                O[0:n, g, 0:P].rearrange("p (h d) -> p h d", h=4), ALU.add)\
                    .then_inc(sem(s + "v_out"), 1)
            for g in range(2):
                score_vector(v, s, g, 8, far)
            for g in range(G):
                if g + 2 < G:
                    score_vector(v, s, g + 2, 8, far)
                out_vector(v, s, g, 8, 32)
            v.wait_ge(sem(s + "o"), G)
            norm_vector(v, "L1o_", O, X)
            proj_vector(v, s, H, H)
            s = "L1f_"
            norm_vector(v, s, H, X, taken=True)
            start, run = ffn_vector(v, s, "relu", F1, [0, 1], E // 2, route1_vector(v))
            start()
            split_vector(v, s)
            run()
            s = "L2_"
            norm_vector(v, s, H, X, taken=True)
            linear_vector(v)
            proj_vector(v, s, H, H)
            s = "L2f_"
            norm_vector(v, s, H, X, taken=True)
            start, run = deep_vector(v, s, route2_vector(v))
            start()
            split_vector(v, s)
            run()
            s = "L3_"
            norm_vector(v, s, H, X, taken=True)
            v_ones(v, s, 16, 16)
            v_vector(v, s, 16, 16)
            for g in range(2):
                score_vector(v, s, g, 16, causal)
            for g in range(G):
                if g + 2 < G:
                    score_vector(v, s, g + 2, 16, causal)
                out_vector(v, s, g, 16, 16)
            proj_vector(v, s, H, H)
            s = "L3f_"
            norm_vector(v, s, H, X, taken=True)
            v.sem_inc(sem(s + "gelu"), 2)
            v.sem_inc(sem(s + "ys_free"), 1)
            v.sem_inc(sem(s + "gathered"), 2)
            switch_vector(v)
            switch_loop_vector(v, 8)
        @block.scalar
        def _(a):
            a.wait_ge(consts, 1)
            a.wait_ge(in_small, 16 * n_small)
            norm_scalar(a, "L0i_")
            s = "L0_"
            norm_scalar(a, s)
            turn_scalar(a, s, lambda c: col("L0_g1", c), lambda c: col("L0_n1", c))
            qk_scalar(a, s, (0, 1), ACT.Identity, lambda w, c: col(("L0_bq", "L0_bk")[w], c))
            for n in range(4 * G):
                fourier_scalar(a, *divmod(n, 4))
            turn_scalar(a, "L0o_")
            s = "L0m_"
            start, run = ffn_scalar(a, s, "relu", F1, 0, [MLP], 1)
            start()
            norm_scalar(a, s)
            turn_scalar(a, s, lambda c: col("L0_g2", c), lambda c: col("L0_n2", c))
            run()
            s = "L0f_"
            start, run = ffn_scalar(a, s, "silu", F0, 0, [0, 1], E // 2,
                                    lambda k: route0_scalar(a) if k == 3 else None)
            start()
            norm_scalar(a, s)
            turn_scalar(a, s)
            run()
            s = "L1_"
            a.wait_ge(sem(s + "lam"), 1)
            a.activation(lam[0:GT, 2:4], lam[0:GT, 0:2], ACT.Exp).then_inc(sem(s + "lam_exp"), 1)
            norm_scalar(a, s)
            turn_scalar(a, s)
            qk_scalar(a, s, (0, 1), ACT.Identity, lambda w, c: col(("L1_bq", "L1_bk")[w], c))
            soft_scalar(a, s, 8, 1.0 / 32 ** 0.5)
            norm_scalar(a, "L1o_")
            last = a.activation(aff[:, :], cols[:, 2 * COL.index("L1_g"):2 * COL.index("L1_g") + 4], ACT.Copy,
                                scale=0.2)
            last.then_inc(sem("aff"), 1)
            a.wait_ge(sem("aff"), 1)
            turn_scalar(a, "L1o_", lambda c: aff[:, c:c + 1], lambda c: aff[:, 2 + c:3 + c])
            s = "L1f_"
            start, run = ffn_scalar(a, s, "relu", F1, 4, [0, 1], E // 2,
                                    lambda k: exp_on_scalar(a, "L1f_", 1, R(2), R(2)) if k == 1 else None)
            start()
            norm_scalar(a, s)
            turn_scalar(a, s)
            run()
            s = "L2_"
            norm_scalar(a, s)
            turn_scalar(a, s)
            qk_scalar(a, s, (0,), ACT.Relu, lambda w, c: None)
            linear_scalar(a)
            s = "L2f_"
            start, run = deep_scalar(a, s)
            start()
            norm_scalar(a, s)
            turn_scalar(a, s)
            run()
            s = "L3_"
            norm_scalar(a, s)
            turn_scalar(a, s)
            qk_scalar(a, s, (0, 1), ACT.Identity, lambda w, c: None)
            soft_scalar(a, s, 16, 0.25)
            turn_scalar(a, "L3o_")
            s = "L3f_"
            norm_scalar(a, s)
            turn_scalar(a, s)
            switch_scalar(a)


def _layout(x):
    import numpy as np

    def chunked(w):
        k, n = w.shape
        return w.reshape(k // P, P, n).transpose(1, 0, 2).reshape(P, -1)

    side = 6
    pt = x["x"].reshape(IMAGES, 3, side, 16, side, 16).transpose(1, 3, 5, 0, 2, 4).reshape(PD, IMAGES, PATCHES)
    full = np.zeros((PD, IMAGES, SEQ), pt.dtype)
    full[:, :, 2:] = pt
    t = {"patches": full.reshape(PC, P, TOK).transpose(1, 0, 2),
         "w_patch": x["L0_tok_W"].T.reshape(PC, P, D).transpose(1, 0, 2)}
    pos = np.zeros((2, SEQ, D), pt.dtype)
    pos[0, 0] = x["cls_tok"][0, 0]
    pos[0, 1:] = x["L0_tok_pos_embed"][0]
    pos[1, 1] = x["L0_tok_cls_token"][0, 0]
    pos[1, 2:] = x["L0_tok_b"]
    t["pos"] = pos.reshape(2 * SEQ, D)
    t["place"] = np.tile(np.eye(SEQ, dtype=pt.dtype), (2, IMAGES))
    gb = np.zeros(D, pt.dtype)
    gb[:E], gb[E:2 * E] = x["L2_ffn_gate_b"], x["L3_ffn_b_sw"]
    t["rows"] = np.concatenate([x["L0_attn_bv"], x["L0_attn_bo"], x["L0_attn_b2"], x["L1_attn_bv"], x["L1_attn_bo"],
                                x["L2_attn_proj_bias"], x["L3_attn_bo"], gb])[None]
    names = ["L0_attn_bq", "L0_attn_bk", "L0_attn_ln1_g", "L0_attn_ln1_b", "L0_attn_ln2_g", "L0_attn_ln2_b",
             "L1_attn_bq", "L1_attn_bk", "L1_attn_ln_w", "L1_attn_ln_b"]
    t["cols"] = np.concatenate([x[n].reshape(C, P).T for n in names], 1)
    t["gates"] = np.stack([w.reshape(C, P, E).transpose(1, 0, 2) for w in (
        x["L0_ffn_gate_w"].T, x["L1_ffn_W_gate"], x["L2_ffn_gate_w"].T, x["L3_ffn_W_sw"])], 1)
    t["tab"] = np.stack([x["L1_ffn_b2"], x["L2_ffn_b3"]], 1)
    t["lam"] = np.tile(np.stack([x["L1_attn_lambda_" + n] for n in ("q1", "k1", "q2", "k2")])[None], (GT, 1, 1))
    t["b2"] = np.tile(x["L3_ffn_b2"][None], (CAP, 1, 1))
    t["proj"] = x["L0_attn_proj_mat"]
    t["attn0"] = np.concatenate([chunked(x["L0_attn_w" + n]) for n in "qkvo"], 1)
    t["attn1"] = np.concatenate([chunked(x["L1_attn_W" + n]) for n in "qkvo"], 1)
    qkv = x["L2_attn_qkv_weight"].T
    t["attn2"] = np.concatenate([chunked(qkv[:, :D]), chunked(qkv[:, D:]), chunked(x["L2_attn_proj_weight"].T)], 1)
    t["attn3"] = np.concatenate([chunked(x["L3_attn_W" + n]) for n in "qkvo"], 1)

    def expert(*parts):
        return np.concatenate(parts, 1)

    def bias(b):
        return b.reshape(-1, P).T

    t["mlp0"] = expert(chunked(x["L0_attn_w1"]), chunked(x["L0_attn_w2"]), bias(x["L0_attn_b1"]))
    t["ffn0"] = np.stack([expert(chunked(x["L0_ffn_w1"][e].T), chunked(x["L0_ffn_w3"][e].T),
                                 chunked(x["L0_ffn_w2"][e].T)) for e in range(E)])
    n = "L1_ffn_"
    t["ffn1"] = np.stack([expert(chunked(x[n + "W1"][e]), chunked(x[n + "W2"][e]), bias(x[n + "b1"][e]))
                          for e in range(E)])
    n = "L3_ffn_"
    t["ffn3"] = np.stack([expert(chunked(x[n + "W1"][e]), bias(x[n + "b1"][e]), chunked(x[n + "W2"][e]))
                          for e in range(E)])
    n = "L2_ffn_"
    t["ffn2"] = np.stack([expert(chunked(x[n + "w1"][e]), chunked(x[n + "w2"][e]), chunked(x[n + "w3"][e]),
                                 bias(x[n + "b1"][e]), bias(x[n + "b2"][e])) for e in range(E)])
    return {k: np.ascontiguousarray(v) for k, v in t.items()}


def kernel(**inputs):
    import numpy as np
    import concourse.bacc as bacc
    from concourse.bass_utils import run_bass_kernel_spmd

    nc = bacc.Bacc("TRN2", target_bir_lowering=False, num_devices=1)
    arrays = _layout({k: np.asarray(v) for k, v in inputs.items()})
    t = {k: nc.dram_tensor(k + "_dram", v.shape, mybir.dt.from_np(v.dtype), kind="ExternalInput").ap()
         for k, v in arrays.items()}
    t["out"] = nc.dram_tensor("out_dram", (TOK, D), F32, kind="ExternalOutput").ap()
    build(nc, t)
    r = run_bass_kernel_spmd(nc, [{k + "_dram": v for k, v in arrays.items()}], core_ids=[0])
    return r.results[0]["out_dram"].reshape(IMAGES, SEQ, D)
```
